# Optimizing a Trainium2 kernel written in Bass

```python
import numpy as np
import jax
import jax.numpy as jnp

def _softmax(x, axis=-1):
    return jax.nn.softmax(x, axis=axis)

def _gelu(x):
    return jax.nn.gelu(x, approximate=True)

def _silu(x):
    return jax.nn.silu(x)

def _sigmoid(x):
    return jax.nn.sigmoid(x)

def _layernorm(x, axis=-1, eps=1e-05):
    m = jnp.mean(x, axis=axis, keepdims=True)
    v = jnp.var(x, axis=axis, keepdims=True)
    return (x - m) / jnp.sqrt(v + eps)

def _scatter_add(tgt, idx, src, axis=0):
    return tgt.at[idx].add(src)

def _segment_sum(src, seg, n):
    return jax.ops.segment_sum(src, seg, n)
kernel_name = 'mk_gnn_ffn_d2_gnn_r16_70a71f'

def setup_inputs(seed: int=0):
    np.random.seed(seed)
    _w = jnp.asarray

    def _rec_inputs():
        import jax
        import jax.numpy as jnp
        _gk = jax.random.key(seed)
        x = -0.0003713 + 1 * jax.random.normal(jax.random.fold_in(_gk, 1), (6250, 256), jnp.float32)
        src = jax.random.randint(jax.random.fold_in(_gk, 2), (100000,), 0, 6250, jnp.int32)
        dst = jnp.minimum((6250 * jax.random.uniform(jax.random.fold_in(_gk, 3), (100000,)) ** 2.0).astype(jnp.int32), 99999)
        _o = jnp.argsort(dst, stable=True)
        src = src[_o]
        dst = dst[_o]
        edge_attr_64 = 0.000189758 + 1.00013 * jax.random.normal(jax.random.fold_in(_gk, 12), (100000, 64), jnp.float32)
        return (x, src, dst, edge_attr_64)
    x, src, dst, edge_attr_64 = _rec_inputs()

    def _L0_gnn_setup():
        import jax, jax.numpy as jnp
        import numpy as np
        N_NODES = 3125
        N_EDGES = 50000
        NODE_IN = 256
        EDGE_OUT = 64
        GLOBAL_IN = 128
        NODE_OUT = 256
        HIDDEN = 512
        N_GRAPHS = 64
        key = jax.random.key(seed)
        ks = jax.random.split(key, 8)
        x = jax.random.normal(ks[0], (N_NODES, NODE_IN), dtype=jnp.float32)
        edge_index = jax.random.randint(ks[1], (2, N_EDGES), 0, N_NODES, dtype=jnp.int64)
        edge_attr = jax.random.normal(ks[2], (N_EDGES, EDGE_OUT), dtype=jnp.float32)
        u = jax.random.normal(ks[3], (N_GRAPHS, GLOBAL_IN), dtype=jnp.float32)
        batch = jnp.sort(jax.random.randint(ks[4], (N_NODES,), 0, N_GRAPHS, dtype=jnp.int64))
        in_dim = NODE_IN + EDGE_OUT + GLOBAL_IN
        b1s = 1.0 / np.sqrt(in_dim)
        b2s = 1.0 / np.sqrt(HIDDEN)
        W1 = jax.random.uniform(ks[5], (in_dim, HIDDEN), dtype=jnp.float32, minval=-b1s, maxval=b1s)
        b1 = jnp.zeros((HIDDEN,), dtype=jnp.float32)
        W2 = jax.random.uniform(ks[6], (HIDDEN, NODE_OUT), dtype=jnp.float32, minval=-b2s, maxval=b2s)
        b2 = jnp.zeros((NODE_OUT,), dtype=jnp.float32)
        return {'x': x, 'edge_index': edge_index, 'edge_attr': edge_attr, 'u': u, 'batch': batch, 'W1': W1, 'b1': b1, 'W2': W2, 'b2': b2}
    _L0_gnn_all = _L0_gnn_setup()
    _L0_gnn_in = {k: v for k, v in _L0_gnn_all.items() if k in ('u', 'W1', 'b1', 'W2', 'b2')}
    del _L0_gnn_all

    def _L0_ffn_setup():
        import math
        import jax, jax.numpy as jnp
        import numpy as np
        CAPACITY_FACTOR = 1.25
        TOP_K = 2
        LN_EPS = 1e-05

        def _layer_norm(x, gamma, beta):
            mu = jnp.mean(x, axis=-1, keepdims=True)
            var = jnp.var(x, axis=-1, keepdims=True)
            return (x - mu) * jax.lax.rsqrt(var + LN_EPS) * gamma + beta
        key = jax.random.key(seed)
        ks = jax.random.split(key, 4)
        B, S, D, F, E = (8, 256, 256, 512, 8)
        x = jax.random.normal(ks[0], (B, S, D), dtype=jnp.float32)
        Wr = jax.random.normal(ks[1], (D, E), dtype=jnp.float32) / np.sqrt(D)
        br = jnp.zeros((E,), jnp.float32)
        W1 = jax.random.normal(ks[2], (E, D, F), dtype=jnp.float32) / np.sqrt(D)
        b1 = jnp.zeros((E, F), jnp.float32)
        W2 = jax.random.normal(ks[3], (E, F, D), dtype=jnp.float32) / np.sqrt(F)
        b2 = jnp.zeros((E, D), jnp.float32)
        gamma = jnp.ones((D,), jnp.float32)
        beta = jnp.zeros((D,), jnp.float32)
        return {'x': x, 'Wr': Wr, 'br': br, 'W1': W1, 'b1': b1, 'W2': W2, 'b2': b2, 'gamma': gamma, 'beta': beta}
    _L0_ffn_all = _L0_ffn_setup()
    _L0_ffn_in = {k: v for k, v in _L0_ffn_all.items() if k in ('Wr', 'br', 'W1', 'b1', 'W2', 'b2', 'gamma', 'beta')}
    del _L0_ffn_all

    def _L1_gnn_setup():
        import jax, jax.numpy as jnp
        import numpy as np
        N_NODES = 3125
        key = jax.random.key(seed)
        k1, k2, k3 = jax.random.split(key, 3)
        x = jax.random.normal(k1, (N_NODES, 256), dtype=jnp.float32)
        W = jax.random.normal(k2, (256, 256), dtype=jnp.float32) * (1.0 / np.sqrt(256))
        edge_index = jax.random.randint(k3, (2, 100000), 0, N_NODES, dtype=jnp.int64)
        return {'x': x, 'W': W, 'edge_index': edge_index}
    _L1_gnn_all = _L1_gnn_setup()
    _L1_gnn_in = {k: v for k, v in _L1_gnn_all.items() if k in ('W',)}
    del _L1_gnn_all

    def _L1_ffn_setup():
        import math
        import jax, jax.numpy as jnp
        import numpy as np
        CAPACITY_FACTOR = 1.25
        key = jax.random.key(seed)
        ks = jax.random.split(key, 5)
        B, L, D, F, E = (8, 512, 256, 1024, 8)
        h = jax.random.normal(ks[0], (B, L, D), dtype=jnp.float32)
        gate_w = jax.random.normal(ks[1], (D, E), dtype=jnp.float32) * 0.02
        gate_b = jnp.zeros((E,), dtype=jnp.float32)
        w1 = jax.random.normal(ks[2], (E, D, F), dtype=jnp.float32) * (1.0 / math.sqrt(D))
        b1 = jnp.zeros((E, F), dtype=jnp.float32)
        w2 = jax.random.normal(ks[3], (E, F, D), dtype=jnp.float32) * (1.0 / math.sqrt(F))
        b2 = jnp.zeros((E, D), dtype=jnp.float32)
        return {'h': h, 'gate_w': gate_w, 'gate_b': gate_b, 'w1': w1, 'b1': b1, 'w2': w2, 'b2': b2}
    _L1_ffn_all = _L1_ffn_setup()
    _L1_ffn_in = {k: v for k, v in _L1_ffn_all.items() if k in ('gate_w', 'gate_b', 'w1', 'b1', 'w2', 'b2')}
    del _L1_ffn_all
    return {'x': x, 'src': src, 'dst': dst, 'edge_attr_64': edge_attr_64, 'L0_gnn_u': _L0_gnn_in['u'], 'L0_gnn_W1': _L0_gnn_in['W1'], 'L0_gnn_b1': _L0_gnn_in['b1'], 'L0_gnn_W2': _L0_gnn_in['W2'], 'L0_gnn_b2': _L0_gnn_in['b2'], 'L0_ffn_Wr': _L0_ffn_in['Wr'], 'L0_ffn_br': _L0_ffn_in['br'], 'L0_ffn_W1': _L0_ffn_in['W1'], 'L0_ffn_b1': _L0_ffn_in['b1'], 'L0_ffn_W2': _L0_ffn_in['W2'], 'L0_ffn_b2': _L0_ffn_in['b2'], 'L0_ffn_gamma': _L0_ffn_in['gamma'], 'L0_ffn_beta': _L0_ffn_in['beta'], 'L1_gnn_W': _L1_gnn_in['W'], 'L1_ffn_gate_w': _L1_ffn_in['gate_w'], 'L1_ffn_gate_b': _L1_ffn_in['gate_b'], 'L1_ffn_w1': _L1_ffn_in['w1'], 'L1_ffn_b1': _L1_ffn_in['b1'], 'L1_ffn_w2': _L1_ffn_in['w2'], 'L1_ffn_b2': _L1_ffn_in['b2']}

def reference(x, src, dst, edge_attr_64, L0_gnn_u, L0_gnn_W1, L0_gnn_b1, L0_gnn_W2, L0_gnn_b2, L0_ffn_Wr, L0_ffn_br, L0_ffn_W1, L0_ffn_b1, L0_ffn_W2, L0_ffn_b2, L0_ffn_gamma, L0_ffn_beta, L1_gnn_W, L1_ffn_gate_w, L1_ffn_gate_b, L1_ffn_w1, L1_ffn_b1, L1_ffn_w2, L1_ffn_b2):
    import jax
    import jax.numpy as jnp

    def _L0_gnn_ref(x, edge_index, edge_attr, u, batch, W1, b1, W2, b2):
        import jax, jax.numpy as jnp
        import numpy as np
        N_NODES = 3125
        N_EDGES = 50000
        NODE_IN = 256
        EDGE_OUT = 64
        GLOBAL_IN = 128
        NODE_OUT = 256
        HIDDEN = 512
        N_GRAPHS = 64
        n = x.shape[0]
        src = edge_index[0]
        sums = jax.ops.segment_sum(edge_attr, src, num_segments=n)
        counts = jax.ops.segment_sum(jnp.ones((edge_attr.shape[0],), edge_attr.dtype), src, num_segments=n)
        edge_attr_agg = sums / jnp.maximum(counts, 1.0)[:, None]
        u_expanded = u[batch]
        combined = jnp.concatenate([x, edge_attr_agg, u_expanded], axis=1)
        h = jax.nn.relu(combined @ W1 + b1)
        return h @ W2 + b2

    def _L0_ffn_ref(x, Wr, br, W1, b1, W2, b2, gamma, beta):
        import math
        import jax, jax.numpy as jnp
        import numpy as np
        CAPACITY_FACTOR = 1.25
        TOP_K = 2
        LN_EPS = 1e-05

        def _layer_norm(x, gamma, beta):
            mu = jnp.mean(x, axis=-1, keepdims=True)
            var = jnp.var(x, axis=-1, keepdims=True)
            return (x - mu) * jax.lax.rsqrt(var + LN_EPS) * gamma + beta
        B, S, D = x.shape
        E = Wr.shape[1]
        N = B * S
        K = TOP_K
        logits = jnp.mean(x, axis=1) @ Wr + br
        routing_weights = jax.nn.softmax(logits, axis=-1)
        capacity = float(math.ceil(N * CAPACITY_FACTOR / E))
        expected_loads = routing_weights.sum(axis=0) * (N / B)
        scale = jnp.where(expected_loads > capacity, capacity / expected_loads, 1.0)
        routing_weights = jax.nn.softmax(routing_weights * scale, axis=-1)
        rw_tok = jnp.broadcast_to(routing_weights[:, None, :], (B, S, E)).reshape(N, E)
        top_w, top_i = jax.lax.top_k(rw_tok, K)
        top_w = jax.nn.softmax(top_w, axis=-1)
        xf = x.reshape(N, D)
        h = jax.nn.gelu(jnp.einsum('nd,edf->enf', xf, W1) + b1[:, None, :], approximate=False)
        y = jnp.einsum('enf,efd->end', h, W2) + b2[:, None, :]
        w_dense = jnp.zeros((N, E), x.dtype).at[jnp.arange(N)[:, None], top_i].add(top_w)
        out = jnp.einsum('ne,end->nd', w_dense, y).reshape(B, S, D)
        out = _layer_norm(out + x, gamma, beta)
        return out

    def _L1_gnn_ref(x, W, edge_index):
        import jax, jax.numpy as jnp
        import numpy as np
        N_NODES = 3125
        N = x.shape[0]
        src, dst = (edge_index[0], edge_index[1])
        h = x @ W
        deg = jax.ops.segment_sum(jnp.ones_like(dst, dtype=h.dtype), dst, num_segments=N)
        deg_inv_sqrt = jnp.where(deg > 0, jax.lax.rsqrt(jnp.maximum(deg, 1)), 0.0)
        norm = deg_inv_sqrt[src] * deg_inv_sqrt[dst]
        msgs = h[src] * norm[:, None]
        out = jax.ops.segment_sum(msgs, dst, num_segments=N)
        return out

    def _L1_ffn_ref(h, gate_w, gate_b, w1, b1, w2, b2):
        import math
        import jax, jax.numpy as jnp
        import numpy as np
        CAPACITY_FACTOR = 1.25
        B, L, D = h.shape
        E = gate_w.shape[1]
        T = B * L
        C = max(1, math.ceil(CAPACITY_FACTOR * T / E))
        x = h.reshape(T, D)
        logits = x @ gate_w + gate_b
        probs = jax.nn.softmax(logits, axis=-1)
        idx = jnp.argmax(probs, axis=-1)
        prb = jnp.take_along_axis(probs, idx[:, None], axis=1)[:, 0]
        one_hot = jax.nn.one_hot(idx, E, dtype=jnp.float32)
        pos = (jnp.cumsum(one_hot, axis=0) * one_hot).sum(-1).astype(jnp.int32) - 1
        kept = pos < C
        pos_safe = jnp.where(kept, pos, C)
        buf = jnp.zeros((E, C, D), dtype=h.dtype).at[idx, pos_safe].set(x, mode='drop')
        hmid = jax.nn.relu(jnp.einsum('ecd,edf->ecf', buf, w1) + b1[:, None, :])
        ybuf = jnp.einsum('ecf,efd->ecd', hmid, w2) + b2[:, None, :]
        pos_g = jnp.minimum(pos, C - 1)
        y_tok = ybuf[idx, pos_g] * (prb * kept)[:, None]
        y = y_tok.reshape(B, L, D)
        y = jnp.nan_to_num(y, nan=0.0, posinf=10000.0, neginf=-10000.0)
        return y
    edge_index = jnp.stack([src, dst])
    batch0 = jnp.zeros((6250,), jnp.int32)
    x = x + _L0_gnn_ref(_layernorm(x, axis=-1), edge_index, edge_attr_64, L0_gnn_u, batch0, L0_gnn_W1, L0_gnn_b1, L0_gnn_W2, L0_gnn_b2)
    x = x + _L0_ffn_ref(_layernorm(x, axis=-1)[None], L0_ffn_Wr, L0_ffn_br, L0_ffn_W1, L0_ffn_b1, L0_ffn_W2, L0_ffn_b2, L0_ffn_gamma, L0_ffn_beta)[0]
    x = x + _L1_gnn_ref(_layernorm(x, axis=-1), L1_gnn_W, edge_index)
    x = x + _L1_ffn_ref(_layernorm(x, axis=-1)[None], L1_ffn_gate_w, L1_ffn_gate_b, L1_ffn_w1, L1_ffn_b1, L1_ffn_w2, L1_ffn_b2)[0]
    return x

_drawn_inputs = setup_inputs


def setup_inputs(seed=0):
    import zlib

    import numpy as np

    out = dict(_drawn_inputs(seed))
    spreads = {'L0_gnn_b1': (0.0, 0.1),
     'L0_gnn_b2': (0.0, 0.1),
     'L0_ffn_br': (0.0, 0.8),
     'L0_ffn_b1': (0.0, 0.306),
     'L0_ffn_b2': (0.0, 0.1),
     'L0_ffn_gamma': (1.0, 0.2),
     'L0_ffn_beta': (0.0, 0.1),
     'L1_ffn_gate_b': (0.0, 0.1),
     'L1_ffn_b1': (0.0, 0.8),
     'L1_ffn_b2': (0.0, 0.8)}
    factors = {}
    for name, (base, spread) in spreads.items():
        noise = np.random.default_rng([zlib.crc32(name.encode()), seed]).standard_normal(out[name].shape)
        drawn = base * np.exp(spread * noise) if base else spread * noise
        out[name] = jnp.asarray(drawn.astype(out[name].dtype))
    for name, factor in factors.items():
        out[name] = (out[name] * factor).astype(out[name].dtype)
    return out
```

```python
import concourse.bass as bass
from concourse import mybir
from contextlib import ExitStack

NODES, EDGES, D, DE, DG = 6250, 100000, 256, 64, 128
P = 125
T, ET = NODES // P, EDGES // P
GT = 2
G, N = T // GT, GT * P
EB = 10
B = ET // EB
K = 5
HID0, HID1, HID2 = 512, 512, 1024
E, CAP = 8, 977
SLOTS = 1000
ST = SLOTS // P
XW = D + 1
EPS = 1e-5
FMAX = 3.4028234663852886e38


class Steps:

    def __init__(self):
        self.base, self.k = 0, 0

    def up(self):
        self.k += 1
        return 1

    def value(self):
        return self.base + self.k


def in_turns(eng, steps, body, total, head, tail, unit):
    for g in range(head):
        before = steps.value()
        body(g)
    per, start = steps.value() - before, steps.value()
    with eng.Fori(head // unit, (total - tail) // unit) as i:
        for s in range(unit):
            g = i * unit + s
            steps.base, steps.k = start + (g - head) * per, 0
            body(g, s)
            assert steps.k == per
    steps.base, steps.k = start + (total - tail - head) * per, 0
    for g in range(total - tail, total):
        body(g)


def build(nc, a, out):
    f32, bf16, i32, u32 = mybir.dt.float32, mybir.dt.bfloat16, mybir.dt.int32, mybir.dt.uint32
    ALU, ACT, AX = mybir.AluOpType, mybir.ActivationFunctionType, mybir.AxisListType.X
    ctx = ExitStack()
    with ctx:
        def sb(name, shape, dt=f32):
            return ctx.enter_context(nc.sbuf_tensor(name, shape, dt))

        def sem(name):
            return ctx.enter_context(nc.semaphore(name))

        def dram(name, rows, cols):
            return nc.dram_tensor(name, (rows, cols), f32, kind="Internal").ap()

        edge_sum = [dram(f"edge_sum{k}", NODES + P, DE) for k in range(K)]
        node_sum = [dram(f"node_sum{k}", NODES + P, D) for k in range(K)]
        h_rows = dram("h_rows", NODES, D)
        slot_x = dram("slot_x", E * SLOTS + NODES, XW)
        slot_y = dram("slot_y", E * SLOTS + P, D)

        x = sb("x", [P, T, D])
        big = sb("big", [128, T * XW])
        mid = sb("mid", [128, 10240])
        hT = sb("hT", [128, 2, 8, N])
        xg = sb("xg", [P, 2, GT, D + DE])
        xh = sb("xh", [P, 2, GT, D])
        xTg = sb("xTg", [128, 2, 2, N])
        aT = sb("aT", [DE, 2, N])
        yb = sb("yb", [P, 2, GT, D])
        wk = sb("wk", [P, 2, GT, D])
        hb = sb("hb", [P, 2, GT, D])
        src_f = sb("src_f", [P, ET])
        dst_f = sb("dst_f", [P, ET])
        idx_a = sb("idx_a", [P, 2, EB], u32)
        idx_b = sb("idx_b", [P, 2, EB], u32)
        ident = sb("ident", [128, 128])
        before = sb("before", [P, P])
        ones = sb("ones", [P, P])
        lo_iota = sb("lo_iota", [P, P])
        hi_iota = sb("hi_iota", [P, T])
        e_iota = sb("e_iota", [P, E])
        n_iota = sb("n_iota", [P, T])
        spare = sb("spare", [P, 1])
        not_first = sb("not_first", [P, P])
        dup = sb("dup", [P, 2, EB])
        firsts = sb("firsts", [P, 2, EB])
        away = sb("away", [P, 2, EB])
        iota_i = sb("iota_i", [P, P], i32)
        neg_half = sb("neg_half", [P, T])
        stat = sb("stat", [P, 2, GT, 6])
        mv = sb("mv", [P, 2, GT, 2])
        var = sb("var", [P, 2, GT])
        rstd = sb("rstd", [P, 2, GT])
        stat2 = sb("stat2", [P, 2, GT, 6])
        mv2 = sb("mv2", [P, 2, GT, 2])
        var2 = sb("var2", [P, 2, GT])
        rstd2 = sb("rstd2", [P, 2, GT])
        mv1 = sb("mv1", [P, T, 2])
        rstd1 = sb("rstd1", [P, T])
        cnt = sb("cnt", [P, T])
        deg = sb("deg", [P, T])
        has = sb("has", [P, T])
        dis = sb("dis", [P, T])
        biasA = sb("biasA", [128, 4])
        b1A = sb("b1A", [128, 4])
        u0 = sb("u0", [DG, 1])
        b2A = sb("b2A", [P, D])
        msum = sb("msum", [128, 2, G])
        mean = sb("mean", [128, 2])
        wr = sb("wr", [128, 2, E])
        rt = sb("rt", [1, 16, E])
        rt_id = sb("rt_id", [1, E], u32)
        wcol = sb("wcol", [128, 2])
        wrow = sb("wrow", [1, 2, P])
        bB1 = sb("bB1", [128, 8])
        b2rows = sb("b2rows", [1, 2, D])
        b2B = sb("b2B", [P, D])
        gamma = sb("gamma", [P, D])
        beta = sb("beta", [P, D])
        wG = sb("wG", [128, 2, D])
        gw = sb("gw", [128, 2, E])
        gb = sb("gb", [P, E])
        b1E = sb("b1E", [128, 2, 8])
        b2E = sb("b2E", [P, 2, D])
        ps = ctx.enter_context(nc.psum_tensor("ps", [128, 8, 512], f32))

        def cut(area, rows, at, size):
            return area[0:rows, at:at + size], at + size

        rowb, o = cut(big, P, 0, 2 * EB * P)
        S, o = cut(big, P, o, 2 * EB * P)
        va, o = cut(big, P, o, 2 * EB * DE)
        ma, o = cut(big, P, o, 2 * EB * DE)
        oh, o = cut(big, P, o, 2 * EB * (P + T))
        SL, o = cut(big, P, o, EB * P)
        SL = SL.rearrange("p (t q) -> p t q", t=EB)
        rowb = rowb.bitcast(i32).rearrange("p (s t q) -> p s t q", s=2, t=EB)
        S = S.rearrange("p (s t q) -> p s t q", s=2, t=EB)
        va = va.rearrange("p (s t d) -> p s t d", s=2, t=EB)
        ma = ma.rearrange("p (s t d) -> p s t d", s=2, t=EB)
        oh = oh.bitcast(bf16)
        w = 2 * EB * P
        ohl = [oh[:, k * w:(k + 1) * w].rearrange("p (s t q) -> p s t q", s=2, t=EB) for k in range(2)]
        w2 = 2 * EB * T
        ohh = [oh[:, 2 * w + k * w2:2 * w + (k + 1) * w2].rearrange("p (s t q) -> p s t q", s=2, t=EB) for k in range(2)]
        hilo = [mid[0:P, k * ET:(k + 1) * ET] for k in range(4)]
        hl_i = mid[0:P, 4 * ET:5 * ET].bitcast(i32)
        hl_w = mid[0:P, 5 * ET:6 * ET]
        raw_i = mid[0:100, 6 * ET:6 * ET + 2000].bitcast(i32).rearrange("t (k c p) -> t k c p", k=2, c=8)
        raw_f = hT[0:100, 1, :, :].rearrange("t c n -> t (c n)").rearrange("t (k c p) -> t k c p", k=2, c=8)
        agg = mid[0:P, 0:T * DE]
        agg3 = agg.rearrange("p (t d) -> p t d", t=T)
        part = mid[0:P, T * DE:2 * T * DE]
        wA1 = mid[:, 6400:6400 + 3 * HID0].rearrange("p (c f) -> p c f", c=3)
        wA2 = mid[:, 7936:7936 + 4 * D].rearrange("p (c d) -> p c d", c=4)
        wU = mid[:, 8960:8960 + HID0]
        xnT = big[:, 0:2 * NODES].rearrange("p (c n) -> p c n", c=2)
        wB1 = mid[:, 0:2 * 2 * HID1].rearrange("p (c f) -> p c f", c=2)
        wB2 = mid[:, 2048:2048 + 8 * D].rearrange("p (c d) -> p c d", c=8)
        mg = mid[0:P, 0:2 * EB * D].rearrange("p (s t d) -> p s t d", s=2, t=EB)
        ms = mid[0:P, 2 * EB * D:4 * EB * D].rearrange("p (s t d) -> p s t d", s=2, t=EB)
        tab = mid[0:P, 0:2 * K * GT * D].rearrange("p (s k t d) -> p s k t d", s=2, k=K, t=GT)
        xn3 = big[0:P, 0:T * XW].rearrange("p (t d) -> p t d", t=T)
        gate = mid[0:P, 5120:5120 + 12 * T * E].rearrange("p (k q) -> p k q", k=12)
        gate3 = gate.rearrange("p k (t e) -> p k t e", t=T)
        g50 = hb[:, :, :, :].rearrange("p s t d -> p (s t d)")[:, 0:16 * T].rearrange("p (k t) -> p k t", k=16)
        sc_idx = sb("sc_idx", [P, T], u32)
        ga_idx = sb("ga_idx", [P, T], u32)
        xe = big[0:P, 0:2 * ST * XW].rearrange("p (s t d) -> p s t d", s=2, t=ST)
        w1E = mid[:, 0:2 * 2 * HID2].rearrange("p (s c f) -> p s c f", s=2, c=2)
        w2E = mid[:, 4096:4096 + 2 * 8 * D].rearrange("p (s c d) -> p s c d", s=2, c=8)
        nanw = mid[0:P, 8192:8192 + 4 * GT * D].rearrange("p (k t d) -> p k t d", k=4, t=GT)
        yg = big[0:P, 0:T * D].rearrange("p (t d) -> p t d", t=T)

        x_in = a["x"].rearrange("(t p) d -> p t d", p=P)
        out_v = out.rearrange("(t p) d -> p t d", p=P)
        attr = a["edge_attr_64"].rearrange("(t p) d -> p t d", p=P)
        h_v = h_rows.rearrange("(t p) d -> p t d", p=P)
        ns_v = [t[0:NODES, :].rearrange("(t p) d -> p t d", p=P) for t in node_sum]
        es_v = [t[0:NODES, :].rearrange("(t p) d -> p t d", p=P) for t in edge_sum]
        sx_v = slot_x[0:E * SLOTS, :].rearrange("(e p t) d -> e p t d", e=E, t=ST)
        sy_v = slot_y[0:E * SLOTS, :].rearrange("(e p t) d -> e p t d", e=E, t=ST)

        s_dve, s_pool, s_act = sem("dve_steps"), sem("pool_steps"), sem("act_steps")
        s_raw, s_x, s_wA, s_cst, s_wB, s_b2r = sem("raw_ends_in"), sem("x_in"), sem("wA_in"), sem("small_in"), sem("wB_in"), sem("b2rows_in")
        s_zero, s_zeroed, s_ztab = sem("zeros_set"), sem("scratch_zeroed"), sem("tables_zeroed")
        s_iota, s_const = sem("iotas_set"), sem("constants_set")
        s_rawf, s_rawT, s_ends = sem("ends_as_float"), sem("ends_transposed"), sem("ends_in_columns")
        s_row, s_va = [sem(f"edge_rows_in{i}") for i in range(2)], [sem(f"edge_attr_in{i}") for i in range(2)]
        s_esel, s_emm, s_ecp = sem("edge_select_set"), sem("edge_sums_in_psum"), sem("edge_sums_in_sbuf")
        s_tab = [sem(f"edge_scattered{k}") for k in range(K)]
        s_deg, s_dis = sem("degrees_set"), sem("dis_set")
        s_part, s_added, s_agg = sem("edge_table_in"), sem("edge_table_added"), sem("edge_means_set")
        s_bA, s_bAset = sem("u_term_in_psum"), sem("biasA_set")
        s_v0, s_r0, s_x0 = sem("ln0_var"), sem("ln0_rstd"), sem("ln0_rows")
        s_t0, s_t0e, s_h0, s_h0e = sem("ln0_T_in_psum"), sem("ln0_T_in_sbuf"), sem("mlp_hidden_in_psum"), sem("mlp_hidden_in_sbuf")
        s_o0, s_o0e = sem("mlp_out_in_psum"), sem("mlp_out_read")
        s_v1, s_r1, s_x1, s_t1, s_t1e = sem("ln1_var"), sem("ln1_rstd"), sem("ln1_rows"), sem("ln1_T_in_psum"), sem("ln1_T_in_sbuf")
        s_mean, s_lg, s_e1, s_e1x, s_e2x, s_rid = sem("mean_set"), sem("logits_in_psum"), sem("router_args"), sem("router_exp"), sem("router_rows"), sem("router_ids")
        s_wb, s_wbc, s_wBs = sem("router_w_in_psum"), sem("router_w_set"), sem("wB2_scaled")
        s_hB, s_hBe, s_oB, s_oBe = sem("ffn0_hidden_in_psum"), sem("ffn0_hidden_in_sbuf"), sem("ffn0_out_in_psum"), sem("ffn0_out_read")
        s_vB, s_rB = sem("lnB_var"), sem("lnB_rstd")
        s_v2, s_r2, s_x2, s_t2, s_t2e = sem("ln2_var"), sem("ln2_rstd"), sem("ln2_rows"), sem("ln2_T_in_psum"), sem("ln2_T_in_sbuf")
        s_hm, s_hrow, s_hw = sem("h_in_psum"), sem("h_in_sbuf"), [sem(f"h_written{i}") for i in range(2)]
        s_dsel, s_ga, s_mmm, s_mcp = sem("msg_select_set"), [sem(f"msg_gathered{i}") for i in range(2)], sem("msg_sums_in_psum"), sem("msg_sums_in_sbuf")
        s_drow = [sem(f"dst_rows_in{i}") for i in range(2)]
        s_mt = [sem(f"msg_scattered{k}") for k in range(K)]
        s_nt = [sem(f"node_tables_in{i}") for i in range(2)]
        s_nadd = sem("node_tables_added")
        s_v3, s_r3, s_x3, s_x3c, s_t3, s_t3e, s_l3, s_l3e = sem("ln3_var"), sem("ln3_rstd"), sem("ln3_rows"), sem("ln3_rows_kept"), sem("ln3_T_in_psum"), sem("ln3_T_in_sbuf"), sem("gate_in_psum"), sem("gate_in_sbuf")
        s_ga1, s_gexp, s_goh, s_grk, s_slots = sem("gate_args"), sem("gate_exp"), sem("gate_onehot"), sem("gate_ranks"), sem("slots_set")
        s_disp = sem("rows_dispatched")
        s_xe, s_wE = [sem(f"slot_rows_in{i}") for i in range(2)], [sem(f"wE_in{i}") for i in range(2)]
        s_t5, s_t5e, s_h5, s_h5e, s_o5, s_o5e = sem("slots_T_in_psum"), sem("slots_T_in_sbuf"), sem("ffn1_hidden_in_psum"), sem("ffn1_hidden_in_sbuf"), sem("ffn1_out_in_psum"), sem("ffn1_out_read")
        s_y5, s_yw = sem("slot_y_set"), [sem(f"slot_y_written{i}") for i in range(2)]
        s_yg = [sem(f"rows_returned{i}") for i in range(T // EB)]
        s_fin, s_out = sem("out_set"), sem("out_written")

        QN = E * ST // GT
        QE = ST // GT
        block = ctx.enter_context(nc.Block())

        @block.sync
        def _(sp):
            steps = Steps()
            sp.dma_start(raw_i[:, 0], a["src"].rearrange("(c t p) -> t c p", c=8, p=P)).then_inc(s_raw, 16)
            sp.dma_start(raw_i[:, 1], a["dst"].rearrange("(c t p) -> t c p", c=8, p=P)).then_inc(s_raw, 16)

            def load_block(b, s=None):
                s = b % 2 if s is None else s
                if not (isinstance(b, int) and b < 2):
                    sp.wait_ge(s_emm, b - 1)
                sp.dma_start(rowb[:, s], a["src"][bass.ds(b * (EB * P), EB * P)].partition_broadcast(P)
                             .rearrange("p (t q) -> p t q", t=EB)).then_inc(s_row[s], 16)
                sp.dma_start(va[:, s], attr[:, bass.ds(b * EB, EB), :]).then_inc(s_va[s], 16)

            in_turns(sp, steps, load_block, B, 2, 2, 2)
            sp.wait_ge(s_deg, 1)
            w1 = a["L0_gnn_W1"]
            sp.dma_start(wA1[:, 0:2, :], w1[0:D, :].rearrange("(c p) f -> p c f", p=128)).then_inc(s_wA, 16)
            sp.dma_start(wA1[0:DE, 2, :], w1[D:D + DE, :]).then_inc(s_wA, 16)
            sp.dma_start(wU, w1[D + DE:D + DE + DG, :]).then_inc(s_wA, 16)
            sp.dma_start(wA2, a["L0_gnn_W2"].rearrange("(c p) d -> p c d", p=128)).then_inc(s_wA, 16)
            for k in range(K):
                sp.wait_ge(s_tab[k], 16 * EB // K * B)
                if k >= 2:
                    sp.wait_ge(s_added, k - 1)
                sp.dma_start((part if k else agg).rearrange("p (t d) -> p t d", t=T), es_v[k]).then_inc(s_part, 16)
                if k:
                    sp.wait_ge(s_added, k)
            sp.wait_ge(s_rid, 1)
            for k in range(2):
                e = sp.value_load(rt_id[0:1, k:k + 1], min_val=0, max_val=E - 1)
                sp.dma_start(wB1[:, :, k * HID1:(k + 1) * HID1],
                             a["L0_ffn_W1"][bass.ds(e, 1)].rearrange("a (c p) f -> p (a c) f", p=128)).then_inc(s_wB, 16)
                sp.dma_start(wB2[:, 4 * k:4 * k + 4, :],
                             a["L0_ffn_W2"][bass.ds(e, 1)].rearrange("a (c p) d -> p (a c) d", p=128)).then_inc(s_wB, 16)
                with nc.allow_non_contiguous_dma(reason="a bias as a column"):
                    sp.dma_start(bB1[:, 4 * k:4 * k + 4],
                                 a["L0_ffn_b1"][bass.ds(e, 1)].rearrange("a (c p) -> p (a c)", p=128)).then_inc(s_wB, 16)
                sp.dma_start(b2rows[:, k, :], a["L0_ffn_b2"][bass.ds(e, 1)]).then_inc(s_b2r, 16)

            def store_h(g, s=None):
                s = g % 2 if s is None else s
                sp.wait_ge(s_hrow, g + 1)
                sp.dma_start(h_v[:, bass.ds(g * GT, GT), :], hb[:, s]).then_inc(s_hw[s], 16)

            in_turns(sp, steps, store_h, G, 2, 3, 2)

            def load_dst(b, s=None):
                s = b % 2 if s is None else s
                if isinstance(b, int) and b < 2:
                    sp.wait_ge(s_t2, G)
                else:
                    sp.wait_ge(s_dsel, b - 1)
                sp.dma_start(rowb[:, s], a["dst"][bass.ds(b * (EB * P), EB * P)].partition_broadcast(P)
                             .rearrange("p (t q) -> p t q", t=EB)).then_inc(s_drow[s], 16)

            in_turns(sp, steps, load_dst, B, 2, 2, 2)
            for k in range(K):
                sp.wait_ge(s_mt[k], 16 * EB // K * B)

            def load_tables(g, s=None):
                s = g % 2 if s is None else s
                if not (isinstance(g, int) and g < 2):
                    sp.wait_ge(s_nadd, g - 1)
                for k in range(K):
                    sp.dma_start(tab[:, s, k], ns_v[k][:, bass.ds(g * GT, GT), :]).then_inc(s_nt[s], 16)

            in_turns(sp, steps, load_tables, G, 2, 3, 2)

            def load_expert(e, s=None):
                s = e % 2 if s is None else s
                if isinstance(e, int) and e < 2:
                    if e == 0:
                        sp.wait_ge(s_slots, 1)
                else:
                    sp.wait_ge(s_o5e, (e - 1) * QE)
                sp.dma_start(w1E[:, s], a["L1_ffn_w1"][bass.ds(e, 1)].rearrange("a (c p) f -> p (a c) f", p=128)).then_inc(s_wE[s], 16)
                sp.dma_start(w2E[:, s], a["L1_ffn_w2"][bass.ds(e, 1)].rearrange("a (c p) d -> p (a c) d", p=128)).then_inc(s_wE[s], 16)
                with nc.allow_non_contiguous_dma(reason="a bias as a column"):
                    sp.dma_start(b1E[:, s], a["L1_ffn_b1"][bass.ds(e, 1)].rearrange("a (c p) -> p (a c)", p=128)).then_inc(s_wE[s], 16)
                sp.dma_start(b2E[:, s], a["L1_ffn_b2"][bass.ds(e, 1)].rearrange("a d -> (a d)").partition_broadcast(P)).then_inc(s_wE[s], 16)
                if isinstance(e, int) and e == 0:
                    sp.wait_ge(s_disp, 16 * T)
                sp.dma_start(xe[:, s], sx_v[bass.ds(e, 1)].rearrange("a p t d -> p (a t) d")).then_inc(s_xe[s], 16)

            load_expert(0)
            load_expert(1)

            def expert_io(e, s=None):
                s0 = e % 2 if s is None else s
                for j in range(QE):
                    sp.wait_ge(s_y5, e * QE + (j + 1))
                    sp.dma_start(sy_v[bass.ds(e, 1), :, GT * j:GT * (j + 1), :].rearrange("a p t d -> p (a t) d"),
                                 yb[:, j % 2]).then_inc(s_yw[j % 2], 16)
                if not (isinstance(e, int) and e >= E - 2):
                    load_expert(e + 2, s0)

            in_turns(sp, steps, expert_io, E, 2, 2, 2)
            for c in range(T // EB):
                sp.wait_ge(s_fin, c + 1)
                sp.dma_start(out_v[:, c * EB:(c + 1) * EB, :], x[:, c * EB:(c + 1) * EB, :]).then_inc(s_out, 16)
            sp.wait_ge(s_out, 16 * (T // EB))
            sp.wait_ge(s_zeroed, 16 * 10)

        @block.scalar
        def _(act):
            steps = Steps()
            act.dma_start(x[:, :, :], x_in).then_inc(s_x, 16)
            act.wait_ge(s_zero, 1)
            z = hT[0:P, 0, :, :].rearrange("p m n -> p (m n)")
            zf = z[:, 0:(T + 1) * DE // 2]
            for k in range(K):
                for c in range(2):
                    act.dma_start(edge_sum[k].rearrange("(p t) d -> p (t d)", p=P)[:, c * 1632:(c + 1) * 1632], zf).then_inc(s_ztab, 16)
            def row(name):
                return a[name].partition_broadcast(P)
            with nc.allow_non_contiguous_dma(reason="biases and u[0] as columns"):
                act.dma_start(b1A[:, :], a["L0_gnn_b1"].rearrange("(c p) -> p c", p=128)).then_inc(s_cst, 16)
                act.dma_start(u0[:, :], a["L0_gnn_u"][0:1, :].rearrange("a p -> p a")).then_inc(s_cst, 16)
            act.dma_start(b2A[:, :], row("L0_gnn_b2")).then_inc(s_cst, 16)
            act.dma_start(wr[:, :, :], a["L0_ffn_Wr"].rearrange("(c p) e -> p c e", p=128)).then_inc(s_cst, 16)
            act.dma_start(rt[:, 0, :], a["L0_ffn_br"].rearrange("(a e) -> a e", a=1)).then_inc(s_cst, 16)
            act.dma_start(gamma[:, :], row("L0_ffn_gamma")).then_inc(s_cst, 16)
            act.dma_start(beta[:, :], row("L0_ffn_beta")).then_inc(s_cst, 16)
            act.dma_start(wG[:, :, :], a["L1_gnn_W"].rearrange("(c p) e -> p c e", p=128)).then_inc(s_cst, 16)
            act.dma_start(gw[:, :, :], a["L1_ffn_gate_w"].rearrange("(c p) e -> p c e", p=128)).then_inc(s_cst, 16)
            act.dma_start(gb[:, :], row("L1_ffn_gate_b")).then_inc(s_cst, 16)
            for k in range(K):
                for c in range(8):
                    act.dma_start(node_sum[k].rearrange("(p t) d -> p (t d)", p=P)[:, c * 1632:(c + 1) * 1632], zf).then_inc(s_zeroed, 16)
            sx_z = slot_x[0:E * SLOTS, :].rearrange("(p c r) d -> p c (r d)", p=P, c=16)
            for c in range(16):
                act.dma_start(sx_z[:, c, :], z[:, 0:4 * XW]).then_inc(s_zeroed, 16)
            act.dma_start(slot_y[E * SLOTS:E * SLOTS + P, :], z[:, 0:D]).then_inc(s_zeroed, 16)

            def edge_copy(b, s=None):
                s = b % 2 if s is None else s
                act.wait_ge(s_emm, b + 1)
                if not (isinstance(b, int) and b < 2):
                    for k in range(K):
                        act.wait_ge(s_tab[k], 16 * EB // K * (b - 1))
                act.activation(ma[:, s].rearrange("p (h t) d -> p h (t d)", h=2),
                               ps[0:P, 2 + 2 * s:4 + 2 * s, 0:EB // 2 * DE], ACT.Copy).then_inc(s_ecp, 1)

            in_turns(act, steps, edge_copy, B, 2, 2, 2)

            act.wait_ge(s_bA, 1)
            act.wait_ge(s_cst, 160)
            for m in range(4):
                i_ = act.activation(biasA[:, m:m + 1], ps[:, 7, m:m + 1], ACT.Identity, bias=b1A[:, m:m + 1])
            i_.then_inc(s_bAset, 1)
            act.wait_ge(s_bAset, 1)
            act.wait_ge(s_zeroed, 16 * (8 * K + 17))

            def T0_copy(g, s):
                act.wait_ge(s_t0, g + 1)
                act.activation(xTg[:, s], ps[:, s, 0:2 * N].rearrange("p (c n) -> p c n", c=2), ACT.Copy)
                act.activation(aT[:, s], ps[0:DE, 6, s * N:(s + 1) * N], ACT.Copy).then_inc(s_t0e, 1)

            def T1_copy(g, s):
                act.wait_ge(s_t1, g + 1)
                for c in range(2):
                    i_ = act.activation(xnT[:, c, bass.ds(g * N, N)], ps[:, 7, c * N:(c + 1) * N], ACT.Copy,
                                        accum_out=msum[:, c, bass.ds(g, 1)])
                i_.then_inc(s_t1e, 1)

            def mlp(g, s=None):
                fixed = isinstance(g, int)
                s = g % 2 if s is None else s
                if not (fixed and g == G - 1):
                    T0_copy(g + 1, 1 - s)
                if not (fixed and g < 2):
                    act.wait_ge(s_o0, g - 1)
                for m in range(4):
                    act.wait_ge(s_h0, g * 4 + (m + 1))
                    act.activation(hT[:, s, m, :], ps[:, 2 + m % 2, 0:N], ACT.Relu, bias=biasA[:, m:m + 1]).then_inc(s_h0e, 1)
                if not (fixed and g == 0):
                    T1_copy(g - 1, 1 - s)

            T0_copy(0, 0)
            in_turns(act, steps, mlp, G, 2, 3, 2)
            T1_copy(G - 1, (G - 1) % 2)

            act.wait_ge(s_e1, 1)
            act.activation(rt[:, 2, :], rt[:, 1, :], ACT.Exp, accum_out=rt[:, 9, 0:1]).then_inc(s_e1x, 1)
            act.wait_ge(s_e1, 2)
            act.activation(rt[:, 5, :], rt[:, 4, :], ACT.Exp, accum_out=rt[:, 9, 2:3]).then_inc(s_e1x, 1)
            act.wait_ge(s_e1, 3)
            act.activation(rt[:, 11, 0:2], rt[:, 10, 0:2], ACT.Exp, accum_out=rt[:, 9, 4:5]).then_inc(s_e1x, 1)

            act.wait_ge(s_wbc, 1)
            act.wait_ge(s_wB, 96)
            for k in range(2):
                i_ = act.activation(wB2[:, 4 * k:4 * k + 4, :], wB2[:, 4 * k:4 * k + 4, :], ACT.Copy, scale=wcol[:, k:k + 1])
            i_.then_inc(s_wBs, 1)

            def h_copy(g, s, turns):
                act.wait_ge(s_t2, g + 1)
                act.activation(xTg[:, s], ps[:, s, 0:2 * N].rearrange("p (c n) -> p c n", c=2), ACT.Copy).then_inc(s_t2e, 1)
                act.wait_ge(s_hm, g + 1)
                if not (isinstance(turns, int) and turns == 0):
                    act.wait_ge(s_hw[s], turns * 16)
                for t in range(GT):
                    i_ = act.activation(hb[:, s, t, :], ps[0:P, 7, t * D:(t + 1) * D], ACT.Copy, scale=dis[:, bass.ds(g * GT + t, 1)])
                i_.then_inc(s_hrow, 1)

            def ffn0(g, s, turns):
                fixed = isinstance(g, int)
                if not (fixed and g < 2):
                    act.wait_ge(s_oB, g - 1)
                for m in range(8):
                    act.wait_ge(s_hB, g * 8 + (m + 1))
                    act.activation(hT[:, s, m, :], ps[:, 2 + m % 2, 0:N], ACT.Gelu, bias=bB1[:, m:m + 1]).then_inc(s_hBe, 1)
                if not (fixed and g < 2):
                    h_copy(g - 2, s, turns - 1)

            for g in range(4):
                ffn0(g, g % 2, g // 2)
            with act.Fori(2, G // 2) as i:
                for s in range(2):
                    ffn0(i * 2 + s, s, i)
            ffn0(G - 1, 0, G // 2)
            h_copy(G - 2, 1, (G - 2) // 2)
            h_copy(G - 1, 0, (G - 1) // 2)

            def msg_copy(b, s=None):
                s = b % 2 if s is None else s
                act.wait_ge(s_mmm, b + 1)
                if not (isinstance(b, int) and b < 2):
                    for k in range(K):
                        act.wait_ge(s_mt[k], 16 * EB // K * (b - 1))
                act.activation(ms[:, s].rearrange("p (h t) d -> p h (t d)", h=5), ps[0:P, 0:5, :], ACT.Copy).then_inc(s_mcp, 1)

            in_turns(act, steps, msg_copy, B, 2, 2, 2)

            def gate_copy(g, s=None):
                s = g % 2 if s is None else s
                act.wait_ge(s_x3, g + 1)
                act.activation(xn3[:, bass.ds(g * GT, GT), 0:D], xh[:, s], ACT.Copy).then_inc(s_x3c, 1)
                act.wait_ge(s_t3, g + 1)
                act.activation(xTg[:, s], ps[:, s, 0:2 * N].rearrange("p (c n) -> p c n", c=2), ACT.Copy).then_inc(s_t3e, 1)

            in_turns(act, steps, gate_copy, G, 2, 3, 2)
            act.wait_ge(s_ga1, 1)
            act.activation(gate[:, 1, :], gate[:, 1, :], ACT.Exp).then_inc(s_gexp, 1)

            def T5_copy(q, s):
                act.wait_ge(s_t5, q + 1)
                act.activation(xTg[:, s], ps[:, s, 0:2 * N].rearrange("p (c n) -> p c n", c=2), ACT.Copy).then_inc(s_t5e, 1)

            def expert(e, es=None):
                fixed = isinstance(e, int)
                es = e % 2 if es is None else es
                act.wait_ge(s_wE[es], (e // 2 + 1) * 64 if fixed else wE_turn[0] * 64)
                for j in range(QE):
                    q, s = e * QE + j, j % 2
                    if not (fixed and e == E - 1 and j == QE - 1):
                        T5_copy(q + 1, 1 - s)
                    if not (fixed and q < 2):
                        act.wait_ge(s_o5, q - 1)
                    for m in range(8):
                        act.wait_ge(s_h5, q * 8 + (m + 1))
                        act.activation(hT[:, s, m, :], ps[:, 2 + m % 2, 0:N], ACT.Relu, bias=b1E[:, es, m:m + 1]).then_inc(s_h5e, 1)

            T5_copy(0, 0)
            wE_turn = [None]
            expert(0)
            expert(1)
            with act.Fori(1, E // 2 - 1) as i:
                wE_turn[0] = i + 1
                expert(i * 2, 0)
                expert(i * 2 + 1, 1)
            expert(E - 2)
            expert(E - 1)

        @block.gpsimd
        def _(pool):
            steps = Steps()
            nc.gpsimd.memset(ident[:, :], 0.0).then_inc(s_pool, steps.up())
            nc.gpsimd.memset(not_first[:, :], 0.0).then_inc(s_pool, steps.up())
            nc.gpsimd.memset(before[:, :], 0.0).then_inc(s_pool, steps.up())
            nc.gpsimd.memset(ones[:, :], 1.0).then_inc(s_pool, steps.up())
            nc.gpsimd.memset(neg_half[:, :], -0.5).then_inc(s_pool, steps.up())
            nc.gpsimd.iota(iota_i[:, :], [[1, P]], base=0, channel_multiplier=0).then_inc(s_pool, steps.up())
            pool.wait_ge(s_pool, steps.value())
            nc.gpsimd.affine_select(out=ident[:, :], in_=ident[:, :], compare_op=ALU.not_equal, fill=1.0, base=0,
                                    pattern=[[-1, 128]], channel_multiplier=1).then_inc(s_pool, steps.up())
            nc.gpsimd.affine_select(out=before[:, :], in_=before[:, :], compare_op=ALU.is_ge, fill=1.0, base=0,
                                    pattern=[[-1, P]], channel_multiplier=1).then_inc(s_pool, steps.up())
            nc.gpsimd.affine_select(out=not_first[:, :], in_=not_first[:, :], compare_op=ALU.is_ge, fill=1.0, base=0,
                                    pattern=[[1, P]], channel_multiplier=-1).then_inc(s_pool, steps.up())
            nc.gpsimd.tensor_copy(lo_iota[:, :], iota_i[:, :]).then_inc(s_pool, steps.up())
            nc.gpsimd.tensor_copy(hi_iota[:, :], iota_i[:, 0:T]).then_inc(s_pool, steps.up())
            nc.gpsimd.tensor_copy(e_iota[:, :], iota_i[:, 0:E]).then_inc(s_pool, steps.up())
            pool.wait_ge(s_pool, steps.value())
            nc.gpsimd.iota(iota_i[:, 0:T], [[P, T]], base=0, channel_multiplier=1).then_inc(s_pool, steps.up())
            pool.wait_ge(s_pool, steps.value())
            nc.gpsimd.tensor_copy(n_iota[:, :], iota_i[:, 0:T]).then_inc(s_pool, steps.up())
            nc.gpsimd.tensor_scalar(spare[:, :], iota_i[:, 0:1], float(NODES), None, ALU.add).then_inc(s_pool, steps.up())
            pool.wait_ge(s_pool, steps.value())
            nc.gpsimd.memset(iota_i[:, :], 0).then_inc(s_const, 1)

            pool.wait_ge(s_ztab, 16 * 2 * K)

            def edge_scatter(b, s=None):
                s = b % 2 if s is None else s
                pool.wait_ge(s_ecp, b + 1)
                for i in range(EB):
                    k = i % K
                    if not (isinstance(b, int) and b == 0 and i < K):
                        pool.wait_ge(s_tab[k], b * (16 * EB // K) + 16 * (i // K))
                    pool.nop(nofuse=True)
                    nc.gpsimd.indirect_dma_start(edge_sum[k], bass.IndirectOffsetOnAxis(idx_a[:, s, i:i + 1], 0),
                                                 ma[:, s, i, :], None, compute_op=ALU.add).then_inc(s_tab[k], 16)

            in_turns(pool, steps, edge_scatter, B, 2, 2, 2)
            pool.wait_ge(s_deg, 1)
            nc.gpsimd.tensor_tensor(dis[:, :], deg[:, :], neg_half[:, :], ALU.pow).then_inc(s_pool, steps.up())
            pool.wait_ge(s_pool, steps.value())
            nc.gpsimd.tensor_tensor(dis[:, :], dis[:, :], has[:, :], ALU.mult).then_inc(s_dis, 1)

            def root(ready, done, n, out_, in_):
                pool.wait_ge(ready, n)
                nc.gpsimd.tensor_tensor(out_, in_, neg_half[:, 0:GT], ALU.pow).then_inc(done, 1)

            def mlp_roots(g, s=None):
                s = g % 2 if s is None else s
                if not (isinstance(g, int) and g >= G - 2):
                    root(s_v0, s_r0, g + 3, rstd[:, s, :], var[:, s, :])
                root(s_v1, s_r1, g + 1, rstd1[:, bass.ds(g * GT, GT)], var2[:, s, :])

            root(s_v0, s_r0, 1, rstd[:, 0, :], var[:, 0, :])
            root(s_v0, s_r0, 2, rstd[:, 1, :], var[:, 1, :])
            in_turns(pool, steps, mlp_roots, G, 2, 3, 2)

            def ffn0_roots(g, s=None):
                s = g % 2 if s is None else s
                root(s_vB, s_rB, g + 1, rstd[:, s, :], var[:, s, :])
                root(s_v2, s_r2, g + 1, rstd2[:, s, :], var2[:, s, :])

            in_turns(pool, steps, ffn0_roots, G, 2, 3, 2)

            pool.wait_ge(s_hw[0], 16 * ((G + 1) // 2))
            pool.wait_ge(s_hw[1], 16 * (G // 2))
            pool.wait_ge(s_zeroed, 16 * (8 * K + 17))

            def gather(b, s):
                pool.wait_ge(s_dsel, b + 1)
                if not (isinstance(b, int) and b < 2):
                    pool.wait_ge(s_mmm, b - 1)
                pool.nop(nofuse=True)
                for i in range(EB):
                    nc.gpsimd.indirect_dma_start(mg[:, s, i, :], None, h_rows, bass.IndirectOffsetOnAxis(idx_a[:, s, i:i + 1], 0)).then_inc(s_ga[s], 16)

            def messages(b, s=None):
                s = b % 2 if s is None else s
                if not (isinstance(b, int) and b == B - 1):
                    gather(b + 1, 1 - s)
                pool.wait_ge(s_mcp, b + 1)
                for i in range(EB):
                    k = i % K
                    if not (isinstance(b, int) and b == 0 and i < K):
                        pool.wait_ge(s_mt[k], b * (16 * EB // K) + 16 * (i // K))
                    pool.nop(nofuse=True)
                    nc.gpsimd.indirect_dma_start(node_sum[k], bass.IndirectOffsetOnAxis(idx_b[:, s, i:i + 1], 0),
                                                 ms[:, s, i, :], None, compute_op=ALU.add).then_inc(s_mt[k], 16)

            gather(0, 0)
            in_turns(pool, steps, messages, B, 2, 2, 2)

            def gate_roots(g, s=None):
                s = g % 2 if s is None else s
                root(s_v3, s_r3, g + 1, rstd[:, s, :], var[:, s, :])

            in_turns(pool, steps, gate_roots, G, 2, 3, 2)
            pool.wait_ge(s_slots, 1)
            pool.wait_ge(s_x3c, G)
            for t in range(T):
                nc.gpsimd.indirect_dma_start(slot_x, bass.IndirectOffsetOnAxis(sc_idx[:, t:t + 1], 0), xn3[:, t, :], None).then_inc(s_disp, 16)
            pool.wait_ge(s_yw[0], 16 * (QN // 2))
            pool.wait_ge(s_yw[1], 16 * (QN // 2))
            pool.wait_ge(s_t5, QN)
            pool.wait_ge(s_o5e, QN)
            for t in range(T):
                nc.gpsimd.indirect_dma_start(yg[:, t, :], None, slot_y, bass.IndirectOffsetOnAxis(ga_idx[:, t:t + 1], 0)).then_inc(s_yg[t // EB], 16)

        @block.vector
        def _(dve):
            v = nc.vector
            st = Steps()

            def settle():
                dve.wait_ge(s_dve, st.value())

            def settle_fixed():
                settle()
                dve.nop(nofuse=True)

            v.memset(hT[:, 0, :, :], 0.0).then_inc(s_zero, 1)
            dve.wait_ge(s_raw, 32)
            v.tensor_copy(raw_f, raw_i).then_inc(s_rawf, 1)
            dve.wait_ge(s_rawT, 1)
            for k, f in enumerate((src_f, dst_f)):
                v.tensor_copy(f[:, :].rearrange("p (h c t) -> p h (c t)", h=2, c=4), ps[0:P, 2 * k:2 * k + 2, 0:400]).then_inc(s_dve, st.up())
            settle()
            dve.wait_ge(s_const, 1)
            for k, f in enumerate((src_f, dst_f)):
                hi, lo, fv = hilo[2 * k], hilo[2 * k + 1], f[:, :]
                v.tensor_scalar(hl_i, fv, 1.0 / P, None, ALU.mult).then_inc(s_dve, st.up())
                settle()
                v.tensor_copy(hi, hl_i).then_inc(s_dve, st.up())
                settle()
                v.scalar_tensor_tensor(lo, hi, -float(P), fv, ALU.mult, ALU.add).then_inc(s_dve, st.up())
                settle()
                for sign, op, bound in ((-1.0, ALU.is_lt, 0.0), (1.0, ALU.is_ge, float(P))):
                    v.tensor_scalar(hl_w, lo, bound, sign, op, ALU.mult).then_inc(s_dve, st.up())
                    settle()
                    v.tensor_tensor(hi, hi, hl_w, ALU.add).then_inc(s_dve, st.up())
                    v.scalar_tensor_tensor(lo, hl_w, -float(P), lo, ALU.mult, ALU.add).then_inc(s_dve, st.up())
                    settle()

            def rows_to_add(s, col, idx, done):
                v.tensor_tensor(SL, S[:, s], not_first[:, :].unsqueeze(1).to_broadcast([P, EB, P]), ALU.mult).then_inc(s_dve, st.up())
                v.tensor_scalar(away[:, s], col, -1.0, spare[:, 0:1], ALU.mult, ALU.add).then_inc(s_dve, st.up())
                settle()
                v.tensor_reduce(dup[:, s], SL, AX, ALU.max).then_inc(s_dve, st.up())
                settle()
                v.tensor_tensor(firsts[:, s], dup[:, s], away[:, s], ALU.mult).then_inc(s_dve, st.up())
                settle()
                v.tensor_tensor(idx[:, s], firsts[:, s], col, ALU.add).then_inc(done, 1)

            def edge_select(b, s=None):
                fixed = isinstance(b, int)
                s = b % 2 if s is None else s
                dve.wait_ge(s_row[s], (b // 2 + 1) * 16 if fixed else turn[0] * 16)
                if not (fixed and b < 2):
                    dve.wait_ge(s_emm, b - 1)
                    for k in range(K):
                        dve.wait_ge(s_tab[k], (b - 1) * (16 * EB // K))
                tiles = bass.ds(b * EB, EB)

                def col(c, n):
                    return c[:, tiles].unsqueeze(2).to_broadcast([P, EB, n])

                def row(r, n):
                    return r[:, 0:n].unsqueeze(1).to_broadcast([P, EB, n])
                v.tensor_tensor(S[:, s], rowb[:, s], col(src_f, P), ALU.is_equal).then_inc(s_dve, st.up())
                for k in range(2):
                    v.tensor_tensor(ohh[k][:, s], row(hi_iota, T), col(hilo[2 * k], T), ALU.is_equal).then_inc(s_dve, st.up())
                    v.tensor_tensor(ohl[k][:, s], row(lo_iota, P), col(hilo[2 * k + 1], P), ALU.is_equal).then_inc(s_dve, st.up())
                settle()
                rows_to_add(s, src_f[:, tiles], idx_a, s_esel)

            turn = [None]
            edge_select(0)
            before_ = st.value()
            edge_select(1)
            per, start = st.value() - before_, st.value()
            with dve.Fori(1, B // 2) as i:
                turn[0] = i + 1
                for s in range(2):
                    st.base, st.k = start + (i * 2 + s - 2) * per, 0
                    edge_select(i * 2 + s, s)
            st.base, st.k = start + (B - 2) * per, 0

            dve.wait_ge(s_emm, B)
            v.tensor_scalar(cnt[:, :], ps[0:P, 6, 0:T], 1.0, None, ALU.max).then_inc(s_dve, st.up())
            v.tensor_scalar(has[:, :], ps[0:P, 7, 0:T], 0.0, None, ALU.is_gt).then_inc(s_dve, st.up())
            settle()
            v.reciprocal(cnt[:, :], cnt[:, :]).then_inc(s_dve, st.up())
            settle()
            v.tensor_scalar(deg[:, :], ps[0:P, 7, 0:T], 1.0, None, ALU.max).then_inc(s_deg, 1)
            for k in range(1, K):
                dve.wait_ge(s_part, 16 * (k + 1))
                v.tensor_tensor(agg, agg, part, ALU.add).then_inc(s_added, 1)
                dve.wait_ge(s_added, k)

            def ln_stats(rows, s, stat_, mv_of, var_, ready):
                dve.nop(nofuse=True)
                for t in range(GT):
                    v.bn_stats(stat_[:, s, t, :], rows(t)).then_inc(s_dve, st.up())
                settle_fixed()
                for t in range(GT):
                    v.bn_aggr(mv_of(t), stat_[:, s, t, :]).then_inc(s_dve, st.up())
                settle()
                for t in range(GT):
                    i_ = v.tensor_scalar(var_[:, s, t:t + 1], mv_of(t)[:, 1:2], EPS, None, ALU.add)
                i_.then_inc(ready, 1)

            def ln0(g, s):
                ln_stats(lambda t: x[:, bass.ds(g * GT + t, 1), :].rearrange("p a d -> p (a d)"), s, stat,
                         lambda t: mv[:, s, t, :], var, s_v0)
                dve.wait_ge(s_r0, g + 1)
                if not (isinstance(g, int) and g < 2):
                    dve.wait_ge(s_t0, g - 1)
                for t in range(GT):
                    v.tensor_scalar(xg[:, s, t, 0:D], x[:, bass.ds(g * GT + t, 1), :].rearrange("p a d -> p (a d)"),
                                    mv[:, s, t, 0:1], rstd[:, s, t:t + 1], ALU.subtract, ALU.mult)
                    i_ = v.tensor_scalar(xg[:, s, t, D:D + DE], agg3[:, bass.ds(g * GT + t, 1), :].rearrange("p a d -> p (a d)"),
                                         cnt[:, bass.ds(g * GT + t, 1)], None, ALU.mult)
                i_.then_inc(s_x0, 1)

            def mlp(g, s=None):
                fixed = isinstance(g, int)
                s = g % 2 if s is None else s
                if not (fixed and g >= G - 2):
                    ln0(g + 2, s)
                xs = x[:, bass.ds(g * GT, GT), :]
                dve.wait_ge(s_o0, g + 1)
                v.tensor_tensor(yb[:, s], ps[0:P, 4 + s, :].rearrange("p (t d) -> p t d", t=GT),
                                b2A[:, :].unsqueeze(1).to_broadcast([P, GT, D]), ALU.add).then_inc(s_o0e, 1)
                dve.wait_ge(s_o0e, g + 1)
                v.tensor_tensor(xs, xs, yb[:, s], ALU.add).then_inc(s_dve, st.up())
                settle()
                ln_stats(lambda t: x[:, bass.ds(g * GT + t, 1), :].rearrange("p a d -> p (a d)"), s, stat2,
                         lambda t: mv2[:, s, t, :], var2, s_v1)
                v.tensor_copy(mv1[:, bass.ds(g * GT, GT), :], mv2[:, s]).then_inc(s_dve, st.up())
                dve.wait_ge(s_r1, g + 1)
                if not (fixed and g < 2):
                    dve.wait_ge(s_t1, g - 1)
                for t in range(GT):
                    i_ = v.tensor_scalar(xh[:, s, t, :], x[:, bass.ds(g * GT + t, 1), :].rearrange("p a d -> p (a d)"),
                                         mv2[:, s, t, 0:1], rstd1[:, bass.ds(g * GT + t, 1)], ALU.subtract, ALU.mult)
                i_.then_inc(s_x1, 1)

            dve.wait_ge(s_x, 16)
            dve.wait_ge(s_cst, 160)
            ln0(0, 0)
            ln0(1, 1)
            in_turns(dve, st, mlp, G, 2, 3, 2)

            dve.wait_ge(s_t1e, G)
            v.tensor_reduce(mean[:, :], msum[:, :, :], AX, ALU.add).then_inc(s_dve, st.up())
            settle()
            v.tensor_scalar(mean[:, :], mean[:, :], 1.0 / NODES, None, ALU.mult).then_inc(s_mean, 1)
            dve.wait_ge(s_lg, 1)
            v.tensor_tensor(rt[:, 1, :], ps[0:1, 6, 0:E], rt[:, 0, :], ALU.add).then_inc(s_dve, st.up())
            settle()

            def less_max(dst, src_, n):
                v.tensor_reduce(rt[:, 9, 6:7], src_, AX, ALU.max).then_inc(s_dve, st.up())
                settle()
                v.tensor_scalar(dst, src_, rt[:, 9, 6:7], None, ALU.subtract).then_inc(s_e1, 1)
                dve.wait_ge(s_e1x, n)

            def over_sum(dst, src_, at):
                v.reciprocal(rt[:, 9, at + 1:at + 2], rt[:, 9, at:at + 1]).then_inc(s_dve, st.up())
                settle()
                v.tensor_scalar(dst, src_, rt[:, 9, at + 1:at + 2], None, ALU.mult).then_inc(s_dve, st.up())
                settle()

            less_max(rt[:, 1, :], rt[:, 1, :], 1)
            over_sum(rt[:, 3, :], rt[:, 2, :], 0)
            v.tensor_scalar(rt[:, 6, :], rt[:, 3, :], float(NODES), None, ALU.mult).then_inc(s_dve, st.up())
            settle()
            v.reciprocal(rt[:, 7, :], rt[:, 6, :]).then_inc(s_dve, st.up())
            settle()
            v.tensor_scalar(rt[:, 8, :], rt[:, 7, :], float(CAP), 1.0, ALU.mult, ALU.min).then_inc(s_dve, st.up())
            settle()
            v.tensor_tensor(rt[:, 4, :], rt[:, 3, :], rt[:, 8, :], ALU.mult).then_inc(s_dve, st.up())
            settle()
            less_max(rt[:, 4, :], rt[:, 4, :], 2)
            over_sum(rt[:, 12, :], rt[:, 5, :], 2)
            v.max(rt[:, 13, :], rt[:, 12, :]).then_inc(s_dve, st.up())
            settle()
            v.max_index(rt_id[:, :], rt[:, 13, :], rt[:, 12, :]).then_inc(s_rid, 1)
            v.tensor_scalar(rt[:, 10, 0:2], rt[:, 13, 0:2], rt[:, 13, 0:1], None, ALU.subtract).then_inc(s_e1, 1)
            dve.wait_ge(s_e1x, 3)
            over_sum(rt[:, 14, 0:2], rt[:, 11, 0:2], 4)
            for k in range(2):
                i_ = v.tensor_copy(wrow[:, k, :], rt[:, 14, k:k + 1].to_broadcast([1, P]))
            i_.then_inc(s_e2x, 1)
            dve.wait_ge(s_wb, 1)
            v.tensor_copy(b2B[:, :], ps[0:P, 5, 0:D]).then_inc(s_dve, st.up())
            v.tensor_copy(wcol[:, :], ps[:, 4, 0:2]).then_inc(s_wbc, 1)
            dve.wait_ge(s_wbc, 1)

            def ffn0(g, s=None):
                fixed = isinstance(g, int)
                s = g % 2 if s is None else s
                xs = x[:, bass.ds(g * GT, GT), :]
                y, z = yb[:, s], wk[:, s]

                def wide(r):
                    return r[:, :].unsqueeze(1).to_broadcast([P, GT, D])
                for t in range(GT):
                    v.tensor_scalar(z[:, t, :], x[:, bass.ds(g * GT + t, 1), :].rearrange("p a d -> p (a d)"),
                                    mv1[:, bass.ds(g * GT + t, 1), 0:1].rearrange("p a d -> p (a d)"),
                                    rstd1[:, bass.ds(g * GT + t, 1)], ALU.subtract, ALU.mult).then_inc(s_dve, st.up())
                settle()
                v.tensor_tensor(z, z, wide(b2B), ALU.add).then_inc(s_dve, st.up())
                settle()
                dve.wait_ge(s_oB, g + 1)
                v.tensor_tensor(y, ps[0:P, 4 + s, :].rearrange("p (t d) -> p t d", t=GT), z, ALU.add).then_inc(s_oBe, 1)
                dve.wait_ge(s_oBe, g + 1)
                ln_stats(lambda t: y[:, t, :], s, stat, lambda t: mv[:, s, t, :], var, s_vB)
                dve.wait_ge(s_rB, g + 1)
                for t in range(GT):
                    v.tensor_scalar(z[:, t, :], y[:, t, :], mv[:, s, t, 0:1], rstd[:, s, t:t + 1], ALU.subtract, ALU.mult).then_inc(s_dve, st.up())
                settle()
                v.tensor_tensor(z, z, wide(gamma), ALU.mult).then_inc(s_dve, st.up())
                settle()
                v.tensor_tensor(z, z, wide(beta), ALU.add).then_inc(s_dve, st.up())
                settle()
                v.tensor_tensor(xs, xs, z, ALU.add).then_inc(s_dve, st.up())
                settle()
                ln_stats(lambda t: x[:, bass.ds(g * GT + t, 1), :].rearrange("p a d -> p (a d)"), s, stat2,
                         lambda t: mv2[:, s, t, :], var2, s_v2)
                dve.wait_ge(s_r2, g + 1)
                if not (fixed and g < 2):
                    dve.wait_ge(s_t2, g - 1)
                for t in range(GT):
                    i_ = v.tensor_scalar(xh[:, s, t, :], x[:, bass.ds(g * GT + t, 1), :].rearrange("p a d -> p (a d)"),
                                         mv2[:, s, t, 0:1], rstd2[:, s, t:t + 1], ALU.subtract, ALU.mult)
                i_.then_inc(s_x2, 1)

            in_turns(dve, st, ffn0, G, 2, 3, 2)

            def msg_select(b, s=None):
                fixed = isinstance(b, int)
                s = b % 2 if s is None else s
                dve.wait_ge(s_drow[s], (b // 2 + 1) * 16 if fixed else turn[0] * 16)
                if not (fixed and b < 2):
                    dve.wait_ge(s_mmm, b - 1)
                    for k in range(K):
                        dve.wait_ge(s_mt[k], (b - 1) * (16 * EB // K))
                tiles = bass.ds(b * EB, EB)
                v.tensor_copy(idx_a[:, s, :], src_f[:, tiles]).then_inc(s_dve, st.up())
                v.tensor_tensor(S[:, s], rowb[:, s], dst_f[:, tiles].unsqueeze(2).to_broadcast([P, EB, P]), ALU.is_equal).then_inc(s_dve, st.up())
                settle()
                rows_to_add(s, dst_f[:, tiles], idx_b, s_dsel)

            msg_select(0)
            before_ = st.value()
            msg_select(1)
            per, start = st.value() - before_, st.value()
            with dve.Fori(1, B // 2) as i:
                turn[0] = i + 1
                for s in range(2):
                    st.base, st.k = start + (i * 2 + s - 2) * per, 0
                    msg_select(i * 2 + s, s)
            st.base, st.k = start + (B - 2) * per, 0

            def gate_rows(g, s, turns):
                fixed = isinstance(g, int)
                dve.wait_ge(s_nt[s], turns * (16 * K))
                v.tensor_tensor(yb[:, s], tab[:, s, 0], tab[:, s, 1], ALU.add).then_inc(s_dve, st.up())
                for k in range(2, K):
                    settle()
                    v.tensor_tensor(yb[:, s], yb[:, s], tab[:, s, k], ALU.add).then_inc(s_dve, st.up())
                settle()
                for t in range(GT):
                    xs = x[:, bass.ds(g * GT + t, 1), :].rearrange("p a d -> p (a d)")
                    v.scalar_tensor_tensor(xs, yb[:, s, t, :], dis[:, bass.ds(g * GT + t, 1)], xs, ALU.mult, ALU.add).then_inc(s_dve if t < GT - 1 else s_nadd, st.up() if t < GT - 1 else 1)
                dve.wait_ge(s_nadd, g + 1)
                ln_stats(lambda t: x[:, bass.ds(g * GT + t, 1), :].rearrange("p a d -> p (a d)"), s, stat,
                         lambda t: mv[:, s, t, :], var, s_v3)
                dve.wait_ge(s_r3, g + 1)
                if not (fixed and g < 2):
                    dve.wait_ge(s_t3, g - 1)
                    dve.wait_ge(s_x3c, g - 1)
                for t in range(GT):
                    i_ = v.tensor_scalar(xh[:, s, t, :], x[:, bass.ds(g * GT + t, 1), :].rearrange("p a d -> p (a d)"),
                                         mv[:, s, t, 0:1], rstd[:, s, t:t + 1], ALU.subtract, ALU.mult)
                i_.then_inc(s_x3, 1)

            def logits(g, s):
                dve.wait_ge(s_l3, g + 1)
                v.tensor_tensor(gate3[:, 0, bass.ds(g * GT, GT), :], ps[0:P, 6 + s, 0:GT * E].rearrange("p (t e) -> p t e", t=GT),
                                gb[:, :].unsqueeze(1).to_broadcast([P, GT, E]), ALU.add).then_inc(s_l3e, 1)

            dve.wait_ge(s_dis, 1)

            def gate_group(g, s, turns):
                gate_rows(g, s, turns)
                if not (isinstance(g, int) and g == 0):
                    logits(g - 1, 1 - s)

            gate_group(0, 0, 1)
            before_ = st.value()
            gate_group(1, 1, 1)
            per, start = st.value() - before_, st.value()
            with dve.Fori(1, G // 2) as i:
                for s in range(2):
                    st.base, st.k = start + (i * 2 + s - 2) * per, 0
                    gate_group(i * 2 + s, s, i + 1)
            st.base, st.k = start + (G - 3) * per, 0
            gate_group(G - 1, 0, G // 2 + 1)
            logits(G - 1, 0)
            dve.wait_ge(s_l3e, G)

            def tt(o_, i0, i1, op):
                v.tensor_tensor(o_, i0, i1, op).then_inc(s_dve, st.up())
                settle()

            def ts(o_, i0, c1, c2, op0, op1=ALU.bypass):
                v.tensor_scalar(o_, i0, c1, c2, op0, op1).then_inc(s_dve, st.up())
                settle()

            def red(o_, i_, op):
                v.tensor_reduce(o_, i_, AX, op).then_inc(s_dve, st.up())
                settle()

            def per_token(k):
                return g50[:, k, :].unsqueeze(2).to_broadcast([P, T, E])

            def per_expert(r):
                return r.unsqueeze(1).to_broadcast([P, T, E])
            red(g50[:, 0, :], gate3[:, 0], ALU.max)
            v.tensor_tensor(gate3[:, 1], gate3[:, 0], per_token(0), ALU.subtract).then_inc(s_ga1, 1)
            dve.wait_ge(s_gexp, 1)
            red(g50[:, 1, :], gate3[:, 1], ALU.add)
            red(g50[:, 2, :], gate3[:, 1], ALU.max)
            v.reciprocal(g50[:, 3, :], g50[:, 1, :]).then_inc(s_dve, st.up())
            settle()
            tt(xn3[:, :, D:D + 1].rearrange("p t a -> p (t a)"), g50[:, 2, :], g50[:, 3, :], ALU.mult)
            tt(gate3[:, 2], gate3[:, 1], per_token(2), ALU.is_ge)
            ts(gate3[:, 3], gate3[:, 2], -float(E), float(E), ALU.mult, ALU.add)
            tt(gate3[:, 4], gate3[:, 3], per_expert(e_iota[:, :]), ALU.add)
            red(g50[:, 4, :], gate3[:, 4], ALU.min)
            v.tensor_tensor(gate3[:, 5], per_expert(e_iota[:, :]), per_token(4), ALU.is_equal).then_inc(s_goh, 1)
            dve.wait_ge(s_grk, 1)
            v.tensor_copy(gate[:, 6, :], ps[0:P, 2, 0:T * E]).then_inc(s_dve, st.up())
            v.tensor_copy(gate[:, 7, :], ps[0:P, 3, 0:T * E]).then_inc(s_dve, st.up())
            v.memset(gate[:, 8, :], 1.0).then_inc(s_dve, st.up())
            settle()
            for e in range(E):
                v.tensor_tensor_scan(gate3[:, 9, :, e], gate3[:, 8, :, e], gate3[:, 7, :, e], 0.0, ALU.mult, ALU.add).then_inc(s_dve, st.up())
            settle()
            tt(gate3[:, 9], gate3[:, 9], gate3[:, 7], ALU.subtract)
            tt(gate3[:, 9], gate3[:, 9], gate3[:, 6], ALU.add)
            tt(gate3[:, 9], gate3[:, 9], gate3[:, 5], ALU.mult)
            red(g50[:, 5, :], gate3[:, 9], ALU.add)
            ts(g50[:, 6, :], g50[:, 5, :], float(CAP), None, ALU.is_lt)
            v.scalar_tensor_tensor(g50[:, 7, :], g50[:, 4, :], float(SLOTS), g50[:, 5, :], ALU.mult, ALU.add).then_inc(s_dve, st.up())
            settle()
            ts(g50[:, 8, :], n_iota[:, :], float(E * SLOTS), None, ALU.add)
            tt(g50[:, 9, :], g50[:, 7, :], g50[:, 8, :], ALU.subtract)
            tt(g50[:, 9, :], g50[:, 9, :], g50[:, 6, :], ALU.mult)
            tt(g50[:, 9, :], g50[:, 9, :], g50[:, 8, :], ALU.add)
            v.tensor_copy(sc_idx[:, :], g50[:, 9, :]).then_inc(s_dve, st.up())
            ts(g50[:, 10, :], g50[:, 7, :], -float(E * SLOTS), None, ALU.add)
            tt(g50[:, 10, :], g50[:, 10, :], g50[:, 6, :], ALU.mult)
            ts(g50[:, 10, :], g50[:, 10, :], float(E * SLOTS), None, ALU.add)
            v.tensor_copy(ga_idx[:, :], g50[:, 10, :]).then_inc(s_slots, 1)

            def expert_out(e, es, turns):
                fixed = isinstance(e, int)
                for j in range(QE):
                    s = j % 2
                    q = e * QE + j
                    y, r = yb[:, s], nanw
                    dve.wait_ge(s_wE[es], turns * 64)
                    dve.wait_ge(s_xe[es], turns * 16)
                    dve.wait_ge(s_o5, q + 1)
                    v.tensor_tensor(r[:, 0], ps[0:P, 4 + s, :].rearrange("p (t d) -> p t d", t=GT),
                                    b2E[:, es, :].unsqueeze(1).to_broadcast([P, GT, D]), ALU.add).then_inc(s_dve, st.up())
                    settle()
                    for t in range(GT):
                        i_ = v.tensor_scalar(r[:, 1, t, :], r[:, 0, t, :], xe[:, es, GT * j + t, D:D + 1], None, ALU.mult)
                    i_.then_inc(s_o5e, 1)
                    dve.wait_ge(s_o5e, q + 1)
                    if not (fixed and q < 2):
                        dve.wait_ge(s_yw[s], (q // 2) * 16 if fixed else (turns - 1) * (16 * QE) + (es * QE + j) // 2 * 16)
                    v.tensor_scalar(r[:, 2], r[:, 1], FMAX, 1e4, ALU.is_gt, ALU.mult).then_inc(s_dve, st.up())
                    v.tensor_scalar(r[:, 0], r[:, 1], -FMAX, -1e4, ALU.is_lt, ALU.mult).then_inc(s_dve, st.up())
                    v.tensor_scalar(r[:, 3], r[:, 1], FMAX, None, ALU.is_le).then_inc(s_dve, st.up())
                    settle()
                    v.tensor_tensor(y, r[:, 2], r[:, 0], ALU.add).then_inc(s_dve, st.up())
                    v.scalar_tensor_tensor(r[:, 3], r[:, 1], -FMAX, r[:, 3], ALU.is_ge, ALU.mult).then_inc(s_dve, st.up())
                    settle_fixed()
                    v.copy_predicated(y, r[:, 3].bitcast(u32), r[:, 1]).then_inc(s_y5, 1)
                    dve.wait_ge(s_y5, q + 1)

            expert_out(0, 0, 1)
            before_ = st.value()
            expert_out(1, 1, 1)
            per, start = st.value() - before_, st.value()
            with dve.Fori(1, E // 2) as i:
                for s in range(2):
                    st.base, st.k = start + (i * 2 + s - 2) * per, 0
                    expert_out(i * 2 + s, s, i + 1)
            st.base, st.k = start + (E - 2) * per, 0

            for c in range(T // EB):
                dve.wait_ge(s_yg[c], 16 * EB)
                xs = x[:, c * EB:(c + 1) * EB, :]
                v.tensor_tensor(xs, xs, yg[:, c * EB:(c + 1) * EB, :], ALU.add).then_inc(s_fin, 1)

        @block.tensor
        def _(pe):
            steps = Steps()
            mm, tr = nc.tensor.matmul, nc.tensor.transpose
            pe.wait_ge(s_const, 1)
            pe.wait_ge(s_rawf, 1)
            for k in range(2):
                for c in range(8):
                    i_ = tr(ps[0:P, 2 * k + c // 4, (c % 4) * 100:(c % 4 + 1) * 100], raw_f[:, k, c, :], ident[0:100, 0:100])
            i_.then_inc(s_rawT, 1)

            def edge_sums(b, s, turns, first=False, last=False):
                pe.wait_ge(s_esel, b + 1)
                pe.wait_ge(s_va[s], turns * 16)
                if not first:
                    pe.wait_ge(s_ecp, b - 1)
                for i in range(EB):
                    for k in range(2):
                        mm(ps[0:P, 6 + k, 0:T], ohl[k][:, s, i, :], ohh[k][:, s, i, :],
                           start=(first and s == 0 and i == 0), stop=(last and s == 1 and i == EB - 1))
                    i_ = mm(ps[0:P, 2 + 2 * s + i // 5, (i % 5) * DE:(i % 5 + 1) * DE], S[:, s, i, :], va[:, s, i, :], start=True, stop=True)
                i_.then_inc(s_emm, 1)

            edge_sums(0, 0, 1, first=True)
            edge_sums(1, 1, 1, first=True)
            with pe.Fori(1, B // 2 - 1) as i:
                edge_sums(i * 2, 0, i + 1)
                edge_sums(i * 2 + 1, 1, i + 1)
            edge_sums(B - 2, 0, B // 2, last=True)
            edge_sums(B - 1, 1, B // 2, last=True)

            pe.wait_ge(s_wA, 64)
            pe.wait_ge(s_cst, 160)
            pe.wait_ge(s_deg, 1)
            for m in range(4):
                i_ = mm(ps[:, 7, m:m + 1], wU[:, m * 128:(m + 1) * 128], u0[:, :], start=True, stop=True)
            i_.then_inc(s_bA, 1)

            def T0(g, s):
                pe.wait_ge(s_x0, g + 1)
                if not (isinstance(g, int) and g == 0):
                    pe.wait_ge(s_t0e, g)
                for t in range(GT):
                    for c in range(2):
                        tr(ps[:, s, c * N + t * P:c * N + (t + 1) * P], xg[:, s, t, c * 128:(c + 1) * 128], ident[0:P, 0:P])
                    i_ = tr(ps[0:DE, 6, s * N + t * P:s * N + (t + 1) * P], xg[:, s, t, D:D + DE], ident[0:P, 0:P])
                i_.then_inc(s_t0, 1)

            def T1(g, s):
                pe.wait_ge(s_x1, g + 1)
                if isinstance(g, int) and g == 0:
                    pe.wait_ge(s_bAset, 1)
                else:
                    pe.wait_ge(s_t1e, g)
                for t in range(GT):
                    for c in range(2):
                        i_ = tr(ps[:, 7, c * N + t * P:c * N + (t + 1) * P], xh[:, s, t, c * 128:(c + 1) * 128], ident[0:P, 0:P])
                i_.then_inc(s_t1, 1)

            def mlp(g, s=None):
                fixed = isinstance(g, int)
                s = g % 2 if s is None else s
                if not (fixed and g == G - 1):
                    T0(g + 1, 1 - s)
                pe.wait_ge(s_t0e, g + 1)
                for m in range(4):
                    if not (fixed and g == 0 and m < 2):
                        pe.wait_ge(s_h0e, g * 4 + (m - 1))
                    f = slice(m * 128, (m + 1) * 128)
                    for c in range(2):
                        mm(ps[:, 2 + m % 2, 0:N], wA1[:, c, f], xTg[:, s, c, :], start=(c == 0), stop=False)
                    mm(ps[:, 2 + m % 2, 0:N], wA1[0:DE, 2, f], aT[:, s, :], start=False, stop=True).then_inc(s_h0, 1)
                if not (fixed and g == 0):
                    T1(g - 1, 1 - s)
                pe.wait_ge(s_h0e, g * 4 + 4)
                if not (fixed and g < 2):
                    pe.wait_ge(s_o0e, g - 1)
                for t in range(GT):
                    for m in range(4):
                        i_ = mm(ps[0:P, 4 + s, t * D:(t + 1) * D], hT[:, s, m, t * P:(t + 1) * P], wA2[:, m, :], start=(m == 0), stop=(m == 3))
                i_.then_inc(s_o0, 1)

            pe.wait_ge(s_ecp, B)
            T0(0, 0)
            in_turns(pe, steps, mlp, G, 2, 3, 2)
            T1(G - 1, (G - 1) % 2)

            pe.wait_ge(s_mean, 1)
            for c in range(2):
                i_ = mm(ps[0:1, 6, 0:E], mean[:, c:c + 1], wr[:, c, :], start=(c == 0), stop=(c == 1))
            i_.then_inc(s_lg, 1)
            pe.wait_ge(s_o0e, G)
            pe.wait_ge(s_e2x, 1)
            pe.wait_ge(s_b2r, 32)
            mm(ps[:, 4, 0:2], ones[0:1, 0:1].to_broadcast([1, 128]), rt[:, 14, 0:2], start=True, stop=True)
            for k in range(2):
                i_ = mm(ps[0:P, 5, 0:D], wrow[:, k, :], b2rows[:, k, :], start=(k == 0), stop=(k == 1))
            i_.then_inc(s_wb, 1)

            def T2(g, s):
                pe.wait_ge(s_x2, g + 1)
                if not (isinstance(g, int) and g < 2):
                    pe.wait_ge(s_t2e, g - 1)
                for t in range(GT):
                    for c in range(2):
                        i_ = tr(ps[:, s, c * N + t * P:c * N + (t + 1) * P], xh[:, s, t, c * 128:(c + 1) * 128], ident[0:P, 0:P])
                i_.then_inc(s_t2, 1)

            def H(g, s):
                pe.wait_ge(s_t2e, g + 1)
                if not (isinstance(g, int) and g == 0):
                    pe.wait_ge(s_hrow, g)
                for t in range(GT):
                    for c in range(2):
                        i_ = mm(ps[0:P, 7, t * D:(t + 1) * D], xTg[:, s, c, t * P:(t + 1) * P], wG[:, c, :], start=(c == 0), stop=(c == 1))
                i_.then_inc(s_hm, 1)

            def ffn0(g, s=None):
                fixed = isinstance(g, int)
                s = g % 2 if s is None else s
                for m in range(8):
                    if not (fixed and g == 0 and m < 2):
                        pe.wait_ge(s_hBe, g * 8 + (m - 1))
                    for c in range(2):
                        i_ = mm(ps[:, 2 + m % 2, 0:N], wB1[:, c, m * 128:(m + 1) * 128], xnT[:, c, bass.ds(g * N, N)], start=(c == 0), stop=(c == 1))
                    i_.then_inc(s_hB, 1)
                if not (fixed and g < 2):
                    T2(g - 2, s)
                pe.wait_ge(s_hBe, g * 8 + 8)
                if not (fixed and g < 2):
                    pe.wait_ge(s_oBe, g - 1)
                for t in range(GT):
                    for m in range(8):
                        i_ = mm(ps[0:P, 4 + s, t * D:(t + 1) * D], hT[:, s, m, t * P:(t + 1) * P], wB2[:, m, :], start=(m == 0), stop=(m == 7))
                i_.then_inc(s_oB, 1)
                if not (fixed and g < 2):
                    H(g - 2, s)

            pe.wait_ge(s_wbc, 1)
            pe.wait_ge(s_wB, 96)
            pe.wait_ge(s_wBs, 1)
            in_turns(pe, steps, ffn0, G, 4, 3, 2)
            for g in (G - 2, G - 1):
                T2(g, g % 2)
                H(g, g % 2)

            def msg_sums(b, s, turns, first=False):
                pe.wait_ge(s_dsel, b + 1)
                pe.wait_ge(s_ga[s], turns * (16 * EB))
                if not first:
                    pe.wait_ge(s_mcp, b)
                for i in range(EB):
                    i_ = mm(ps[0:P, i // 2, (i % 2) * D:(i % 2 + 1) * D], S[:, s, i, :], mg[:, s, i, :], start=True, stop=True)
                i_.then_inc(s_mmm, 1)

            pe.wait_ge(s_hrow, G)
            msg_sums(0, 0, 1, first=True)
            msg_sums(1, 1, 1)
            with pe.Fori(1, B // 2) as i:
                msg_sums(i * 2, 0, i + 1)
                msg_sums(i * 2 + 1, 1, i + 1)

            def gate_mm(g, s=None):
                s = g % 2 if s is None else s
                pe.wait_ge(s_x3, g + 1)
                if not (isinstance(g, int) and g < 2):
                    pe.wait_ge(s_t3e, g - 1)
                for t in range(GT):
                    for c in range(2):
                        i_ = tr(ps[:, s, c * N + t * P:c * N + (t + 1) * P], xh[:, s, t, c * 128:(c + 1) * 128], ident[0:P, 0:P])
                i_.then_inc(s_t3, 1)
                pe.wait_ge(s_t3e, g + 1)
                if not (isinstance(g, int) and g < 2):
                    pe.wait_ge(s_l3e, g - 1)
                for t in range(GT):
                    for c in range(2):
                        i_ = mm(ps[0:P, 6 + s, t * E:(t + 1) * E], xTg[:, s, c, t * P:(t + 1) * P], gw[:, c, :], start=(c == 0), stop=(c == 1))
                i_.then_inc(s_l3, 1)

            pe.wait_ge(s_mcp, B)
            in_turns(pe, steps, gate_mm, G, 2, 3, 2)
            pe.wait_ge(s_goh, 1)
            mm(ps[0:P, 2, 0:T * E], before[:, :], gate[:, 5, :], start=True, stop=True)
            mm(ps[0:P, 3, 0:T * E], ones[:, :], gate[:, 5, :], start=True, stop=True).then_inc(s_grk, 1)

            def T5(q, s, es, j):
                if not (isinstance(q, int) and q < 2):
                    pe.wait_ge(s_t5e, q - 1)
                for t in range(GT):
                    for c in range(2):
                        i_ = tr(ps[:, s, c * N + t * P:c * N + (t + 1) * P], xe[:, es, GT * j + t, c * 128:(c + 1) * 128], ident[0:P, 0:P])
                i_.then_inc(s_t5, 1)

            def expert(e, es, turns, last=False):
                fixed = isinstance(e, int)
                pe.wait_ge(s_wE[es], turns * 64)
                for j in range(QE):
                    q, s = e * QE + j, j % 2
                    if j < QE - 1:
                        T5(q + 1, 1 - s, es, j + 1)
                    elif not last:
                        pe.wait_ge(s_xe[1 - es], (turns + es) * 16)
                        T5(q + 1, 1 - s, 1 - es, 0)
                    pe.wait_ge(s_t5e, q + 1)
                    for m in range(8):
                        if not (fixed and q == 0 and m < 2):
                            pe.wait_ge(s_h5e, q * 8 + (m - 1))
                        for c in range(2):
                            i_ = mm(ps[:, 2 + m % 2, 0:N], w1E[:, es, c, m * 128:(m + 1) * 128], xTg[:, s, c, :], start=(c == 0), stop=(c == 1))
                        i_.then_inc(s_h5, 1)
                    pe.wait_ge(s_h5e, q * 8 + 8)
                    if not (fixed and q < 2):
                        pe.wait_ge(s_o5e, q - 1)
                    for t in range(GT):
                        for m in range(8):
                            i_ = mm(ps[0:P, 4 + s, t * D:(t + 1) * D], hT[:, s, m, t * P:(t + 1) * P], w2E[:, es, m, :], start=(m == 0), stop=(m == 7))
                    i_.then_inc(s_o5, 1)

            pe.wait_ge(s_slots, 1)
            pe.wait_ge(s_xe[0], 16)
            T5(0, 0, 0, 0)
            expert(0, 0, 1)
            expert(1, 1, 1)
            with pe.Fori(1, E // 2 - 1) as i:
                expert(i * 2, 0, i + 1)
                expert(i * 2 + 1, 1, i + 1)
            expert(E - 2, 0, E // 2)
            expert(E - 1, 1, E // 2, last=True)


_INS = ["x", "src", "dst", "edge_attr_64", "L0_gnn_u", "L0_gnn_W1", "L0_gnn_b1", "L0_gnn_W2", "L0_gnn_b2", "L0_ffn_Wr",
        "L0_ffn_br", "L0_ffn_W1", "L0_ffn_b1", "L0_ffn_W2", "L0_ffn_b2", "L0_ffn_gamma", "L0_ffn_beta", "L1_gnn_W",
        "L1_ffn_gate_w", "L1_ffn_gate_b", "L1_ffn_w1", "L1_ffn_b1", "L1_ffn_w2", "L1_ffn_b2"]


def kernel(**inputs):
    import numpy as np
    import concourse.bacc as bacc
    from concourse import mybir as mb
    from concourse.bass_utils import run_bass_kernel_spmd as run

    nc = bacc.Bacc("TRN2", target_bir_lowering=False, num_devices=1)
    arrays, aps = {}, {}
    for name in _INS:
        v = np.ascontiguousarray(inputs[name])
        arrays[f"in_{name}"] = v
        aps[name] = nc.dram_tensor(f"in_{name}", v.shape, mb.dt.from_np(v.dtype), kind="ExternalInput").ap()
    out = nc.dram_tensor("out_0", (NODES, D), mb.dt.float32, kind="ExternalOutput").ap()
    build(nc, aps, out)
    return run(nc, [arrays], core_ids=[0]).results[0]["out_0"]
```

```python
import concourse.bass as bass
from concourse import mybir
from contextlib import ExitStack

NODES, EDGES, D, DE, DG = 6250, 100000, 256, 64, 128
P = 125
T, ET = NODES // P, EDGES // P
GT = 2
G, N = T // GT, GT * P
EB = 10
B = ET // EB
K = 5
HID0, HID1, HID2 = 512, 512, 1024
E, CAP = 8, 977
SLOTS = 1000
ST = SLOTS // P
DC = DE + 1
HB = B // 2
TURNS = ET + T - 1
MB = -(-TURNS // EB)
XW = D + 1
EPS = 1e-5
FMAX = 3.4028234663852886e38


class Steps:

    def __init__(self, sem=None):
        self.sem, self.base, self.k = sem, 0, 0

    def up(self):
        self.k += 1
        return 1

    def value(self):
        return self.base + self.k


def in_turns(eng, steps, body, total, head, tail, unit):
    for g in range(head):
        before = steps.value()
        body(g)
    per, start = steps.value() - before, steps.value()
    with eng.Fori(head // unit, (total - tail) // unit) as i:
        for s in range(unit):
            g = i * unit + s
            steps.base, steps.k = start + (g - head) * per, 0
            body(g, s)
            assert steps.k == per
    steps.base, steps.k = start + (total - tail - head) * per, 0
    for g in range(total - tail, total):
        body(g)


def build(nc, a, out):
    f32, bf16, i32, u32 = mybir.dt.float32, mybir.dt.bfloat16, mybir.dt.int32, mybir.dt.uint32
    ALU, ACT, AX = mybir.AluOpType, mybir.ActivationFunctionType, mybir.AxisListType.X
    ctx = ExitStack()
    with ctx:
        def sb(name, shape, dt=f32):
            return ctx.enter_context(nc.sbuf_tensor(name, shape, dt))

        def sem(name):
            return ctx.enter_context(nc.semaphore(name))

        def dram(name, rows, cols):
            return nc.dram_tensor(name, (rows, cols), f32, kind="Internal").ap()

        edge_sum = [dram(f"edge_sum{k}", NODES + P, DC) for k in range(K)]
        node_sum = [dram(f"node_sum{k}", NODES + P, D) for k in range(K)]
        h_rows = dram("h_rows", NODES, D)
        slot_x = dram("slot_x", E * SLOTS + NODES, XW)
        slot_y = dram("slot_y", E * SLOTS + P, D)

        x = sb("x", [P, T, D])
        big = sb("big", [128, T * XW])
        mid = sb("mid", [128, 10240])
        hT = sb("hT", [128, 2, 8, N])
        xg = sb("xg", [P, 2, GT, D + DE])
        xh = sb("xh", [P, 2, GT, D])
        xTg = sb("xTg", [128, 2, 2, N])
        aT = sb("aT", [DE, 2, N])
        yb = sb("yb", [P, 2, GT, D])
        wk = sb("wk", [P, 2, GT, D])
        src_f = sb("src_f", [P, ET])
        dst_f = sb("dst_f", [P, ET])
        idx_a = sb("idx_a", [P, 2, EB], u32)
        idx_b = sb("idx_b", [P, 2, EB], u32)
        ident = sb("ident", [128, 128])
        before = sb("before", [P, P])
        ones = sb("ones", [P, P])
        lo_iota = sb("lo_iota", [P, P])
        hi_iota = sb("hi_iota", [P, T])
        e_iota = sb("e_iota", [P, E])
        n_iota = sb("n_iota", [P, T])
        spare = sb("spare", [P, 1])
        not_first = sb("not_first", [P, P])
        dup = sb("dup", [P, 2, EB])
        firsts = sb("firsts", [P, 2, EB])
        src_at = sb("src_at", [P, MB * EB])
        not_dst = sb("not_dst", [P, MB * EB])
        words = sb("words", [1, MB], i32)
        walk = sb("walk", [T, 6])
        walk_i = sb("walk_i", [T, 1], i32)
        wsum = sb("wsum", [1, MB])
        met = sb("met", [P, 1])
        pow2 = sb("pow2", [1, EB - 1])
        tile_no = sb("tile_no", [P, 8])
        in_order = sb("in_order", [1, 1], i32)
        away = sb("away", [P, 2, EB])
        iota_i = sb("iota_i", [P, P], i32)
        neg_half = sb("neg_half", [P, T])
        stat = sb("stat", [P, 2, GT, 6])
        mv = sb("mv", [P, 2, GT, 2])
        var = sb("var", [P, 2, GT])
        rstd = sb("rstd", [P, 2, GT])
        stat2 = sb("stat2", [P, 2, GT, 6])
        mv2 = sb("mv2", [P, 2, GT, 2])
        var2 = sb("var2", [P, 2, GT])
        rstd2 = sb("rstd2", [P, 2, GT])
        mv1 = sb("mv1", [P, T, 2])
        rstd1 = sb("rstd1", [P, T])
        cnt = sb("cnt", [P, T])
        deg = sb("deg", [P, T])
        has = sb("has", [P, T])
        dis = sb("dis", [P, T])
        biasA = sb("biasA", [128, 4])
        b1A = sb("b1A", [128, 4])
        u0 = sb("u0", [DG, 1])
        b2A = sb("b2A", [P, D])
        msum = sb("msum", [128, 2, G])
        mean = sb("mean", [128, 2])
        wr = sb("wr", [128, 2, E])
        rt = sb("rt", [1, 16, E])
        rt_id = sb("rt_id", [1, E], u32)
        wcol = sb("wcol", [128, 2])
        bB1 = sb("bB1", [128, 8])
        b2B = b2A
        gamma = sb("gamma", [P, D])
        beta = sb("beta", [P, D])
        wG = sb("wG", [128, 2, D])
        gw = sb("gw", [128, 2, E])
        gb = sb("gb", [P, E])
        b1E = sb("b1E", [128, 2, 8])
        b2E = sb("b2E", [P, 2, D])
        ps = ctx.enter_context(nc.psum_tensor("ps", [128, 8, 512], f32))

        def cut(area, rows, at, size):
            return area[0:rows, at:at + size], at + size

        rowb, o = cut(big, P, 0, 2 * EB * P)
        S, o = cut(big, P, o, 2 * EB * P)
        SL, o = cut(big, P, o, EB * P)
        va, o = cut(big, P, o, 2 * EB * DC)
        ma, o = cut(big, P, o, 2 * EB * DC)
        oh, o = cut(big, P, o, 2 * EB * (P + T))
        SL = SL.rearrange("p (t q) -> p t q", t=EB)
        rowb = rowb.bitcast(i32).rearrange("p (s t q) -> p s t q", s=2, t=EB)
        S = S.rearrange("p (s t q) -> p s t q", s=2, t=EB)
        va = va.rearrange("p (s t d) -> p s t d", s=2, t=EB)
        ma = ma.rearrange("p (s t d) -> p s t d", s=2, t=EB)
        oh = oh.bitcast(bf16)
        ohl = oh[:, 0:4 * EB * P].rearrange("p (s t q) -> p s t q", s=2, t=2 * EB)
        ohh = oh[:, 4 * EB * P:4 * EB * (P + T)].rearrange("p (s t q) -> p s t q", s=2, t=2 * EB)
        hi, lo = mid[0:P, 0:ET], mid[0:P, ET:2 * ET]
        hl_i = mid[0:P, 2 * ET:3 * ET].bitcast(i32)
        hl_w = mid[0:P, 3 * ET:4 * ET]
        raw_i = mid[0:100, 4 * ET:4 * ET + 2000].bitcast(i32).rearrange("t (k c p) -> t k c p", k=2, c=8)
        raw_f = hT[0:100, 1, :, :].rearrange("t c n -> t (c n)").rearrange("t (k c p) -> t k c p", k=2, c=8)
        w_at = mid[0:P, 1600:1600 + MB * EB]
        t_at = mid[0:P, 2450:2450 + MB * EB]
        step_i = mid[0:P, 3300:3300 + MB * EB]
        step_ii = hits_i = mid[0:P, 8400:8400 + MB * EB].bitcast(i32)
        sel = mid[0:100, 4150:4150 + 4 * MB * EB].rearrange("t (k q) -> t k q", k=4)
        past = mid[0:T - 1, 7550:7550 + MB * EB]
        hits = [mid[0:P, 8400 + k * MB * EB:8400 + (k + 1) * MB * EB] for k in range(2)]
        agg = mid[0:P, 0:T * DC]
        agg3 = agg.rearrange("p (t d) -> p t d", t=T)
        part = mid[0:P, T * DC:2 * T * DC]
        wA1 = mid[:, 6500:6500 + 3 * HID0].rearrange("p (c f) -> p c f", c=3)
        wA2 = mid[:, 8036:8036 + 4 * D].rearrange("p (c d) -> p c d", c=4)
        wU = mid[:, 9060:9060 + HID0]
        xnT = big[:, 0:2 * NODES].rearrange("p (c n) -> p c n", c=2)
        wB1 = mid[:, 0:2 * 2 * HID1].rearrange("p (c f) -> p c f", c=2)
        wB2 = mid[:, 2048:2048 + 8 * D].rearrange("p (c d) -> p c d", c=8)
        wrow = wk[0:1, 0].rearrange("a t d -> a (t d)")[:, 0:2 * P].rearrange("a (k p) -> a k p", k=2)
        b2rows = wk[0:1, 1]
        hb = xg[:, :, :, 0:D]
        mg = mid[0:P, 0:2 * EB * D].rearrange("p (s t d) -> p s t d", s=2, t=EB)
        ms = mid[0:P, 2 * EB * D:4 * EB * D].rearrange("p (s t d) -> p s t d", s=2, t=EB)
        acc = big[0:P, T:T + T * D].rearrange("p (t d) -> p t d", t=T)
        onto = mid[0:P, 5120:5120 + 2 * EB * P].rearrange("p (s t q) -> p s t q", s=2, t=EB)
        off = mid[0:P, 7620:7620 + EB * P].rearrange("p (t q) -> p t q", t=EB)
        tab = mid[0:P, 0:2 * K * GT * D].rearrange("p (s k t d) -> p s k t d", s=2, k=K, t=GT)
        xn3 = big[0:P, 0:T * XW].rearrange("p (t d) -> p t d", t=T)
        gate = mid[0:P, 5120:5120 + 12 * T * E].rearrange("p (k q) -> p k q", k=12)
        gate3 = gate.rearrange("p k (t e) -> p k t e", t=T)
        g50 = xg[:, :, :, :].rearrange("p s t d -> p (s t d)")[:, 0:16 * T].rearrange("p (k t) -> p k t", k=16)
        sc_idx = sb("sc_idx", [P, T], u32)
        ga_idx = sb("ga_idx", [P, T], u32)
        xe = big[0:P, 0:2 * ST * XW].rearrange("p (s t d) -> p s t d", s=2, t=ST)
        w1E = mid[:, 0:2 * 2 * HID2].rearrange("p (s c f) -> p s c f", s=2, c=2)
        w2E = mid[:, 4096:4096 + 2 * 8 * D].rearrange("p (s c d) -> p s c d", s=2, c=8)
        nanw = mid[0:P, 8192:8192 + 4 * GT * D].rearrange("p (k t d) -> p k t d", k=4, t=GT)
        yg = big[0:P, 0:T * D].rearrange("p (t d) -> p t d", t=T)

        x_in = a["x"].rearrange("(t p) d -> p t d", p=P)
        out_v = out.rearrange("(t p) d -> p t d", p=P)
        attr = a["edge_attr_64"].rearrange("(t p) d -> p t d", p=P)
        h_v = h_rows.rearrange("(t p) d -> p t d", p=P)
        ns_v = [t[0:NODES, :].rearrange("(t p) d -> p t d", p=P) for t in node_sum]
        es_v = [t[0:NODES, :].rearrange("(t p) d -> p t d", p=P) for t in edge_sum]
        sx_v = slot_x[0:E * SLOTS, :].rearrange("(e p t) d -> e p t d", e=E, t=ST)
        sy_v = slot_y[0:E * SLOTS, :].rearrange("(e p t) d -> e p t d", e=E, t=ST)

        s_dve, s_pool, s_act = sem("dve_steps"), sem("pool_steps"), sem("act_steps")
        s_raw, s_x, s_wA, s_cst, s_wB, s_b2r = sem("raw_ends_in"), sem("x_in"), sem("wA_in"), sem("small_in"), sem("wB_in"), sem("b2rows_in")
        s_zero, s_zeroed, s_ztab = sem("zeros_set"), sem("scratch_zeroed"), sem("tables_zeroed")
        s_iota, s_const = sem("iotas_set"), sem("constants_set")
        s_rawf, s_rawT, s_ends = sem("ends_as_float"), sem("ends_transposed"), sem("ends_in_columns")
        s_row, s_va = [sem(f"edge_rows_in{i}") for i in range(2)], [sem(f"edge_attr_in{i}") for i in range(2)]
        s_esel, s_emm, s_ecp = sem("edge_select_set"), sem("edge_sums_in_psum"), sem("edge_sums_in_sbuf")
        s_tab = [sem(f"edge_scattered{k}") for k in range(K)]
        s_deg, s_dis = sem("degrees_set"), sem("dis_set")
        s_part, s_added, s_agg = sem("edge_table_in"), sem("edge_table_added"), sem("edge_means_set")
        s_bA, s_bAset = sem("u_term_in_psum"), sem("biasA_set")
        s_v0, s_r0, s_x0 = sem("ln0_var"), sem("ln0_rstd"), sem("ln0_rows")
        s_t0, s_t0e, s_h0, s_h0e = sem("ln0_T_in_psum"), sem("ln0_T_in_sbuf"), sem("mlp_hidden_in_psum"), sem("mlp_hidden_in_sbuf")
        s_o0, s_o0e = sem("mlp_out_in_psum"), sem("mlp_out_read")
        s_v1, s_r1, s_x1, s_t1, s_t1e = sem("ln1_var"), sem("ln1_rstd"), sem("ln1_rows"), sem("ln1_T_in_psum"), sem("ln1_T_in_sbuf")
        s_mean, s_lg, s_e1, s_e1x, s_e2x, s_rid = sem("mean_set"), sem("logits_in_psum"), sem("router_args"), sem("router_exp"), sem("router_rows"), sem("router_ids")
        s_wb, s_wbc, s_wBs = sem("router_w_in_psum"), sem("router_w_set"), sem("wB2_scaled")
        s_hB, s_hBe, s_oB, s_oBe = sem("ffn0_hidden_in_psum"), sem("ffn0_hidden_in_sbuf"), sem("ffn0_out_in_psum"), sem("ffn0_out_read")
        s_vB, s_rB = sem("lnB_var"), sem("lnB_rstd")
        s_v2, s_r2, s_x2, s_t2, s_t2e = sem("ln2_var"), sem("ln2_rstd"), sem("ln2_rows"), sem("ln2_T_in_psum"), sem("ln2_T_in_sbuf")
        s_hm, s_hrow, s_hw = sem("h_in_psum"), sem("h_in_sbuf"), [sem(f"h_written{i}") for i in range(2)]
        s_dsel, s_ga, s_mmm, s_mcp = sem("msg_select_set"), [sem(f"msg_gathered{i}") for i in range(2)], sem("msg_sums_in_psum"), sem("msg_sums_in_sbuf")
        s_flag, s_sch, s_schp, s_sched, s_wrd = sem("flag_set"), sem("schedule_args"), sem("schedule_products"), sem("schedule_set"), sem("dst_counts_read")
        s_onto, s_offs, s_gk, s_pair, s_acc, s_accz = sem("window_select_set"), sem("window_offsets_set"), [sem(f"step_gathered{i}") for i in range(2)], sem("step_sums_in_psum"), sem("step_sums_added"), sem("window_sums_zeroed")
        s_idx = sem("step_indices_set")
        s_dvf, s_fz, s_fzd, s_fs = sem("dve_steps_unsorted"), sem("unsorted_zeros_set"), sem("node_tables_zeroed"), sem("node_tables_summed")
        s_drow = [sem(f"dst_rows_in{i}") for i in range(2)]
        s_mt = [sem(f"msg_scattered{k}") for k in range(K)]
        s_nt = [sem(f"node_tables_in{i}") for i in range(2)]
        s_nadd = sem("node_tables_added")
        s_v3, s_r3, s_x3, s_x3c, s_t3, s_t3e, s_l3, s_l3e = sem("ln3_var"), sem("ln3_rstd"), sem("ln3_rows"), sem("ln3_rows_kept"), sem("ln3_T_in_psum"), sem("ln3_T_in_sbuf"), sem("gate_in_psum"), sem("gate_in_sbuf")
        s_ga1, s_gexp, s_goh, s_grk, s_slots = sem("gate_args"), sem("gate_exp"), sem("gate_onehot"), sem("gate_ranks"), sem("slots_set")
        s_disp = sem("rows_dispatched")
        s_xe, s_wE = [sem(f"slot_rows_in{i}") for i in range(2)], [sem(f"wE_in{i}") for i in range(2)]
        s_t5, s_t5e, s_h5, s_h5e, s_o5, s_o5e = sem("slots_T_in_psum"), sem("slots_T_in_sbuf"), sem("ffn1_hidden_in_psum"), sem("ffn1_hidden_in_sbuf"), sem("ffn1_out_in_psum"), sem("ffn1_out_read")
        s_y5, s_yw = sem("slot_y_set"), [sem(f"slot_y_written{i}") for i in range(2)]
        s_yg = [sem(f"rows_returned{i}") for i in range(T // EB)]
        s_fin, s_out = sem("out_set"), sem("out_written")

        QN = E * ST // GT
        QE = ST // GT
        block = ctx.enter_context(nc.Block())

        @block.sync
        def _(sp):
            steps = Steps()
            sp.dma_start(raw_i[:, 0], a["src"].rearrange("(c t p) -> t c p", c=8, p=P)).then_inc(s_raw, 16)
            sp.dma_start(raw_i[:, 1], a["dst"].rearrange("(c t p) -> t c p", c=8, p=P)).then_inc(s_raw, 16)

            def load_block(b, s=None):
                s = b % 2 if s is None else s
                if not (isinstance(b, int) and b < 2):
                    sp.wait_ge(s_emm, b - 1)
                sp.dma_start(rowb[:, s], a["src"][bass.ds(b * (EB * P), EB * P)].partition_broadcast(P)
                             .rearrange("p (t q) -> p t q", t=EB)).then_inc(s_row[s], 16)
                sp.dma_start(va[:, s, :, 0:DE], attr[:, bass.ds(b * EB, EB), :]).then_inc(s_va[s], 16)

            in_turns(sp, steps, load_block, B, 2, 2, 2)
            sp.wait_ge(s_sched, 1)
            w1 = a["L0_gnn_W1"]
            sp.dma_start(wA1[:, 0:2, :], w1[0:D, :].rearrange("(c p) f -> p c f", p=128)).then_inc(s_wA, 16)
            sp.dma_start(wA1[0:DE, 2, :], w1[D:D + DE, :]).then_inc(s_wA, 16)
            sp.dma_start(wU, w1[D + DE:D + DE + DG, :]).then_inc(s_wA, 16)
            sp.dma_start(wA2, a["L0_gnn_W2"].rearrange("(c p) d -> p c d", p=128)).then_inc(s_wA, 16)
            for k in range(K):
                sp.wait_ge(s_tab[k], 16 * EB // K * B)
                if k >= 2:
                    sp.wait_ge(s_added, k - 1)
                sp.dma_start((part if k else agg).rearrange("p (t d) -> p t d", t=T), es_v[k]).then_inc(s_part, 16)
                if k:
                    sp.wait_ge(s_added, k)
            sp.wait_ge(s_rid, 1)
            for k in range(2):
                e = sp.value_load(rt_id[0:1, k:k + 1], min_val=0, max_val=E - 1)
                sp.dma_start(wB1[:, :, k * HID1:(k + 1) * HID1],
                             a["L0_ffn_W1"][bass.ds(e, 1)].rearrange("a (c p) f -> p (a c) f", p=128)).then_inc(s_wB, 16)
                sp.dma_start(wB2[:, 4 * k:4 * k + 4, :],
                             a["L0_ffn_W2"][bass.ds(e, 1)].rearrange("a (c p) d -> p (a c) d", p=128)).then_inc(s_wB, 16)
                with nc.allow_non_contiguous_dma(reason="a bias as a column"):
                    sp.dma_start(bB1[:, 4 * k:4 * k + 4],
                                 a["L0_ffn_b1"][bass.ds(e, 1)].rearrange("a (c p) -> p (a c)", p=128)).then_inc(s_wB, 16)
                sp.dma_start(b2rows[:, k, :], a["L0_ffn_b2"][bass.ds(e, 1)]).then_inc(s_b2r, 16)

            def store_h(g, s=None):
                s = g % 2 if s is None else s
                sp.wait_ge(s_hrow, g + 1)
                sp.dma_start(h_v[:, bass.ds(g * GT, GT), :], hb[:, s]).then_inc(s_hw[s], 16)

            in_turns(sp, steps, store_h, G, 2, 3, 2)

            def load_dst(b, s=None):
                s = b % 2 if s is None else s
                if isinstance(b, int) and b < 2:
                    sp.wait_ge(s_t2, G)
                else:
                    sp.wait_ge(s_dsel, b - 1)
                sp.dma_start(rowb[:, s], a["dst"][bass.ds(b * (EB * P), EB * P)].partition_broadcast(P)
                             .rearrange("p (t q) -> p t q", t=EB)).then_inc(s_drow[s], 16)

            def load_tables(g, s=None):
                s = g % 2 if s is None else s
                if not (isinstance(g, int) and g < 2):
                    sp.wait_ge(s_fs, g - 1)
                for k in range(K):
                    sp.dma_start(tab[:, s, k], ns_v[k][:, bass.ds(g * GT, GT), :]).then_inc(s_nt[s], 16)

            with sp.If_eq(sp.to_reg(sp.value_load(in_order[0:1, 0:1], min_val=0, max_val=1)), 0):
                in_turns(sp, steps, load_dst, B, 2, 2, 2)
                for k in range(K):
                    sp.wait_ge(s_mt[k], 16 * EB // K * B)
                in_turns(sp, steps, load_tables, G, 2, 3, 2)

            def load_expert(e, s=None):
                s = e % 2 if s is None else s
                if isinstance(e, int) and e < 2:
                    if e == 0:
                        sp.wait_ge(s_slots, 1)
                else:
                    sp.wait_ge(s_o5e, (e - 1) * QE)
                sp.dma_start(w1E[:, s], a["L1_ffn_w1"][bass.ds(e, 1)].rearrange("a (c p) f -> p (a c) f", p=128)).then_inc(s_wE[s], 16)
                sp.dma_start(w2E[:, s], a["L1_ffn_w2"][bass.ds(e, 1)].rearrange("a (c p) d -> p (a c) d", p=128)).then_inc(s_wE[s], 16)
                with nc.allow_non_contiguous_dma(reason="a bias as a column"):
                    sp.dma_start(b1E[:, s], a["L1_ffn_b1"][bass.ds(e, 1)].rearrange("a (c p) -> p (a c)", p=128)).then_inc(s_wE[s], 16)
                sp.dma_start(b2E[:, s], a["L1_ffn_b2"][bass.ds(e, 1)].rearrange("a d -> (a d)").partition_broadcast(P)).then_inc(s_wE[s], 16)
                if isinstance(e, int) and e == 0:
                    sp.wait_ge(s_disp, 16 * T)
                sp.dma_start(xe[:, s], sx_v[bass.ds(e, 1)].rearrange("a p t d -> p (a t) d")).then_inc(s_xe[s], 16)

            load_expert(0)
            load_expert(1)

            def expert_io(e, s=None):
                s0 = e % 2 if s is None else s
                for j in range(QE):
                    sp.wait_ge(s_y5, e * QE + (j + 1))
                    sp.dma_start(sy_v[bass.ds(e, 1), :, GT * j:GT * (j + 1), :].rearrange("a p t d -> p (a t) d"),
                                 yb[:, j % 2]).then_inc(s_yw[j % 2], 16)
                if not (isinstance(e, int) and e >= E - 2):
                    load_expert(e + 2, s0)

            in_turns(sp, steps, expert_io, E, 2, 2, 2)
            for c in range(T // EB):
                sp.wait_ge(s_fin, c + 1)
                sp.dma_start(out_v[:, c * EB:(c + 1) * EB, :], x[:, c * EB:(c + 1) * EB, :]).then_inc(s_out, 16)
            sp.wait_ge(s_out, 16 * (T // EB))
            sp.wait_ge(s_zeroed, 16 * 17)

        @block.scalar
        def _(act):
            steps = Steps()
            act.wait_ge(s_zero, 1)
            z = hT[0:P, 0, :, :].rearrange("p m n -> p (m n)")
            for k in range(K):
                for c in range(3):
                    act.dma_start(edge_sum[k].rearrange("(p t) d -> p (t d)", p=P)[:, c * 1105:(c + 1) * 1105], z[:, 0:1105]).then_inc(s_ztab, 16)
            act.dma_start(x[:, :, :], x_in).then_inc(s_x, 16)
            def row(name):
                return a[name].partition_broadcast(P)
            with nc.allow_non_contiguous_dma(reason="biases and u[0] as columns"):
                act.dma_start(b1A[:, :], a["L0_gnn_b1"].rearrange("(c p) -> p c", p=128)).then_inc(s_cst, 16)
                act.dma_start(u0[:, :], a["L0_gnn_u"][0:1, :].rearrange("a p -> p a")).then_inc(s_cst, 16)
            act.dma_start(b2A[:, :], row("L0_gnn_b2")).then_inc(s_cst, 16)
            act.dma_start(wr[:, :, :], a["L0_ffn_Wr"].rearrange("(c p) e -> p c e", p=128)).then_inc(s_cst, 16)
            act.dma_start(rt[:, 0, :], a["L0_ffn_br"].rearrange("(a e) -> a e", a=1)).then_inc(s_cst, 16)
            act.dma_start(gamma[:, :], row("L0_ffn_gamma")).then_inc(s_cst, 16)
            act.dma_start(beta[:, :], row("L0_ffn_beta")).then_inc(s_cst, 16)
            act.dma_start(wG[:, :, :], a["L1_gnn_W"].rearrange("(c p) e -> p c e", p=128)).then_inc(s_cst, 16)
            act.dma_start(gw[:, :, :], a["L1_ffn_gate_w"].rearrange("(c p) e -> p c e", p=128)).then_inc(s_cst, 16)
            act.dma_start(gb[:, :], row("L1_ffn_gate_b")).then_inc(s_cst, 16)
            sx_z = slot_x[0:E * SLOTS, :].rearrange("(p c r) d -> p c (r d)", p=P, c=16)
            for c in range(16):
                act.dma_start(sx_z[:, c, :], z[:, 0:4 * XW]).then_inc(s_zeroed, 16)
            act.dma_start(slot_y[E * SLOTS:E * SLOTS + P, :], z[:, 0:D]).then_inc(s_zeroed, 16)

            def edge_copy(b, s=None):
                s = b % 2 if s is None else s
                act.wait_ge(s_emm, b + 1)
                if not (isinstance(b, int) and b < 2):
                    for k in range(K):
                        act.wait_ge(s_tab[k], 16 * EB // K * (b - 1))
                act.activation(ma[:, s].rearrange("p (h t) d -> p h (t d)", h=2),
                               ps[0:P, 2 + 2 * s:4 + 2 * s, 0:EB // 2 * DC], ACT.Copy)
                act.activation(idx_a[:, s, :], firsts[:, s], ACT.Copy).then_inc(s_ecp, 1)

            in_turns(act, steps, edge_copy, B, 2, 2, 2)

            act.wait_ge(s_bA, 1)
            act.wait_ge(s_cst, 160)
            for m in range(4):
                i_ = act.activation(biasA[:, m:m + 1], ps[:, 7, m:m + 1], ACT.Identity, bias=b1A[:, m:m + 1])
            i_.then_inc(s_bAset, 1)
            act.wait_ge(s_bAset, 1)
            act.wait_ge(s_zeroed, 16 * 17)

            def T0_copy(g, s):
                act.wait_ge(s_t0, g + 1)
                act.activation(xTg[:, s], ps[:, s, 0:2 * N].rearrange("p (c n) -> p c n", c=2), ACT.Copy)
                act.activation(aT[:, s], ps[0:DE, 6, s * N:(s + 1) * N], ACT.Copy).then_inc(s_t0e, 1)

            def T1_copy(g, s):
                act.wait_ge(s_t1, g + 1)
                for c in range(2):
                    i_ = act.activation(xnT[:, c, bass.ds(g * N, N)], ps[:, 7, c * N:(c + 1) * N], ACT.Copy,
                                        accum_out=msum[:, c, bass.ds(g, 1)])
                i_.then_inc(s_t1e, 1)

            def mlp(g, s=None):
                fixed = isinstance(g, int)
                s = g % 2 if s is None else s
                if not (fixed and g == G - 1):
                    T0_copy(g + 1, 1 - s)
                if not (fixed and g < 2):
                    act.wait_ge(s_o0, g - 1)
                for m in range(4):
                    act.wait_ge(s_h0, g * 4 + (m + 1))
                    act.activation(hT[:, s, m, :], ps[:, 2 + m % 2, 0:N], ACT.Relu, bias=biasA[:, m:m + 1]).then_inc(s_h0e, 1)
                if not (fixed and g == 0):
                    T1_copy(g - 1, 1 - s)

            T0_copy(0, 0)
            in_turns(act, steps, mlp, G, 2, 3, 2)
            T1_copy(G - 1, (G - 1) % 2)

            act.wait_ge(s_e1, 1)
            act.activation(rt[:, 2, :], rt[:, 1, :], ACT.Exp, accum_out=rt[:, 9, 0:1]).then_inc(s_e1x, 1)
            act.wait_ge(s_e1, 2)
            act.activation(rt[:, 5, :], rt[:, 4, :], ACT.Exp, accum_out=rt[:, 9, 2:3]).then_inc(s_e1x, 1)
            act.wait_ge(s_e1, 3)
            act.activation(rt[:, 11, 0:2], rt[:, 10, 0:2], ACT.Exp, accum_out=rt[:, 9, 4:5]).then_inc(s_e1x, 1)

            act.wait_ge(s_wbc, 1)
            act.wait_ge(s_wB, 96)
            for k in range(2):
                i_ = act.activation(wB2[:, 4 * k:4 * k + 4, :], wB2[:, 4 * k:4 * k + 4, :], ACT.Copy, scale=wcol[:, k:k + 1])
            i_.then_inc(s_wBs, 1)

            def h_copy(g, s, turns):
                act.wait_ge(s_t2, g + 1)
                act.activation(xTg[:, s], ps[:, s, 0:2 * N].rearrange("p (c n) -> p c n", c=2), ACT.Copy).then_inc(s_t2e, 1)
                act.wait_ge(s_hm, g + 1)
                if not (isinstance(turns, int) and turns == 0):
                    act.wait_ge(s_hw[s], turns * 16)
                for t in range(GT):
                    i_ = act.activation(hb[:, s, t, :], ps[0:P, 7, t * D:(t + 1) * D], ACT.Copy, scale=dis[:, bass.ds(g * GT + t, 1)])
                i_.then_inc(s_hrow, 1)

            def ffn0(g, s, turns):
                fixed = isinstance(g, int)
                if not (fixed and g < 2):
                    act.wait_ge(s_oB, g - 1)
                for m in range(8):
                    act.wait_ge(s_hB, g * 8 + (m + 1))
                    act.activation(hT[:, s, m, :], ps[:, 2 + m % 2, 0:N], ACT.Gelu, bias=bB1[:, m:m + 1]).then_inc(s_hBe, 1)
                if not (fixed and g < 2):
                    h_copy(g - 2, s, turns - 1)

            for g in range(4):
                ffn0(g, g % 2, g // 2)
            with act.Fori(2, G // 2) as i:
                for s in range(2):
                    ffn0(i * 2 + s, s, i)
            ffn0(G - 1, 0, G // 2)
            h_copy(G - 2, 1, (G - 2) // 2)
            h_copy(G - 1, 0, (G - 1) // 2)

            def step_select(b, s=None):
                s = b % 2 if s is None else s
                if not (isinstance(b, int) and b < 2):
                    act.wait_ge(s_pair, (b - 1) * (EB // 2))
                act.activation(idx_a[:, s, :], src_at[:, bass.ds(b * EB, EB)], ACT.Copy).then_inc(s_idx, 1)
                if not (isinstance(b, int) and b == 0):
                    act.wait_ge(s_onto, b)
                for i in range(EB):
                    i_ = act.activation(off[:, i, :], lo_iota[:, :], ACT.Abs, bias=not_dst[:, bass.ds(b * EB + i, 1)])
                i_.then_inc(s_offs, 1)
                act.wait_ge(s_offs, b + 1)
                act.activation(onto[:, s], off, ACT.Relu, bias=1.0, scale=-1.0).then_inc(s_onto, 1)

            def msg_copy(b, s=None):
                s = b % 2 if s is None else s
                act.wait_ge(s_mmm, b + 1)
                if not (isinstance(b, int) and b < 2):
                    for k in range(K):
                        act.wait_ge(s_mt[k], 16 * EB // K * (b - 1))
                act.activation(ms[:, s].rearrange("p (h t) d -> p h (t d)", h=5), ps[0:P, 0:5, :], ACT.Copy).then_inc(s_mcp, 1)

            act.wait_ge(s_sched, 1)
            with act.If_eq(act.to_reg(act.value_load(in_order[0:1, 0:1], min_val=0, max_val=1)), 1):
                in_turns(act, steps, step_select, MB, 2, 3, 2)
            with act.Else():
                act.wait_ge(s_fz, 1)
                for k in range(K):
                    for c in range(8):
                        act.dma_start(node_sum[k].rearrange("(p t) d -> p (t d)", p=P)[:, c * 1632:(c + 1) * 1632], z[:, 0:1632]).then_inc(s_fzd, 16)
                in_turns(act, steps, msg_copy, B, 2, 2, 2)
                act.wait_ge(s_fzd, 16 * 8 * K)

            def gate_copy(g, s=None):
                s = g % 2 if s is None else s
                act.wait_ge(s_x3, g + 1)
                act.activation(xn3[:, bass.ds(g * GT, GT), 0:D], xh[:, s], ACT.Copy).then_inc(s_x3c, 1)
                act.wait_ge(s_t3, g + 1)
                act.activation(xTg[:, s], ps[:, s, 0:2 * N].rearrange("p (c n) -> p c n", c=2), ACT.Copy).then_inc(s_t3e, 1)

            in_turns(act, steps, gate_copy, G, 2, 3, 2)
            act.wait_ge(s_ga1, 1)
            act.activation(gate[:, 1, :], gate[:, 1, :], ACT.Exp).then_inc(s_gexp, 1)

            def T5_copy(q, s):
                act.wait_ge(s_t5, q + 1)
                act.activation(xTg[:, s], ps[:, s, 0:2 * N].rearrange("p (c n) -> p c n", c=2), ACT.Copy).then_inc(s_t5e, 1)

            def expert(e, es=None):
                fixed = isinstance(e, int)
                es = e % 2 if es is None else es
                act.wait_ge(s_wE[es], (e // 2 + 1) * 64 if fixed else wE_turn[0] * 64)
                for j in range(QE):
                    q, s = e * QE + j, j % 2
                    if not (fixed and e == E - 1 and j == QE - 1):
                        T5_copy(q + 1, 1 - s)
                    if not (fixed and q < 2):
                        act.wait_ge(s_o5, q - 1)
                    for m in range(8):
                        act.wait_ge(s_h5, q * 8 + (m + 1))
                        act.activation(hT[:, s, m, :], ps[:, 2 + m % 2, 0:N], ACT.Relu, bias=b1E[:, es, m:m + 1]).then_inc(s_h5e, 1)

            T5_copy(0, 0)
            wE_turn = [None]
            expert(0)
            expert(1)
            with act.Fori(1, E // 2 - 1) as i:
                wE_turn[0] = i + 1
                expert(i * 2, 0)
                expert(i * 2 + 1, 1)
            expert(E - 2)
            expert(E - 1)

        @block.gpsimd
        def _(pool):
            steps = Steps()
            nc.gpsimd.memset(ident[:, :], 0.0).then_inc(s_pool, steps.up())
            nc.gpsimd.memset(not_first[:, :], 0.0).then_inc(s_pool, steps.up())
            nc.gpsimd.memset(before[:, :], 0.0).then_inc(s_pool, steps.up())
            nc.gpsimd.memset(ones[:, :], 1.0).then_inc(s_pool, steps.up())
            nc.gpsimd.memset(neg_half[:, :], -0.5).then_inc(s_pool, steps.up())
            nc.gpsimd.iota(iota_i[:, :], [[1, P]], base=0, channel_multiplier=0).then_inc(s_pool, steps.up())
            pool.wait_ge(s_pool, steps.value())
            nc.gpsimd.affine_select(out=ident[:, :], in_=ident[:, :], compare_op=ALU.not_equal, fill=1.0, base=0,
                                    pattern=[[-1, 128]], channel_multiplier=1).then_inc(s_pool, steps.up())
            nc.gpsimd.affine_select(out=before[:, :], in_=before[:, :], compare_op=ALU.is_ge, fill=1.0, base=0,
                                    pattern=[[-1, P]], channel_multiplier=1).then_inc(s_pool, steps.up())
            nc.gpsimd.affine_select(out=not_first[:, :], in_=not_first[:, :], compare_op=ALU.is_ge, fill=1.0, base=0,
                                    pattern=[[1, P]], channel_multiplier=-1).then_inc(s_pool, steps.up())
            nc.gpsimd.tensor_copy(lo_iota[:, :], iota_i[:, :]).then_inc(s_pool, steps.up())
            nc.gpsimd.tensor_copy(hi_iota[:, :], iota_i[:, 0:T]).then_inc(s_pool, steps.up())
            nc.gpsimd.tensor_copy(e_iota[:, :], iota_i[:, 0:E]).then_inc(s_pool, steps.up())
            pool.wait_ge(s_pool, steps.value())
            nc.gpsimd.iota(iota_i[:, 0:T], [[P, T]], base=0, channel_multiplier=1).then_inc(s_pool, steps.up())
            pool.wait_ge(s_pool, steps.value())
            nc.gpsimd.tensor_copy(n_iota[:, :], iota_i[:, 0:T]).then_inc(s_pool, steps.up())
            nc.gpsimd.tensor_scalar(spare[:, :], iota_i[:, 0:1], float(NODES), None, ALU.add).then_inc(s_pool, steps.up())
            pool.wait_ge(s_pool, steps.value())
            nc.gpsimd.iota(step_ii, [[1, MB * EB]], base=0, channel_multiplier=0).then_inc(s_pool, steps.up())
            nc.gpsimd.iota(iota_i[:, 0:8], [[100, 8]], base=0, channel_multiplier=1).then_inc(s_pool, steps.up())
            for k in range(EB - 1):
                nc.gpsimd.memset(pow2[:, k:k + 1], float(1 << k)).then_inc(s_pool, steps.up())
            for k in range(2):
                nc.gpsimd.memset(va[:, k, :, DE:DC], 1.0).then_inc(s_pool, steps.up())
            pool.wait_ge(s_pool, steps.value())
            nc.gpsimd.tensor_copy(tile_no[:, :], iota_i[:, 0:8]).then_inc(s_pool, steps.up())
            pool.wait_ge(s_pool, steps.value())
            nc.gpsimd.memset(iota_i[:, :], 0).then_inc(s_const, 1)

            pool.wait_ge(s_ztab, 16 * 3 * K)

            def edge_scatter(b, s=None):
                s = b % 2 if s is None else s
                pool.wait_ge(s_ecp, b + 1)
                for i in range(EB):
                    k = i % K
                    if not (isinstance(b, int) and b == 0 and i < K):
                        pool.wait_ge(s_tab[k], b * (16 * EB // K) + 16 * (i // K))
                    pool.nop(nofuse=True)
                    nc.gpsimd.indirect_dma_start(edge_sum[k], bass.IndirectOffsetOnAxis(idx_a[:, s, i:i + 1], 0),
                                                 ma[:, s, i, :], None, compute_op=ALU.add).then_inc(s_tab[k], 16)

            in_turns(pool, steps, edge_scatter, B, 2, 2, 2)
            pool.wait_ge(s_deg, 1)
            nc.gpsimd.tensor_tensor(dis[:, :], deg[:, :], neg_half[:, :], ALU.pow).then_inc(s_pool, steps.up())
            pool.wait_ge(s_pool, steps.value())
            nc.gpsimd.tensor_tensor(dis[:, :], dis[:, :], has[:, :], ALU.mult).then_inc(s_dis, 1)

            def root(ready, done, n, out_, in_):
                pool.wait_ge(ready, n)
                nc.gpsimd.tensor_tensor(out_, in_, neg_half[:, 0:GT], ALU.pow).then_inc(done, 1)

            def mlp_roots(g, s=None):
                s = g % 2 if s is None else s
                if not (isinstance(g, int) and g >= G - 2):
                    root(s_v0, s_r0, g + 3, rstd[:, s, :], var[:, s, :])
                root(s_v1, s_r1, g + 1, rstd1[:, bass.ds(g * GT, GT)], var2[:, s, :])

            root(s_v0, s_r0, 1, rstd[:, 0, :], var[:, 0, :])
            root(s_v0, s_r0, 2, rstd[:, 1, :], var[:, 1, :])
            in_turns(pool, steps, mlp_roots, G, 2, 3, 2)

            def ffn0_roots(g, s=None):
                s = g % 2 if s is None else s
                root(s_vB, s_rB, g + 1, rstd[:, s, :], var[:, s, :])
                root(s_v2, s_r2, g + 1, rstd2[:, s, :], var2[:, s, :])

            in_turns(pool, steps, ffn0_roots, G, 2, 3, 2)

            pool.wait_ge(s_hw[0], 16 * ((G + 1) // 2))
            pool.wait_ge(s_hw[1], 16 * (G // 2))

            def step_gather(b, s=None):
                s = b % 2 if s is None else s
                pool.wait_ge(s_idx, b + 1)
                if not (isinstance(b, int) and b < 2):
                    pool.wait_ge(s_pair, (b - 1) * (EB // 2))
                pool.nop(nofuse=True)
                for i in range(EB):
                    nc.gpsimd.indirect_dma_start(mg[:, s, i, :], None, h_rows, bass.IndirectOffsetOnAxis(idx_a[:, s, i:i + 1], 0)).then_inc(s_gk[s], 16)

            def gather(b, s):
                pool.wait_ge(s_dsel, b + 1)
                if not (isinstance(b, int) and b < 2):
                    pool.wait_ge(s_mmm, b - 1)
                pool.nop(nofuse=True)
                for i in range(EB):
                    nc.gpsimd.indirect_dma_start(mg[:, s, i, :], None, h_rows, bass.IndirectOffsetOnAxis(idx_a[:, s, i:i + 1], 0)).then_inc(s_ga[s], 16)

            def messages(b, s=None):
                s = b % 2 if s is None else s
                if not (isinstance(b, int) and b == B - 1):
                    gather(b + 1, 1 - s)
                pool.wait_ge(s_mcp, b + 1)
                for i in range(EB):
                    k = i % K
                    if not (isinstance(b, int) and b == 0 and i < K):
                        pool.wait_ge(s_mt[k], b * (16 * EB // K) + 16 * (i // K))
                    pool.nop(nofuse=True)
                    nc.gpsimd.indirect_dma_start(node_sum[k], bass.IndirectOffsetOnAxis(idx_b[:, s, i:i + 1], 0),
                                                 ms[:, s, i, :], None, compute_op=ALU.add).then_inc(s_mt[k], 16)

            with pool.If_eq(pool.to_reg(pool.value_load(in_order[0:1, 0:1], min_val=0, max_val=1)), 1):
                in_turns(pool, steps, step_gather, MB, 2, 3, 2)
            with pool.Else():
                pool.wait_ge(s_fzd, 16 * 8 * K)
                gather(0, 0)
                in_turns(pool, steps, messages, B, 2, 2, 2)

            def gate_roots(g, s=None):
                s = g % 2 if s is None else s
                root(s_v3, s_r3, g + 1, rstd[:, s, :], var[:, s, :])

            in_turns(pool, steps, gate_roots, G, 2, 3, 2)
            pool.wait_ge(s_slots, 1)
            pool.wait_ge(s_x3c, G)
            for t in range(T):
                nc.gpsimd.indirect_dma_start(slot_x, bass.IndirectOffsetOnAxis(sc_idx[:, t:t + 1], 0), xn3[:, t, :], None).then_inc(s_disp, 16)
            pool.wait_ge(s_yw[0], 16 * (QN // 2))
            pool.wait_ge(s_yw[1], 16 * (QN // 2))
            pool.wait_ge(s_t5, QN)
            pool.wait_ge(s_o5e, QN)
            for t in range(T):
                nc.gpsimd.indirect_dma_start(yg[:, t, :], None, slot_y, bass.IndirectOffsetOnAxis(ga_idx[:, t:t + 1], 0)).then_inc(s_yg[t // EB], 16)

        @block.vector
        def _(dve):
            v = nc.vector
            st = Steps(s_dve)
            unsorted = Steps(s_dvf)

            def settle(c=st):
                dve.wait_ge(c.sem, c.value())

            def settle_fixed():
                settle()
                dve.nop(nofuse=True)

            v.memset(hT[:, 0, :, :], 0.0).then_inc(s_zero, 1)
            dve.wait_ge(s_raw, 32)
            v.tensor_copy(raw_f, raw_i).then_inc(s_rawf, 1)
            dve.wait_ge(s_rawT, 1)
            for k, f in enumerate((src_f, dst_f)):
                v.tensor_copy(f[:, :].rearrange("p (h c t) -> p h (c t)", h=2, c=4), ps[0:P, 2 * k:2 * k + 2, 0:400]).then_inc(s_dve, st.up())
            settle()
            dve.wait_ge(s_const, 1)
            v.tensor_scalar(hl_i, dst_f[:, :], 1.0 / P, None, ALU.mult).then_inc(s_dve, st.up())
            settle()
            v.tensor_copy(hi, hl_i).then_inc(s_dve, st.up())
            settle()
            v.scalar_tensor_tensor(lo, hi, -float(P), dst_f[:, :], ALU.mult, ALU.add).then_inc(s_dve, st.up())
            settle()
            for sign, op, bound in ((-1.0, ALU.is_lt, 0.0), (1.0, ALU.is_ge, float(P))):
                v.tensor_scalar(hl_w, lo, bound, sign, op, ALU.mult).then_inc(s_dve, st.up())
                settle()
                v.tensor_tensor(hi, hi, hl_w, ALU.add).then_inc(s_dve, st.up())
                v.scalar_tensor_tensor(lo, hl_w, -float(P), lo, ALU.mult, ALU.add).then_inc(s_dve, st.up())
                settle()

            def rows_to_add(s, col, rows, done, c=st):
                v.tensor_tensor(SL, S[:, s], not_first[:, :].unsqueeze(1).to_broadcast([P, EB, P]), ALU.mult).then_inc(c.sem, c.up())
                v.tensor_scalar(away[:, s], col, -1.0, spare[:, 0:1], ALU.mult, ALU.add).then_inc(c.sem, c.up())
                settle(c)
                v.tensor_reduce(dup[:, s], SL, AX, ALU.max).then_inc(c.sem, c.up())
                settle(c)
                v.tensor_tensor(dup[:, s], dup[:, s], away[:, s], ALU.mult).then_inc(c.sem, c.up())
                settle(c)
                v.tensor_tensor(rows, dup[:, s], col, ALU.add).then_inc(done, 1)

            def by_turns(body, total, c, first_turn=0):
                body(total[0], 0, total[0] // 2 + 1)
                had = c.value()
                body(total[0] + 1, 1, total[0] // 2 + 1)
                per, start = c.value() - had, c.value()
                with dve.Fori(total[0] // 2 + 1, total[1] // 2) as i:
                    for s in range(2):
                        c.base, c.k = start + (i * 2 + s - 2 - total[0]) * per, 0
                        body(i * 2 + s, s, i + 1)
                        assert c.k == per
                c.base, c.k = start + (total[1] - total[0] - 2) * per, 0

            def edge_select(b, s, turn, counts):
                dve.wait_ge(s_row[s], turn * 16)
                if not (isinstance(b, int) and b < 2):
                    dve.wait_ge(s_emm, b - 1)
                    dve.wait_ge(s_ecp, b - 1)
                col = src_f[:, bass.ds(b * EB, EB)]
                v.tensor_tensor(S[:, s], rowb[:, s], col.unsqueeze(2).to_broadcast([P, EB, P]), ALU.is_equal).then_inc(s_dve, st.up())
                if counts:
                    two = bass.ds(b * (2 * EB), 2 * EB)
                    v.tensor_tensor(ohh[:, s], hi_iota[:, :].unsqueeze(1).to_broadcast([P, 2 * EB, T]),
                                    hi[:, two].unsqueeze(2).to_broadcast([P, 2 * EB, T]), ALU.is_equal).then_inc(s_dve, st.up())
                    v.tensor_tensor(ohl[:, s], lo_iota[:, :].unsqueeze(1).to_broadcast([P, 2 * EB, P]),
                                    lo[:, two].unsqueeze(2).to_broadcast([P, 2 * EB, P]), ALU.is_equal).then_inc(s_dve, st.up())
                settle()
                rows_to_add(s, col, firsts[:, s], s_esel)

            by_turns(lambda b, s, turn: edge_select(b, s, turn, True), (0, HB), st)

            dve.wait_ge(s_emm, HB)
            v.tensor_copy(cnt[:, :], ps[0:P, 7, 0:T]).then_inc(s_sch, 1)
            dve.wait_ge(s_sch, 1)
            v.tensor_scalar(has[:, :], cnt[:, :], 0.0, None, ALU.is_gt).then_inc(s_dve, st.up())
            v.tensor_scalar(deg[:, :], cnt[:, :], 1.0, None, ALU.max).then_inc(s_deg, 1)
            dve.wait_ge(s_schp, 1)
            v.tensor_copy(walk[:, 0:1], ps[0:T, 6, 0:1]).then_inc(s_sch, 1)
            dve.wait_ge(s_schp, 2)
            v.tensor_copy(walk[:, 1:2], ps[0:T, 6, 1:2]).then_inc(s_dve, st.up())
            settle()
            v.tensor_scalar(walk_i[:, :], walk[:, 1:2], 1.0 / P, None, ALU.mult).then_inc(s_dve, st.up())
            settle()
            v.tensor_copy(walk[:, 2:3], walk_i[:, :]).then_inc(s_dve, st.up())
            settle()
            v.scalar_tensor_tensor(walk[:, 3:4], walk[:, 2:3], -float(P), walk[:, 1:2], ALU.mult, ALU.add).then_inc(s_dve, st.up())
            settle()
            for sign, op, bound in ((-1.0, ALU.is_lt, 0.0), (1.0, ALU.is_ge, float(P))):
                v.tensor_scalar(walk[:, 4:5], walk[:, 3:4], bound, sign, op, ALU.mult).then_inc(s_dve, st.up())
                settle()
                v.tensor_tensor(walk[:, 2:3], walk[:, 2:3], walk[:, 4:5], ALU.add).then_inc(s_dve, st.up())
                settle()
            v.tensor_scalar(walk[:, 2:3], walk[:, 2:3], float(ET - 1), None, ALU.min).then_inc(s_dve, st.up())
            settle()
            v.tensor_tensor(walk[:, 5:6], walk[:, 2:3], n_iota[0:T, 0:1], ALU.add).then_inc(s_dve, st.up())
            v.tensor_copy(step_i, step_ii).then_inc(s_dve, st.up())
            settle()
            v.tensor_scalar(past, step_i[0:T - 1, :], walk[0:T - 1, 5:6], None, ALU.is_gt).then_inc(s_sch, 1)
            dve.wait_ge(s_schp, 3)
            v.tensor_copy(w_at.rearrange("p (h q) -> p h q", h=2), ps[0:P, 0:2, 0:MB * EB // 2]).then_inc(s_dve, st.up())
            settle()
            v.tensor_tensor(t_at, step_i, w_at, ALU.subtract).then_inc(s_dve, st.up())
            settle()
            for c in range(8):
                if c >= 4:
                    dve.wait_ge(s_schp, c)
                v.tensor_scalar(sel[:, c % 4, :], t_at[0:100, :], tile_no[0:100, c:c + 1], None, ALU.is_equal).then_inc(s_sch, 1)
            at = w_at[0:1, :].rearrange("a (b k) -> a b k", k=EB)
            ws = hits[1][0:1, 0:MB * (EB - 1)].rearrange("a (b k) -> a b k", k=EB - 1)
            v.tensor_tensor(ws, at[:, :, 1:EB], at[:, :, 0:EB - 1], ALU.subtract).then_inc(s_dve, st.up())
            settle()
            v.tensor_tensor(ws, ws, pow2[:, :].unsqueeze(1).to_broadcast([1, MB, EB - 1]), ALU.mult).then_inc(s_dve, st.up())
            settle()
            v.tensor_reduce(wsum[:, :], ws, AX, ALU.add).then_inc(s_dve, st.up())
            settle()
            v.scalar_tensor_tensor(words[:, :], wsum[:, :], 64.0, at[:, :, 0:1].rearrange("a b k -> a (b k)"), ALU.mult, ALU.add).then_inc(s_dve, st.up())
            dve.wait_ge(s_schp, 11)
            v.tensor_copy(src_at[:, :].rearrange("p (h q) -> p h q", h=2), ps[0:P, 2 * 0:2, 0:MB * EB // 2]).then_inc(s_dve, st.up())
            v.scalar_tensor_tensor(not_dst[:, :].rearrange("p (h q) -> p h q", h=2), w_at.rearrange("p (h q) -> p h q", h=2), float(P),
                                   ps[0:P, 6:8, 0:MB * EB // 2], ALU.mult, ALU.subtract).then_inc(s_dve, st.up())
            settle()
            v.tensor_scalar(hits[0], not_dst[:, :], 0.0, None, ALU.is_le).then_inc(s_dve, st.up())
            settle()
            v.scalar_tensor_tensor(hits[1], not_dst[:, :], -float(P), hits[0], ALU.is_gt, ALU.mult).then_inc(s_dve, st.up())
            settle()
            v.tensor_reduce(met[:, :], hits[1], AX, ALU.add).then_inc(s_sch, 1)
            dve.wait_ge(s_schp, 12)
            v.tensor_scalar(in_order[:, :], ps[0:1, 0, 0:1], float(EDGES), None, ALU.is_equal).then_inc(s_sched, 1)

            by_turns(lambda b, s, turn: edge_select(b, s, turn, False), (HB, B), st)

            for k in range(1, K):
                dve.wait_ge(s_part, 16 * (k + 1))
                v.tensor_tensor(agg, agg, part, ALU.add).then_inc(s_added, 1)
                dve.wait_ge(s_added, k)
            v.tensor_scalar(cnt[:, :], agg3[:, :, DE:DC].rearrange("p t a -> p (t a)"), 1.0, None, ALU.max).then_inc(s_dve, st.up())
            settle()
            v.reciprocal(cnt[:, :], cnt[:, :]).then_inc(s_dve, st.up())
            settle()

            def ln_stats(rows, s, stat_, mv_of, var_, ready):
                dve.nop(nofuse=True)
                for t in range(GT):
                    v.bn_stats(stat_[:, s, t, :], rows(t)).then_inc(s_dve, st.up())
                settle_fixed()
                for t in range(GT):
                    v.bn_aggr(mv_of(t), stat_[:, s, t, :]).then_inc(s_dve, st.up())
                settle()
                for t in range(GT):
                    i_ = v.tensor_scalar(var_[:, s, t:t + 1], mv_of(t)[:, 1:2], EPS, None, ALU.add)
                i_.then_inc(ready, 1)

            def ln0(g, s):
                ln_stats(lambda t: x[:, bass.ds(g * GT + t, 1), :].rearrange("p a d -> p (a d)"), s, stat,
                         lambda t: mv[:, s, t, :], var, s_v0)
                dve.wait_ge(s_r0, g + 1)
                if not (isinstance(g, int) and g < 2):
                    dve.wait_ge(s_t0, g - 1)
                for t in range(GT):
                    v.tensor_scalar(xg[:, s, t, 0:D], x[:, bass.ds(g * GT + t, 1), :].rearrange("p a d -> p (a d)"),
                                    mv[:, s, t, 0:1], rstd[:, s, t:t + 1], ALU.subtract, ALU.mult)
                    i_ = v.tensor_scalar(xg[:, s, t, D:D + DE], agg3[:, bass.ds(g * GT + t, 1), 0:DE].rearrange("p a d -> p (a d)"),
                                         cnt[:, bass.ds(g * GT + t, 1)], None, ALU.mult)
                i_.then_inc(s_x0, 1)

            def mlp(g, s=None):
                fixed = isinstance(g, int)
                s = g % 2 if s is None else s
                if not (fixed and g >= G - 2):
                    ln0(g + 2, s)
                xs = x[:, bass.ds(g * GT, GT), :]
                dve.wait_ge(s_o0, g + 1)
                v.tensor_tensor(yb[:, s], ps[0:P, 4 + s, :].rearrange("p (t d) -> p t d", t=GT),
                                b2A[:, :].unsqueeze(1).to_broadcast([P, GT, D]), ALU.add).then_inc(s_o0e, 1)
                dve.wait_ge(s_o0e, g + 1)
                v.tensor_tensor(xs, xs, yb[:, s], ALU.add).then_inc(s_dve, st.up())
                settle()
                ln_stats(lambda t: x[:, bass.ds(g * GT + t, 1), :].rearrange("p a d -> p (a d)"), s, stat2,
                         lambda t: mv2[:, s, t, :], var2, s_v1)
                v.tensor_copy(mv1[:, bass.ds(g * GT, GT), :], mv2[:, s]).then_inc(s_dve, st.up())
                dve.wait_ge(s_r1, g + 1)
                if not (fixed and g < 2):
                    dve.wait_ge(s_t1, g - 1)
                for t in range(GT):
                    i_ = v.tensor_scalar(xh[:, s, t, :], x[:, bass.ds(g * GT + t, 1), :].rearrange("p a d -> p (a d)"),
                                         mv2[:, s, t, 0:1], rstd1[:, bass.ds(g * GT + t, 1)], ALU.subtract, ALU.mult)
                i_.then_inc(s_x1, 1)

            dve.wait_ge(s_x, 16)
            dve.wait_ge(s_cst, 160)
            ln0(0, 0)
            ln0(1, 1)
            in_turns(dve, st, mlp, G, 2, 3, 2)

            dve.wait_ge(s_t1e, G)
            v.tensor_reduce(mean[:, :], msum[:, :, :], AX, ALU.add).then_inc(s_dve, st.up())
            settle()
            v.tensor_scalar(mean[:, :], mean[:, :], 1.0 / NODES, None, ALU.mult).then_inc(s_mean, 1)
            dve.wait_ge(s_lg, 1)
            v.tensor_tensor(rt[:, 1, :], ps[0:1, 6, 0:E], rt[:, 0, :], ALU.add).then_inc(s_dve, st.up())
            settle()

            def less_max(dst, src_, n):
                v.tensor_reduce(rt[:, 9, 6:7], src_, AX, ALU.max).then_inc(s_dve, st.up())
                settle()
                v.tensor_scalar(dst, src_, rt[:, 9, 6:7], None, ALU.subtract).then_inc(s_e1, 1)
                dve.wait_ge(s_e1x, n)

            def over_sum(dst, src_, at):
                v.reciprocal(rt[:, 9, at + 1:at + 2], rt[:, 9, at:at + 1]).then_inc(s_dve, st.up())
                settle()
                v.tensor_scalar(dst, src_, rt[:, 9, at + 1:at + 2], None, ALU.mult).then_inc(s_dve, st.up())
                settle()

            less_max(rt[:, 1, :], rt[:, 1, :], 1)
            over_sum(rt[:, 3, :], rt[:, 2, :], 0)
            v.tensor_scalar(rt[:, 6, :], rt[:, 3, :], float(NODES), None, ALU.mult).then_inc(s_dve, st.up())
            settle()
            v.reciprocal(rt[:, 7, :], rt[:, 6, :]).then_inc(s_dve, st.up())
            settle()
            v.tensor_scalar(rt[:, 8, :], rt[:, 7, :], float(CAP), 1.0, ALU.mult, ALU.min).then_inc(s_dve, st.up())
            settle()
            v.tensor_tensor(rt[:, 4, :], rt[:, 3, :], rt[:, 8, :], ALU.mult).then_inc(s_dve, st.up())
            settle()
            less_max(rt[:, 4, :], rt[:, 4, :], 2)
            over_sum(rt[:, 12, :], rt[:, 5, :], 2)
            v.max(rt[:, 13, :], rt[:, 12, :]).then_inc(s_dve, st.up())
            settle()
            v.max_index(rt_id[:, :], rt[:, 13, :], rt[:, 12, :]).then_inc(s_rid, 1)
            v.tensor_scalar(rt[:, 10, 0:2], rt[:, 13, 0:2], rt[:, 13, 0:1], None, ALU.subtract).then_inc(s_e1, 1)
            dve.wait_ge(s_e1x, 3)
            over_sum(rt[:, 14, 0:2], rt[:, 11, 0:2], 4)
            for k in range(2):
                i_ = v.tensor_copy(wrow[:, k, :], rt[:, 14, k:k + 1].to_broadcast([1, P]))
            i_.then_inc(s_e2x, 1)
            dve.wait_ge(s_wb, 1)
            v.tensor_copy(b2B[:, :], ps[0:P, 5, 0:D]).then_inc(s_dve, st.up())
            v.tensor_copy(wcol[:, :], ps[:, 4, 0:2]).then_inc(s_wbc, 1)
            dve.wait_ge(s_wbc, 1)

            def ffn0(g, s=None):
                fixed = isinstance(g, int)
                s = g % 2 if s is None else s
                xs = x[:, bass.ds(g * GT, GT), :]
                y, z = yb[:, s], wk[:, s]

                def wide(r):
                    return r[:, :].unsqueeze(1).to_broadcast([P, GT, D])
                for t in range(GT):
                    v.tensor_scalar(z[:, t, :], x[:, bass.ds(g * GT + t, 1), :].rearrange("p a d -> p (a d)"),
                                    mv1[:, bass.ds(g * GT + t, 1), 0:1].rearrange("p a d -> p (a d)"),
                                    rstd1[:, bass.ds(g * GT + t, 1)], ALU.subtract, ALU.mult).then_inc(s_dve, st.up())
                settle()
                v.tensor_tensor(z, z, wide(b2B), ALU.add).then_inc(s_dve, st.up())
                settle()
                dve.wait_ge(s_oB, g + 1)
                v.tensor_tensor(y, ps[0:P, 4 + s, :].rearrange("p (t d) -> p t d", t=GT), z, ALU.add).then_inc(s_oBe, 1)
                dve.wait_ge(s_oBe, g + 1)
                ln_stats(lambda t: y[:, t, :], s, stat, lambda t: mv[:, s, t, :], var, s_vB)
                dve.wait_ge(s_rB, g + 1)
                for t in range(GT):
                    v.tensor_scalar(z[:, t, :], y[:, t, :], mv[:, s, t, 0:1], rstd[:, s, t:t + 1], ALU.subtract, ALU.mult).then_inc(s_dve, st.up())
                settle()
                v.tensor_tensor(z, z, wide(gamma), ALU.mult).then_inc(s_dve, st.up())
                settle()
                v.tensor_tensor(z, z, wide(beta), ALU.add).then_inc(s_dve, st.up())
                settle()
                v.tensor_tensor(xs, xs, z, ALU.add).then_inc(s_dve, st.up())
                settle()
                ln_stats(lambda t: x[:, bass.ds(g * GT + t, 1), :].rearrange("p a d -> p (a d)"), s, stat2,
                         lambda t: mv2[:, s, t, :], var2, s_v2)
                dve.wait_ge(s_r2, g + 1)
                if not (fixed and g < 2):
                    dve.wait_ge(s_t2, g - 1)
                for t in range(GT):
                    i_ = v.tensor_scalar(xh[:, s, t, :], x[:, bass.ds(g * GT + t, 1), :].rearrange("p a d -> p (a d)"),
                                         mv2[:, s, t, 0:1], rstd2[:, s, t:t + 1], ALU.subtract, ALU.mult)
                i_.then_inc(s_x2, 1)

            in_turns(dve, st, ffn0, G, 2, 3, 2)

            def step_add(b, s=None):
                word = dve.value_load(words[0:1, bass.ds(b, 1)], min_val=0, max_val=(64 << (EB - 1)) - 1)
                w, goes_on = dve.snap(word & 63), dve.snap(word >> 6)
                for k in range(EB):
                    row = acc[:, bass.ds(nc.s_assert_within(w, 0, T - 1, skip_runtime_bounds_check_because="the walk ends at the last window"), 1), :].rearrange("p a d -> p (a d)")
                    if k < EB - 1:
                        w = dve.snap(w + ((goes_on >> k) & 1))
                    if k % 2 == 0:
                        dve.wait_ge(s_pair, b * (EB // 2) + (k // 2 + 1))
                    if not (isinstance(b, int) and b == 0 and k == 0):
                        dve.wait_ge(s_acc, b * EB + k)
                    v.tensor_tensor(row, row, ps[0:P, k // 2, (k % 2) * D:(k % 2 + 1) * D], ALU.add).then_inc(s_acc, 1)

            def msg_select(b, s, turn):
                c = unsorted
                dve.wait_ge(s_drow[s], turn * 16)
                if not (isinstance(b, int) and b < 2):
                    dve.wait_ge(s_mmm, b - 1)
                    for k in range(K):
                        dve.wait_ge(s_mt[k], (b - 1) * (16 * EB // K))
                col = dst_f[:, bass.ds(b * EB, EB)]
                v.tensor_copy(idx_a[:, s, :], src_f[:, bass.ds(b * EB, EB)]).then_inc(c.sem, c.up())
                v.tensor_tensor(S[:, s], rowb[:, s], col.unsqueeze(2).to_broadcast([P, EB, P]), ALU.is_equal).then_inc(c.sem, c.up())
                settle(c)
                rows_to_add(s, col, idx_b[:, s, :], s_dsel, c)

            def sum_tables(g, s, turn):
                c = unsorted
                dve.wait_ge(s_nt[s], turn * (16 * K))
                for k in range(1, K):
                    o_ = acc[:, bass.ds(g * GT, GT), :] if k == K - 1 else yb[:, s]
                    v.tensor_tensor(o_, tab[:, s, 0] if k == 1 else yb[:, s], tab[:, s, k], ALU.add).then_inc(
                        s_fs if k == K - 1 else c.sem, 1 if k == K - 1 else c.up())
                    if k < K - 1:
                        settle(c)

            dve.wait_ge(s_dis, 1)
            dve.wait_ge(s_hB, 8 * G)
            with dve.If_eq(dve.to_reg(dve.value_load(in_order[0:1, 0:1], min_val=0, max_val=1)), 1):
                v.memset(acc, 0.0).then_inc(s_accz, 1)
                dve.wait_ge(s_accz, 1)
                in_turns(dve, Steps(), step_add, MB, 2, 3, 2)
                dve.wait_ge(s_acc, MB * EB)
            with dve.Else():
                dve.wait_ge(s_hrow, G)
                v.memset(hT[:, 0, :, :], 0.0).then_inc(s_fz, 1)
                by_turns(msg_select, (0, B), unsorted)
                by_turns(sum_tables, (0, G - 1), unsorted)
                sum_tables(G - 1, 0, G // 2 + 1)
                dve.wait_ge(s_fs, G)

            def gate_rows(g, s):
                fixed = isinstance(g, int)
                for t in range(GT):
                    xs = x[:, bass.ds(g * GT + t, 1), :].rearrange("p a d -> p (a d)")
                    v.scalar_tensor_tensor(xs, acc[:, bass.ds(g * GT + t, 1), :].rearrange("p a d -> p (a d)"), dis[:, bass.ds(g * GT + t, 1)],
                                           xs, ALU.mult, ALU.add).then_inc(s_dve, st.up())
                settle()
                ln_stats(lambda t: x[:, bass.ds(g * GT + t, 1), :].rearrange("p a d -> p (a d)"), s, stat,
                         lambda t: mv[:, s, t, :], var, s_v3)
                dve.wait_ge(s_r3, g + 1)
                if not (fixed and g < 2):
                    dve.wait_ge(s_t3, g - 1)
                    dve.wait_ge(s_x3c, g - 1)
                for t in range(GT):
                    i_ = v.tensor_scalar(xh[:, s, t, :], x[:, bass.ds(g * GT + t, 1), :].rearrange("p a d -> p (a d)"),
                                         mv[:, s, t, 0:1], rstd[:, s, t:t + 1], ALU.subtract, ALU.mult)
                i_.then_inc(s_x3, 1)

            def logits(g, s):
                dve.wait_ge(s_l3, g + 1)
                v.tensor_tensor(gate3[:, 0, bass.ds(g * GT, GT), :], ps[0:P, 6 + s, 0:GT * E].rearrange("p (t e) -> p t e", t=GT),
                                gb[:, :].unsqueeze(1).to_broadcast([P, GT, E]), ALU.add).then_inc(s_l3e, 1)

            def gate_group(g, s=None):
                s = g % 2 if s is None else s
                gate_rows(g, s)
                if not (isinstance(g, int) and g == 0):
                    logits(g - 1, 1 - s)

            in_turns(dve, st, gate_group, G, 2, 3, 2)
            logits(G - 1, 0)
            dve.wait_ge(s_l3e, G)

            def tt(o_, i0, i1, op):
                v.tensor_tensor(o_, i0, i1, op).then_inc(s_dve, st.up())
                settle()

            def ts(o_, i0, c1, c2, op0, op1=ALU.bypass):
                v.tensor_scalar(o_, i0, c1, c2, op0, op1).then_inc(s_dve, st.up())
                settle()

            def red(o_, i_, op):
                v.tensor_reduce(o_, i_, AX, op).then_inc(s_dve, st.up())
                settle()

            def per_token(k):
                return g50[:, k, :].unsqueeze(2).to_broadcast([P, T, E])

            def per_expert(r):
                return r.unsqueeze(1).to_broadcast([P, T, E])
            red(g50[:, 0, :], gate3[:, 0], ALU.max)
            v.tensor_tensor(gate3[:, 1], gate3[:, 0], per_token(0), ALU.subtract).then_inc(s_ga1, 1)
            dve.wait_ge(s_gexp, 1)
            red(g50[:, 1, :], gate3[:, 1], ALU.add)
            red(g50[:, 2, :], gate3[:, 1], ALU.max)
            v.reciprocal(g50[:, 3, :], g50[:, 1, :]).then_inc(s_dve, st.up())
            settle()
            tt(xn3[:, :, D:D + 1].rearrange("p t a -> p (t a)"), g50[:, 2, :], g50[:, 3, :], ALU.mult)
            tt(gate3[:, 2], gate3[:, 1], per_token(2), ALU.is_ge)
            ts(gate3[:, 3], gate3[:, 2], -float(E), float(E), ALU.mult, ALU.add)
            tt(gate3[:, 4], gate3[:, 3], per_expert(e_iota[:, :]), ALU.add)
            red(g50[:, 4, :], gate3[:, 4], ALU.min)
            v.tensor_tensor(gate3[:, 5], per_expert(e_iota[:, :]), per_token(4), ALU.is_equal).then_inc(s_goh, 1)
            dve.wait_ge(s_grk, 1)
            v.tensor_copy(gate[:, 6, :], ps[0:P, 2, 0:T * E]).then_inc(s_dve, st.up())
            v.tensor_copy(gate[:, 7, :], ps[0:P, 3, 0:T * E]).then_inc(s_dve, st.up())
            v.memset(gate[:, 8, :], 1.0).then_inc(s_dve, st.up())
            settle()
            for e in range(E):
                v.tensor_tensor_scan(gate3[:, 9, :, e], gate3[:, 8, :, e], gate3[:, 7, :, e], 0.0, ALU.mult, ALU.add).then_inc(s_dve, st.up())
            settle()
            tt(gate3[:, 9], gate3[:, 9], gate3[:, 7], ALU.subtract)
            tt(gate3[:, 9], gate3[:, 9], gate3[:, 6], ALU.add)
            tt(gate3[:, 9], gate3[:, 9], gate3[:, 5], ALU.mult)
            red(g50[:, 5, :], gate3[:, 9], ALU.add)
            ts(g50[:, 6, :], g50[:, 5, :], float(CAP), None, ALU.is_lt)
            v.scalar_tensor_tensor(g50[:, 7, :], g50[:, 4, :], float(SLOTS), g50[:, 5, :], ALU.mult, ALU.add).then_inc(s_dve, st.up())
            settle()
            ts(g50[:, 8, :], n_iota[:, :], float(E * SLOTS), None, ALU.add)
            tt(g50[:, 9, :], g50[:, 7, :], g50[:, 8, :], ALU.subtract)
            tt(g50[:, 9, :], g50[:, 9, :], g50[:, 6, :], ALU.mult)
            tt(g50[:, 9, :], g50[:, 9, :], g50[:, 8, :], ALU.add)
            v.tensor_copy(sc_idx[:, :], g50[:, 9, :]).then_inc(s_dve, st.up())
            ts(g50[:, 10, :], g50[:, 7, :], -float(E * SLOTS), None, ALU.add)
            tt(g50[:, 10, :], g50[:, 10, :], g50[:, 6, :], ALU.mult)
            ts(g50[:, 10, :], g50[:, 10, :], float(E * SLOTS), None, ALU.add)
            v.tensor_copy(ga_idx[:, :], g50[:, 10, :]).then_inc(s_slots, 1)

            def expert_out(e, es, turns):
                fixed = isinstance(e, int)
                for j in range(QE):
                    s = j % 2
                    q = e * QE + j
                    y, r = yb[:, s], nanw
                    dve.wait_ge(s_wE[es], turns * 64)
                    dve.wait_ge(s_xe[es], turns * 16)
                    dve.wait_ge(s_o5, q + 1)
                    v.tensor_tensor(r[:, 0], ps[0:P, 4 + s, :].rearrange("p (t d) -> p t d", t=GT),
                                    b2E[:, es, :].unsqueeze(1).to_broadcast([P, GT, D]), ALU.add).then_inc(s_dve, st.up())
                    settle()
                    for t in range(GT):
                        i_ = v.tensor_scalar(r[:, 1, t, :], r[:, 0, t, :], xe[:, es, GT * j + t, D:D + 1], None, ALU.mult)
                    i_.then_inc(s_o5e, 1)
                    dve.wait_ge(s_o5e, q + 1)
                    if not (fixed and q < 2):
                        dve.wait_ge(s_yw[s], (q // 2) * 16 if fixed else (turns - 1) * (16 * QE) + (es * QE + j) // 2 * 16)
                    v.tensor_scalar(r[:, 2], r[:, 1], FMAX, 1e4, ALU.is_gt, ALU.mult).then_inc(s_dve, st.up())
                    v.tensor_scalar(r[:, 0], r[:, 1], -FMAX, -1e4, ALU.is_lt, ALU.mult).then_inc(s_dve, st.up())
                    v.tensor_scalar(r[:, 3], r[:, 1], FMAX, None, ALU.is_le).then_inc(s_dve, st.up())
                    settle()
                    v.tensor_tensor(y, r[:, 2], r[:, 0], ALU.add).then_inc(s_dve, st.up())
                    v.scalar_tensor_tensor(r[:, 3], r[:, 1], -FMAX, r[:, 3], ALU.is_ge, ALU.mult).then_inc(s_dve, st.up())
                    settle_fixed()
                    v.copy_predicated(y, r[:, 3].bitcast(u32), r[:, 1]).then_inc(s_y5, 1)
                    dve.wait_ge(s_y5, q + 1)

            by_turns(expert_out, (0, E), st)

            for c in range(T // EB):
                dve.wait_ge(s_yg[c], 16 * EB)
                xs = x[:, c * EB:(c + 1) * EB, :]
                v.tensor_tensor(xs, xs, yg[:, c * EB:(c + 1) * EB, :], ALU.add).then_inc(s_fin, 1)

        @block.tensor
        def _(pe):
            steps = Steps()
            mm, tr = nc.tensor.matmul, nc.tensor.transpose
            pe.wait_ge(s_const, 1)
            pe.wait_ge(s_rawf, 1)
            for k in range(2):
                for c in range(8):
                    i_ = tr(ps[0:P, 2 * k + c // 4, (c % 4) * 100:(c % 4 + 1) * 100], raw_f[:, k, c, :], ident[0:100, 0:100])
            i_.then_inc(s_rawT, 1)

            def edge_sums(b, s, turns, first=False, counts=False, last=False):
                pe.wait_ge(s_esel, b + 1)
                pe.wait_ge(s_va[s], turns * 16)
                if not first:
                    pe.wait_ge(s_ecp, b - 1)
                for i in range(2 * EB if counts else 0):
                    mm(ps[0:P, 7, 0:T], ohl[:, s, i, :], ohh[:, s, i, :], start=(first and s == 0 and i == 0), stop=(last and s == 1 and i == 2 * EB - 1))
                for i in range(EB):
                    i_ = mm(ps[0:P, 2 + 2 * s + i // 5, (i % 5) * DC:(i % 5 + 1) * DC], S[:, s, i, :], va[:, s, i, :], start=True, stop=True)
                i_.then_inc(s_emm, 1)

            edge_sums(0, 0, 1, first=True, counts=True)
            edge_sums(1, 1, 1, first=True, counts=True)
            with pe.Fori(1, HB // 2 - 1) as i:
                edge_sums(i * 2, 0, i + 1, counts=True)
                edge_sums(i * 2 + 1, 1, i + 1, counts=True)
            edge_sums(HB - 2, 0, HB // 2, counts=True, last=True)
            edge_sums(HB - 1, 1, HB // 2, counts=True, last=True)

            pe.wait_ge(s_sch, 1)
            mm(ps[0:T, 6, 0:1], cnt[:, :], ones[:, 0:1], start=True, stop=True).then_inc(s_schp, 1)
            pe.wait_ge(s_sch, 2)
            mm(ps[0:T, 6, 1:2], before[0:T, 0:T], walk[:, 0:1], start=True, stop=False)
            mm(ps[0:T, 6, 1:2], ident[0:T, 0:T], walk[:, 0:1], start=False, stop=True).then_inc(s_schp, 1)
            pe.wait_ge(s_sch, 3)
            for h in range(2):
                q = slice(h * MB * EB // 2, (h + 1) * MB * EB // 2)
                i_ = mm(ps[0:P, h, 0:MB * EB // 2], ones[0:T - 1, :], past[:, q], start=True, stop=True)
            i_.then_inc(s_schp, 1)
            for c in range(8):
                pe.wait_ge(s_sch, c + 4)
                for k in range(2):
                    for h in range(2):
                        q = slice(h * MB * EB // 2, (h + 1) * MB * EB // 2)
                        i_ = mm(ps[0:P, 6 * k + h, 0:MB * EB // 2], raw_f[:, k, c, :], sel[:, c % 4, q], start=(c == 0), stop=(c == 7))
                i_.then_inc(s_schp, 1)
            pe.wait_ge(s_sch, 12)
            mm(ps[0:1, 0, 0:1], met[:, :], ones[:, 0:1], start=True, stop=True).then_inc(s_schp, 1)

            with pe.Fori(HB // 2, B // 2) as i:
                edge_sums(i * 2, 0, i + 1)
                edge_sums(i * 2 + 1, 1, i + 1)

            pe.wait_ge(s_wA, 64)
            pe.wait_ge(s_cst, 160)
            pe.wait_ge(s_sched, 1)
            for m in range(4):
                i_ = mm(ps[:, 7, m:m + 1], wU[:, m * 128:(m + 1) * 128], u0[:, :], start=True, stop=True)
            i_.then_inc(s_bA, 1)

            def T0(g, s):
                pe.wait_ge(s_x0, g + 1)
                if not (isinstance(g, int) and g == 0):
                    pe.wait_ge(s_t0e, g)
                for t in range(GT):
                    for c in range(2):
                        tr(ps[:, s, c * N + t * P:c * N + (t + 1) * P], xg[:, s, t, c * 128:(c + 1) * 128], ident[0:P, 0:P])
                    i_ = tr(ps[0:DE, 6, s * N + t * P:s * N + (t + 1) * P], xg[:, s, t, D:D + DE], ident[0:P, 0:P])
                i_.then_inc(s_t0, 1)

            def T1(g, s):
                pe.wait_ge(s_x1, g + 1)
                if isinstance(g, int) and g == 0:
                    pe.wait_ge(s_bAset, 1)
                else:
                    pe.wait_ge(s_t1e, g)
                for t in range(GT):
                    for c in range(2):
                        i_ = tr(ps[:, 7, c * N + t * P:c * N + (t + 1) * P], xh[:, s, t, c * 128:(c + 1) * 128], ident[0:P, 0:P])
                i_.then_inc(s_t1, 1)

            def mlp(g, s=None):
                fixed = isinstance(g, int)
                s = g % 2 if s is None else s
                if not (fixed and g == G - 1):
                    T0(g + 1, 1 - s)
                pe.wait_ge(s_t0e, g + 1)
                for m in range(4):
                    if not (fixed and g == 0 and m < 2):
                        pe.wait_ge(s_h0e, g * 4 + (m - 1))
                    f = slice(m * 128, (m + 1) * 128)
                    for c in range(2):
                        mm(ps[:, 2 + m % 2, 0:N], wA1[:, c, f], xTg[:, s, c, :], start=(c == 0), stop=False)
                    mm(ps[:, 2 + m % 2, 0:N], wA1[0:DE, 2, f], aT[:, s, :], start=False, stop=True).then_inc(s_h0, 1)
                if not (fixed and g == 0):
                    T1(g - 1, 1 - s)
                pe.wait_ge(s_h0e, g * 4 + 4)
                if not (fixed and g < 2):
                    pe.wait_ge(s_o0e, g - 1)
                for t in range(GT):
                    for m in range(4):
                        i_ = mm(ps[0:P, 4 + s, t * D:(t + 1) * D], hT[:, s, m, t * P:(t + 1) * P], wA2[:, m, :], start=(m == 0), stop=(m == 3))
                i_.then_inc(s_o0, 1)

            pe.wait_ge(s_ecp, B)
            T0(0, 0)
            in_turns(pe, steps, mlp, G, 2, 3, 2)
            T1(G - 1, (G - 1) % 2)

            pe.wait_ge(s_mean, 1)
            for c in range(2):
                i_ = mm(ps[0:1, 6, 0:E], mean[:, c:c + 1], wr[:, c, :], start=(c == 0), stop=(c == 1))
            i_.then_inc(s_lg, 1)
            pe.wait_ge(s_o0e, G)
            pe.wait_ge(s_e2x, 1)
            pe.wait_ge(s_b2r, 32)
            mm(ps[:, 4, 0:2], ones[0:1, 0:1].to_broadcast([1, 128]), rt[:, 14, 0:2], start=True, stop=True)
            for k in range(2):
                i_ = mm(ps[0:P, 5, 0:D], wrow[:, k, :], b2rows[:, k, :], start=(k == 0), stop=(k == 1))
            i_.then_inc(s_wb, 1)

            def T2(g, s):
                pe.wait_ge(s_x2, g + 1)
                if not (isinstance(g, int) and g < 2):
                    pe.wait_ge(s_t2e, g - 1)
                for t in range(GT):
                    for c in range(2):
                        i_ = tr(ps[:, s, c * N + t * P:c * N + (t + 1) * P], xh[:, s, t, c * 128:(c + 1) * 128], ident[0:P, 0:P])
                i_.then_inc(s_t2, 1)

            def H(g, s):
                pe.wait_ge(s_t2e, g + 1)
                if not (isinstance(g, int) and g == 0):
                    pe.wait_ge(s_hrow, g)
                for t in range(GT):
                    for c in range(2):
                        i_ = mm(ps[0:P, 7, t * D:(t + 1) * D], xTg[:, s, c, t * P:(t + 1) * P], wG[:, c, :], start=(c == 0), stop=(c == 1))
                i_.then_inc(s_hm, 1)

            def ffn0(g, s=None):
                fixed = isinstance(g, int)
                s = g % 2 if s is None else s
                for m in range(8):
                    if not (fixed and g == 0 and m < 2):
                        pe.wait_ge(s_hBe, g * 8 + (m - 1))
                    for c in range(2):
                        i_ = mm(ps[:, 2 + m % 2, 0:N], wB1[:, c, m * 128:(m + 1) * 128], xnT[:, c, bass.ds(g * N, N)], start=(c == 0), stop=(c == 1))
                    i_.then_inc(s_hB, 1)
                if not (fixed and g < 2):
                    T2(g - 2, s)
                pe.wait_ge(s_hBe, g * 8 + 8)
                if not (fixed and g < 2):
                    pe.wait_ge(s_oBe, g - 1)
                for t in range(GT):
                    for m in range(8):
                        i_ = mm(ps[0:P, 4 + s, t * D:(t + 1) * D], hT[:, s, m, t * P:(t + 1) * P], wB2[:, m, :], start=(m == 0), stop=(m == 7))
                i_.then_inc(s_oB, 1)
                if not (fixed and g < 2):
                    H(g - 2, s)

            pe.wait_ge(s_wbc, 1)
            pe.wait_ge(s_wB, 96)
            pe.wait_ge(s_wBs, 1)
            in_turns(pe, steps, ffn0, G, 4, 3, 2)
            for g in (G - 2, G - 1):
                T2(g, g % 2)
                H(g, g % 2)

            def step_sums(b, s, turn):
                pe.wait_ge(s_onto, b + 1)
                pe.wait_ge(s_gk[s], turn * (16 * EB))
                for i in range(EB):
                    if i % 2 == 0 and not (isinstance(b, int) and b == 0):
                        pe.wait_ge(s_acc, b * EB - EB + (i + 2))
                    i_ = mm(ps[0:P, i // 2, (i % 2) * D:(i % 2 + 1) * D], onto[:, s, i, :], mg[:, s, i, :], start=True, stop=True)
                    if i % 2:
                        i_.then_inc(s_pair, 1)

            def msg_sums(b, s, turns, first=False):
                pe.wait_ge(s_dsel, b + 1)
                pe.wait_ge(s_ga[s], turns * (16 * EB))
                if not first:
                    pe.wait_ge(s_mcp, b)
                for i in range(EB):
                    i_ = mm(ps[0:P, i // 2, (i % 2) * D:(i % 2 + 1) * D], S[:, s, i, :], mg[:, s, i, :], start=True, stop=True)
                i_.then_inc(s_mmm, 1)

            pe.wait_ge(s_hrow, G)
            with pe.If_eq(pe.to_reg(pe.value_load(in_order[0:1, 0:1], min_val=0, max_val=1)), 1):
                step_sums(0, 0, 1)
                step_sums(1, 1, 1)
                with pe.Fori(1, MB // 2) as i:
                    step_sums(i * 2, 0, i + 1)
                    step_sums(i * 2 + 1, 1, i + 1)
                step_sums(MB - 1, 0, MB // 2 + 1)
                pe.wait_ge(s_acc, MB * EB)
            with pe.Else():
                msg_sums(0, 0, 1, first=True)
                msg_sums(1, 1, 1)
                with pe.Fori(1, B // 2) as i:
                    msg_sums(i * 2, 0, i + 1)
                    msg_sums(i * 2 + 1, 1, i + 1)
                pe.wait_ge(s_mcp, B)

            def gate_mm(g, s=None):
                s = g % 2 if s is None else s
                pe.wait_ge(s_x3, g + 1)
                if not (isinstance(g, int) and g < 2):
                    pe.wait_ge(s_t3e, g - 1)
                for t in range(GT):
                    for c in range(2):
                        i_ = tr(ps[:, s, c * N + t * P:c * N + (t + 1) * P], xh[:, s, t, c * 128:(c + 1) * 128], ident[0:P, 0:P])
                i_.then_inc(s_t3, 1)
                pe.wait_ge(s_t3e, g + 1)
                if not (isinstance(g, int) and g < 2):
                    pe.wait_ge(s_l3e, g - 1)
                for t in range(GT):
                    for c in range(2):
                        i_ = mm(ps[0:P, 6 + s, t * E:(t + 1) * E], xTg[:, s, c, t * P:(t + 1) * P], gw[:, c, :], start=(c == 0), stop=(c == 1))
                i_.then_inc(s_l3, 1)

            in_turns(pe, steps, gate_mm, G, 2, 3, 2)
            pe.wait_ge(s_goh, 1)
            mm(ps[0:P, 2, 0:T * E], before[:, :], gate[:, 5, :], start=True, stop=True)
            mm(ps[0:P, 3, 0:T * E], ones[:, :], gate[:, 5, :], start=True, stop=True).then_inc(s_grk, 1)

            def T5(q, s, es, j):
                if not (isinstance(q, int) and q < 2):
                    pe.wait_ge(s_t5e, q - 1)
                for t in range(GT):
                    for c in range(2):
                        i_ = tr(ps[:, s, c * N + t * P:c * N + (t + 1) * P], xe[:, es, GT * j + t, c * 128:(c + 1) * 128], ident[0:P, 0:P])
                i_.then_inc(s_t5, 1)

            def expert(e, es, turns, last=False):
                fixed = isinstance(e, int)
                pe.wait_ge(s_wE[es], turns * 64)
                for j in range(QE):
                    q, s = e * QE + j, j % 2
                    if j < QE - 1:
                        T5(q + 1, 1 - s, es, j + 1)
                    elif not last:
                        pe.wait_ge(s_xe[1 - es], (turns + es) * 16)
                        T5(q + 1, 1 - s, 1 - es, 0)
                    pe.wait_ge(s_t5e, q + 1)
                    for m in range(8):
                        if not (fixed and q == 0 and m < 2):
                            pe.wait_ge(s_h5e, q * 8 + (m - 1))
                        for c in range(2):
                            i_ = mm(ps[:, 2 + m % 2, 0:N], w1E[:, es, c, m * 128:(m + 1) * 128], xTg[:, s, c, :], start=(c == 0), stop=(c == 1))
                        i_.then_inc(s_h5, 1)
                    pe.wait_ge(s_h5e, q * 8 + 8)
                    if not (fixed and q < 2):
                        pe.wait_ge(s_o5e, q - 1)
                    for t in range(GT):
                        for m in range(8):
                            i_ = mm(ps[0:P, 4 + s, t * D:(t + 1) * D], hT[:, s, m, t * P:(t + 1) * P], w2E[:, es, m, :], start=(m == 0), stop=(m == 7))
                    i_.then_inc(s_o5, 1)

            pe.wait_ge(s_slots, 1)
            pe.wait_ge(s_xe[0], 16)
            T5(0, 0, 0, 0)
            expert(0, 0, 1)
            expert(1, 1, 1)
            with pe.Fori(1, E // 2 - 1) as i:
                expert(i * 2, 0, i + 1)
                expert(i * 2 + 1, 1, i + 1)
            expert(E - 2, 0, E // 2)
            expert(E - 1, 1, E // 2, last=True)


_INS = ["x", "src", "dst", "edge_attr_64", "L0_gnn_u", "L0_gnn_W1", "L0_gnn_b1", "L0_gnn_W2", "L0_gnn_b2", "L0_ffn_Wr",
        "L0_ffn_br", "L0_ffn_W1", "L0_ffn_b1", "L0_ffn_W2", "L0_ffn_b2", "L0_ffn_gamma", "L0_ffn_beta", "L1_gnn_W",
        "L1_ffn_gate_w", "L1_ffn_gate_b", "L1_ffn_w1", "L1_ffn_b1", "L1_ffn_w2", "L1_ffn_b2"]


def kernel(**inputs):
    import numpy as np
    import concourse.bacc as bacc
    from concourse import mybir as mb
    from concourse.bass_utils import run_bass_kernel_spmd as run

    nc = bacc.Bacc("TRN2", target_bir_lowering=False, num_devices=1)
    arrays, aps = {}, {}
    for name in _INS:
        v = np.ascontiguousarray(inputs[name])
        arrays[f"in_{name}"] = v
        aps[name] = nc.dram_tensor(f"in_{name}", v.shape, mb.dt.from_np(v.dtype), kind="ExternalInput").ap()
    out = nc.dram_tensor("out_0", (NODES, D), mb.dt.float32, kind="ExternalOutput").ap()
    build(nc, aps, out)
    return run(nc, [arrays], core_ids=[0]).results[0]["out_0"]
```

```python
import concourse.bass as bass
from concourse import mybir
from contextlib import ExitStack

NODES, EDGES, D, DE, DG = 6250, 100000, 256, 64, 128
P = 125
T, ET = NODES // P, EDGES // P
GT = 2
G, N = T // GT, GT * P
EB = 10
B = ET // EB
K = 5
HID0, HID1, HID2 = 512, 512, 1024
E, CAP = 8, 977
SLOTS = 1000
ST = SLOTS // P
DC = DE + 1
HB = B // 2
PLAN = 4
STAT = T // 5
AHEAD = HB + PLAN + STAT
CHUNKS = (0, 1, 5, 10, 15, 20, G)
XB = 16
HW = EB // 2
MEAN, RSTD, PROB = range(D, D + 3)
XW = D + 3
EPS = 1e-5
FMAX = 3.4028234663852886e38


class Steps:

    def __init__(self, sem=None):
        self.sem, self.base, self.k = sem, 0, 0

    def up(self):
        self.k += 1
        return 1

    def value(self):
        return self.base + self.k


def in_turns(eng, steps, body, total, head, tail, unit, first=0):
    per = 0
    for g in range(first, first + head):
        had = steps.value()
        body(g)
        per = steps.value() - had
    start = steps.value()
    with eng.Fori((first + head) // unit, (total - tail) // unit) as i:
        for s in range(unit):
            g = i * unit + s
            steps.base, steps.k = start + (g - first - head) * per, 0
            body(g, s)
            assert steps.k == per
    steps.base, steps.k = start + (total - tail - first - head) * per, 0
    for g in range(total - tail, total):
        body(g)


def uses(g, s, each):
    return g * (each // 2) + (each - s * (each // 2))


def build(nc, a, out):
    f32, f32r, bf16, i32, u32 = mybir.dt.float32, mybir.dt.float32r, mybir.dt.bfloat16, mybir.dt.int32, mybir.dt.uint32
    ALU, ACT, AX = mybir.AluOpType, mybir.ActivationFunctionType, mybir.AxisListType.X
    ctx = ExitStack()
    with ctx:
        def sb(name, shape, dt=f32):
            return ctx.enter_context(nc.sbuf_tensor(name, shape, dt))

        def sem(name):
            return ctx.enter_context(nc.semaphore(name))

        place = {}

        def area(name, shape):
            place[name] = -(-nc.sbuf_base // 32) * 32
            return sb(name, shape)

        def dram(name, rows, cols):
            return nc.dram_tensor(name, (rows, cols), f32, kind="Internal").ap()

        edge_sum = [dram(f"edge_sum{k}", NODES + P, DC) for k in range(K)]
        node_sum = [dram(f"node_sum{k}", NODES + P, D) for k in range(K)]
        hid_x = nc.dram_tensor("hid_x", (G, 128, 4 * N), f32, kind="Internal").ap()
        h_rows = dram("h_rows", NODES, D)
        ends_kept = dram("ends_kept", P, 3 * ET)
        x3_rows = dram("x3_rows", NODES, XW)
        x_area = area("x", [128, T * D])
        x = x_area[0:P, :].rearrange("p (t d) -> p t d", t=T)
        big = area("big", [128, T * D])
        mid = area("mid", [128, 10240])
        hT = area("hT", [128, 2, 8, N])
        xg = sb("xg", [P, 2, GT, D])
        inv = sb("inv", [P, 2, GT])
        xh = sb("xh", [P, 2, GT, D])
        xTg = area("xTg", [128, 2, 2, N])
        yb = sb("yb", [P, 2, GT, D])
        wk_area = sb("wk", [P, 2 * GT * D])
        wk = wk_area[:, :].rearrange("p (s t d) -> p s t d", s=2, t=GT)
        ends = area("ends", [128, 2 * 8 * N])
        KEPT = 3 * ET
        src_f, dst_f = ends[0:P, 0:ET], ends[0:P, ET:2 * ET]
        not_dst = ends[0:P, 2 * ET:KEPT]
        aT = ends[0:DE, KEPT:KEPT + 2 * N].rearrange("p (s n) -> p s n", s=2)
        ag = ends[0:P, KEPT + 2 * N:KEPT + 2 * N + 2 * GT * DE].rearrange("p (s t d) -> p s t d", s=2, t=GT)
        idx_a = sb("idx_a", [P, 2, EB], u32)
        idx_b = sb("idx_b", [P, 2, EB], u32)
        ident = sb("ident", [128, 128])
        before = sb("before", [P, P])
        ones = sb("ones", [P, P])
        lo_iota = sb("lo_iota", [P, 2 * P])
        hi_iota = sb("hi_iota", [P, T])
        e_iota = sb("e_iota", [P, E])
        n_iota = sb("n_iota", [P, T])
        spare = sb("spare", [P, 1])
        not_first = sb("not_first", [P, P])
        dup = sb("dup", [P, 2, EB])
        firsts = sb("firsts", [P, 2, EB])
        windows = sb("windows", [1, 2 * B])
        words = sb("words", [1, B], i32)
        met = sb("met", [P, 1])
        in_order = sb("in_order", [1, 1], i32)
        away = sb("away", [P, 2, EB])
        iota_i = sb("iota_i", [P, 2 * P], i32)
        neg_half = sb("neg_half", [P, T])
        stat = sb("stat", [P, 2, GT, 6])
        mv = sb("mv", [P, 2, GT, 2])
        var = sb("var", [P, 2, GT])
        rstd = sb("rstd", [P, 2, GT])
        stat2 = sb("stat2", [P, 2, GT, 6])
        mv2 = sb("mv2", [P, 2, GT, 2])
        var2 = sb("var2", [P, 2, GT])
        rstd2 = sb("rstd2", [P, 2, GT])
        stat5 = sb("stat5", [P, 5, 6])
        mv5 = sb("mv5", [P, 5, 2])
        mv1 = sb("mv1", [P, T, 2])
        rstd1 = sb("rstd1", [P, T])
        cnt = sb("cnt", [P, T])
        deg = sb("deg", [P, T])
        has = sb("has", [P, T])
        dis = sb("dis", [P, T])
        biasA = sb("biasA", [128, 4])
        b1A = sb("b1A", [128, 4])
        u0 = sb("u0", [DG, 1])
        b2A = sb("b2A", [P, D])
        msum = sb("msum", [128, 2, G])
        mean = sb("mean", [128, 2])
        wr = sb("wr", [128, 2, E])
        rt = sb("rt", [1, 16, E])
        rt_id = sb("rt_id", [1, E], u32)
        wcol = sb("wcol", [128, 2])
        bB1 = sb("bB1", [128, 8])
        b2B = b2A
        gamma = sb("gamma", [P, D])
        beta = sb("beta", [P, D])
        wG = sb("wG", [128, 2, D])
        gw = sb("gw", [128, 2, E])
        gb = sb("gb", [P, E])
        b1E = sb("b1E", [128, 2, 8])
        b2E = sb("b2E", [P, 2, D])
        ps = ctx.enter_context(nc.psum_tensor("ps", [128, 8, 512], f32))

        def cut(area, rows, at, size):
            return area[0:rows, at:at + size], at + size

        rowb, o = cut(big, P, 0, 2 * EB * P)
        S, o = cut(big, P, o, 2 * EB * P)
        SL, o = cut(big, P, o, EB * P)
        va, o = cut(big, P, o, 2 * EB * DC)
        ma, o = cut(big, P, o, 2 * EB * DC)
        oh, o = cut(big, P, o, 2 * EB * (P + T))
        SL = SL.rearrange("p (t q) -> p t q", t=EB)
        rowb = rowb.bitcast(i32).rearrange("p (s t q) -> p s t q", s=2, t=EB)
        S = S.rearrange("p (s t q) -> p s t q", s=2, t=EB)
        va = va.rearrange("p (s t d) -> p s t d", s=2, t=EB)
        ma = ma.rearrange("p (s t d) -> p s t d", s=2, t=EB)
        oh = oh.bitcast(bf16)
        ohl = oh[:, 0:4 * EB * P].rearrange("p (s t q) -> p s t q", s=2, t=2 * EB)
        ohh = oh[:, 4 * EB * P:4 * EB * (P + T)].rearrange("p (s t q) -> p s t q", s=2, t=2 * EB)
        hi, lo = mid[0:P, 0:ET], mid[0:P, ET:2 * ET]
        hl_i = mid[0:P, 2 * ET:3 * ET].bitcast(i32)
        hl_w = mid[0:P, 3 * ET:4 * ET]
        raw_i = mid[0:100, 4 * ET:4 * ET + 2000].bitcast(i32).rearrange("t (k c p) -> t k c p", k=2, c=8)
        raw_f = hT[0:100, 1, :, :].rearrange("t c n -> t (c n)").rearrange("t (k c p) -> t k c p", k=2, c=8)
        hits = [mid[0:P, (2 + k) * ET:(3 + k) * ET] for k in range(2)]
        agg = mid[0:P, 0:T * DC].rearrange("p (t d) -> p t d", t=T)
        CN = GT * max(b - a for a, b in zip(CHUNKS, CHUNKS[1:]))
        part = [area_[0:P, at:at + (K - 1) * CN * DC].rearrange("p (k t d) -> p k t d", k=K - 1, t=CN)
                for area_, at in ((mid, T * DC), (big, (CHUNKS[-2] - 6) * N), (big, NODES + (CHUNKS[-2] - 6) * N))]
        wA1e = mid[0:DE, 5850:5850 + HID0]
        wA2 = mid[:, 6362:6362 + 4 * D].rearrange("p (c d) -> p c d", c=4)
        hx = mid[:, 7386:7386 + 2 * 4 * N].rearrange("p (s m n) -> p s m n", s=2, m=4)
        wA1x = mid[:, 7386:7386 + 2 * HID0].rearrange("p (c f) -> p c f", c=2)
        wU = mid[:, 8410:8410 + HID0]
        def over(name, area, at, shape):
            return nc.alloc_sbuf_tensor_at(name, shape, f32r, offset=place[area] + 4 * at)

        xnT = big[:, 0:2 * NODES].rearrange("p (c n) -> p c n", c=2)
        wB1 = mid[:, 0:2 * 2 * HID1].rearrange("p (c f) -> p c f", c=2)
        wB2 = mid[:, 2048:2048 + 8 * D].rearrange("p (c d) -> p c d", c=8)
        wB1_lo = over("wB1_lo", "mid", 0, [128, 2, 2 * HID1])
        wB2_lo = over("wB2_lo", "mid", 2048, [128, 8, D])
        wB1_hi = over("wB1_hi", "mid", 4096, [128, 2, 2 * HID1])
        wB2_hi = over("wB2_hi", "mid", 6144, [128, 8, D])
        xB_hi = over("xB_hi", "mid", 8192, [128, 2, 2, N])
        xB_lo = over("xB_lo", "mid", 9192 + 24, [128, 2, 2, N])
        h0_whole = ends[:, 0:2 * 8 * N].rearrange("p (s m n) -> p s m n", s=2, m=8)
        h0_lo = over("h0_lo", "ends", 0, [128, 2, 8, N])
        h_hi = over("h_hi", "hT", 0, [128, 2, 8, N])
        wrow = wk[0:1, 0].rearrange("a t d -> a (t d)")[:, 0:2 * P].rearrange("a (k p) -> a k p", k=2)
        b2rows = wk[0:1, 1]
        hb = xg
        mg = mid[0:P, 0:2 * EB * D].rearrange("p (s t d) -> p s t d", s=2, t=EB)
        ms = mid[0:P, 2 * EB * D:4 * EB * D].rearrange("p (s t d) -> p s t d", s=2, t=EB)
        acc = big[0:P, 0:T * D].rearrange("p (t d) -> p t d", t=T)
        onto = mid[0:P, 5120:5120 + 2 * EB * 2 * P].rearrange("p (s t q) -> p s t q", s=2, t=EB)
        tab = mid[0:P, 0:2 * K * GT * D].rearrange("p (s k t d) -> p s k t d", s=2, k=K, t=GT)
        stage = mid[0:P, 0:2 * GT * XW].rearrange("p (s t d) -> p s t d", s=2, t=GT)
        lo_hot, o = cut(big, P, 0, 2 * EB * P)
        hi_hot, o = cut(big, P, o, 2 * EB * E * ST)
        lo_hot = lo_hot.rearrange("p (s t q) -> p s t q", s=2, t=EB)
        hi_hot = hi_hot.rearrange("p (s t q) -> p s t q", s=2, t=EB)
        slot_token, slot_none, slot_from, slot_to = (wk_area[0:P, k * E * ST:(k + 1) * E * ST] for k in range(4))
        slot_from, slot_to = slot_from.bitcast(u32), slot_to.bitcast(u32)
        gate = mid[0:P, 5120:5120 + 12 * T * E].rearrange("p (k q) -> p k q", k=12)
        gate3 = gate.rearrange("p k (t e) -> p k t e", t=T)
        g50 = xg[:, :, :, :].rearrange("p s t d -> p (s t d)")[:, 0:16 * T].rearrange("p (k t) -> p k t", k=16)
        prob = g50[:, 13, :]
        tile_end = g50[:, 14, 0:E]
        from_idx = idx_a[:, :, 0:ST]
        out_idx = idx_b[:, :, 0:ST]
        XE = -(-2 * ST * XW // 8) * 8
        xe = big[0:P, 0:2 * ST * XW].rearrange("p (s t d) -> p s t d", s=2, t=ST)
        w1E = mid[:, 0:2 * 2 * HID2].rearrange("p (s c f) -> p s c f", s=2, c=2)
        w2E = mid[:, 4096:4096 + 2 * 8 * D].rearrange("p (s c d) -> p s c d", s=2, c=8)
        h_lo = over("h_lo", "x", 0, [128, 2, 8, N])
        xT_lo = over("xT_lo", "x", 4000, [128, 2, 2, N])
        h_whole = x_area[:, 5000:5000 + 8 * N].rearrange("p (m n) -> p m n", m=8)
        w1_hi = [over("w1_hi0", "x", 7000, [128, 2, HID2]), over("w1_hi1", "big", XE, [128, 2, HID2])]
        w2_hi = [over("w2_hi0", "x", 7000 + 2 * HID2, [128, 8, D]), over("w2_hi1", "big", XE + 2 * HID2, [128, 8, D])]
        w1_lo = over("w1_lo", "mid", 0, [128, 2, 2, HID2])
        w2_lo = over("w2_lo", "mid", 4096, [128, 2, 8, D])
        xT_hi = over("xT_hi", "xTg", 0, [128, 2, 2, N])
        nanw = mid[0:P, 8192:8192 + 4 * GT * D].rearrange("p (k t d) -> p k t d", k=4, t=GT)

        x_in = a["x"].rearrange("(t p) d -> p t d", p=P)
        out_v = out.rearrange("(t p) d -> p t d", p=P)
        attr = a["edge_attr_64"].rearrange("(t p) d -> p t d", p=P)
        h_v = h_rows.rearrange("(t p) d -> p t d", p=P)
        ns_v = [t[0:NODES, :].rearrange("(t p) d -> p t d", p=P) for t in node_sum]
        es_v = [t[0:NODES, :].rearrange("(t p) d -> p t d", p=P) for t in edge_sum]
        x3_v = x3_rows.rearrange("(t p) d -> p t d", p=P)

        s_dve, s_pool = sem("dve_steps"), sem("pool_steps")
        s_raw, s_x, s_wA, s_cst, s_wB, s_b2r = sem("raw_ends_in"), sem("x_in"), sem("wA_in"), sem("small_in"), sem("wB_in"), sem("b2rows_in")
        s_zero, s_ztab = sem("zeros_set"), sem("tables_zeroed")
        s_const = sem("constants_set")
        s_rawf, s_rawT = sem("ends_as_float"), sem("ends_transposed")
        s_row, s_va = [sem(f"edge_rows_in{i}") for i in range(2)], [sem(f"edge_attr_in{i}") for i in range(2)]
        s_esel, s_emm, s_ecp = sem("edge_select_set"), sem("edge_sums_in_psum"), sem("edge_sums_in_sbuf")
        s_tab = [sem(f"edge_scattered{k}") for k in range(K)]
        s_deg, s_dis = sem("degrees_set"), sem("dis_set")
        s_part, s_added, s_means = [sem(f"edge_tables_in{i}") for i in range(3)], sem("edge_tables_added"), sem("groups_added")
        s_hx, s_hxw, s_hxin = sem("x_hidden_in_sbuf"), sem("x_hidden_written"), [sem(f"x_hidden_back{i}") for i in range(2)]
        s_a0, s_aT, s_aTe = sem("edge_means_set"), sem("edge_means_T_in_psum"), sem("edge_means_T_in_sbuf")
        s_h1, s_hadd, s_h1e = sem("edge_hidden_in_psum"), sem("hidden_added"), sem("hidden_in_sbuf")
        s_bA, s_bAset = sem("u_term_in_psum"), sem("biasA_set")
        s_v0, s_r0, s_x0 = sem("ln0_var"), sem("ln0_rstd"), sem("ln0_rows")
        s_t0, s_t0e, s_h0 = sem("ln0_T_in_psum"), sem("ln0_T_in_sbuf"), sem("x_hidden_in_psum")
        s_o0, s_o0e = sem("mlp_out_in_psum"), sem("mlp_out_read")
        s_v1, s_r1, s_x1, s_t1, s_t1e = sem("ln1_var"), sem("ln1_rstd"), sem("ln1_rows"), sem("ln1_T_in_psum"), sem("ln1_T_in_sbuf")
        s_mean, s_lg, s_e1, s_e1x, s_e2x, s_rid = sem("mean_set"), sem("logits_in_psum"), sem("router_args"), sem("router_exp"), sem("router_rows"), sem("router_ids")
        s_wb, s_wbc, s_wBhi, s_wBlo = sem("router_w_in_psum"), sem("router_w_set"), sem("wB_hi"), sem("wB_lo")
        s_kept, s_back, s_xhi, s_xlo, s_hBhi, s_hBlo = sem("ends_kept"), sem("ends_back"), sem("xn_hi"), sem("xn_lo"), sem("ffn0_hidden_hi"), sem("ffn0_hidden_lo")
        s_hB, s_hBe, s_oB, s_oBe = sem("ffn0_hidden_in_psum"), sem("ffn0_hidden_in_sbuf"), sem("ffn0_out_in_psum"), sem("ffn0_out_read")
        s_vB, s_rB = sem("lnB_var"), sem("lnB_rstd")
        s_v2, s_r2, s_x2, s_t2, s_t2e = sem("ln2_var"), sem("ln2_rstd"), sem("ln2_rows"), sem("ln2_T_in_psum"), sem("ln2_T_in_sbuf")
        s_hm, s_hrow, s_hw = sem("h_in_psum"), sem("h_in_sbuf"), [sem(f"h_written{i}") for i in range(2)]
        s_dsel, s_mmm, s_mcp = sem("msg_select_set"), sem("msg_sums_in_psum"), sem("msg_sums_in_sbuf")
        s_sch, s_schp, s_sched = sem("schedule_args"), sem("schedule_products"), sem("schedule_set")
        s_onto, s_offs, s_gk, s_pair, s_acc, s_accz = sem("window_select_set"), sem("window_offsets_set"), [sem(f"half_block_gathered{i}") for i in range(4)], sem("window_sums_in_psum"), sem("window_sums_added"), sem("window_sums_zeroed")
        s_idx = sem("step_indices_set")
        s_dvf, s_fz, s_fzd, s_fs = sem("dve_steps_unsorted"), sem("unsorted_zeros_set"), sem("node_tables_zeroed"), sem("node_tables_summed")
        s_drow = [sem(f"dst_rows_in{i}") for i in range(2)]
        s_mt = [sem(f"msg_scattered{k}") for k in range(K)]
        s_nt = [sem(f"node_tables_in{i}") for i in range(2)]
        s_v3, s_r3, s_x3, s_x3c, s_t3, s_t3e, s_l3, s_l3e = sem("ln3_var"), sem("ln3_rstd"), sem("ln3_rows"), sem("ln3_rows_kept"), sem("ln3_T_in_psum"), sem("ln3_T_in_sbuf"), sem("gate_in_psum"), sem("gate_in_sbuf")
        s_ga1, s_gexp, s_goh, s_grk, s_slots = sem("gate_args"), sem("gate_exp"), sem("gate_onehot"), sem("gate_ranks"), sem("slots_set")
        s_rows, s_prob = [sem(f"x3_rows_written{i}") for i in range(2)], sem("probabilities_written")
        s_pset, s_hot, s_inv, s_from = sem("probabilities_set"), sem("slot_onehots_set"), sem("slots_tokens_in_psum"), sem("slot_indices_set")
        s_xe, s_wE = [sem(f"slot_rows_in{i}") for i in range(2)], [sem(f"wE_in{i}") for i in range(2)]
        s_t5, s_t5hi, s_t5lo = sem("slots_T_in_psum"), sem("slots_T_hi"), sem("slots_T_lo")
        s_whi, s_wlo, s_h5, s_h5e, s_hhi, s_hlo = sem("wE_hi"), sem("wE_lo"), sem("ffn1_hidden_in_psum"), sem("ffn1_hidden_in_sbuf"), sem("ffn1_hidden_hi"), sem("ffn1_hidden_lo")
        s_o5, s_o5e = sem("ffn1_out_in_psum"), sem("ffn1_out_read")
        s_xn, s_y5, s_base, s_sc = sem("slot_rows_normalised"), sem("results_set"), sem("x3_written"), [sem(f"results_scattered{i}") for i in range(2)]

        QN = E * ST // GT
        QE = ST // GT
        HALF = (2, 3, 6, 7)
        HALF0 = (2, 3, 6, 1)

        def of_expert(e, es, j):
            return (e, es, j) if j < QE else (e + 1, 1 - es, j - QE)

        def weight_piece(k, w1_, w2_):
            return w1_[:, k, :] if k < 2 else w2_[:, 4 * (k - 2):4 * (k - 1), :]

        block = ctx.enter_context(nc.Block())

        @block.sync
        def _(sp):
            steps = Steps()
            sp.dma_start(raw_i[:, 0], a["src"].rearrange("(c t p) -> t c p", c=8, p=P)).then_inc(s_raw, 16)
            sp.dma_start(raw_i[:, 1], a["dst"].rearrange("(c t p) -> t c p", c=8, p=P)).then_inc(s_raw, 16)

            def load_block(b, s=None):
                s = b % 2 if s is None else s
                if not (isinstance(b, int) and b < 2):
                    sp.wait_ge(s_emm, b - 1)
                sp.dma_start(rowb[:, s], a["src"][bass.ds(b * (EB * P), EB * P)].partition_broadcast(P)
                             .rearrange("p (t q) -> p t q", t=EB)).then_inc(s_row[s], 16)
                sp.dma_start(va[:, s, :, 0:DE], attr[:, bass.ds(b * EB, EB), :]).then_inc(s_va[s], 16)

            in_turns(sp, steps, load_block, AHEAD - 4, 2, 0, 2)
            sp.wait_ge(s_sched, 1)
            w1 = a["L0_gnn_W1"]
            sp.dma_start(wA1x, w1[0:D, :].rearrange("(c p) f -> p c f", p=128)).then_inc(s_wA, 16)
            sp.dma_start(wU, w1[D + DE:D + DE + DG, :]).then_inc(s_wA, 16)
            sp.dma_start(wA1e, w1[D:D + DE, :]).then_inc(s_wA, 16)
            sp.dma_start(wA2, a["L0_gnn_W2"].rearrange("(c p) d -> p c d", p=128)).then_inc(s_wA, 16)
            in_turns(sp, steps, load_block, B, 0, 0, 2, first=AHEAD - 4)

            def load_chunk(c):
                n = slice(CHUNKS[c] * GT, CHUNKS[c + 1] * GT)
                if c >= 3:
                    sp.wait_ge(s_added, (c - 2) * (K - 1))
                for k in range(K):
                    sp.dma_start(part[c % 3][:, k - 1, 0:n.stop - n.start] if k else agg[:, n, :], es_v[k][:, n, :]).then_inc(s_part[c % 3], 16)

            def load_hidden(g, s=None):
                s = g % 2 if s is None else s
                if not (isinstance(g, int) and g < 2):
                    sp.wait_ge(s_h1e, g * 2 - 2)
                sp.dma_start(hx[:, s], hid_x[bass.ds(g, 1)].rearrange("a p (m n) -> p (a m) n", m=4)).then_inc(s_hxin[s], 16)

            for k in range(K):
                sp.wait_ge(s_tab[k], 16 * EB // K * B)
            load_chunk(0)
            sp.wait_ge(s_hxw, 16 * G)
            load_hidden(0)
            load_chunk(1)
            load_hidden(1)
            load_hidden(2)
            load_chunk(2)
            for c in range(3, len(CHUNKS) - 1):
                for g in range(max(CHUNKS[c - 1] - 6, 3), CHUNKS[c] - 6):
                    load_hidden(g)
                load_chunk(c)
            sp.dma_start(ends_kept, ends[0:P, 0:KEPT]).then_inc(s_kept, 16)
            in_turns(sp, steps, load_hidden, G, 0, 3, 2, first=CHUNKS[-2] - 6)
            sp.wait_ge(s_kept, 16)
            sp.wait_ge(s_rid, 1)
            for k in range(2):
                e = sp.value_load(rt_id[0:1, k:k + 1], min_val=0, max_val=E - 1)
                sp.dma_start(wB1[:, :, k * HID1:(k + 1) * HID1],
                             a["L0_ffn_W1"][bass.ds(e, 1)].rearrange("a (c p) f -> p (a c) f", p=128)).then_inc(s_wB, 16)
                sp.dma_start(wB2[:, 4 * k:4 * k + 4, :],
                             a["L0_ffn_W2"][bass.ds(e, 1)].rearrange("a (c p) d -> p (a c) d", p=128)).then_inc(s_wB, 16)
                with nc.allow_non_contiguous_dma(reason="a bias as a column"):
                    sp.dma_start(bB1[:, 4 * k:4 * k + 4],
                                 a["L0_ffn_b1"][bass.ds(e, 1)].rearrange("a (c p) -> p (a c)", p=128)).then_inc(s_wB, 16)
                sp.dma_start(b2rows[:, k, :], a["L0_ffn_b2"][bass.ds(e, 1)]).then_inc(s_b2r, 16)

            def store_h(g, s=None):
                s = g % 2 if s is None else s
                if isinstance(g, int) and g == G - 2:
                    sp.wait_ge(s_oB, G)
                    sp.dma_start(ends[0:P, 0:KEPT], ends_kept).then_inc(s_back, 16)
                sp.wait_ge(s_hrow, g + 1)
                sp.dma_start(h_v[:, bass.ds(g * GT, GT), :], hb[:, s]).then_inc(s_hw[s], 16)

            in_turns(sp, steps, store_h, G, 2, 3, 2)

            def load_dst(b, s=None):
                s = b % 2 if s is None else s
                if isinstance(b, int) and b < 2:
                    sp.wait_ge(s_t2, G)
                else:
                    sp.wait_ge(s_dsel, b - 1)
                sp.dma_start(rowb[:, s], a["dst"][bass.ds(b * (EB * P), EB * P)].partition_broadcast(P)
                             .rearrange("p (t q) -> p t q", t=EB)).then_inc(s_drow[s], 16)

            def load_tables(g, s=None):
                s = g % 2 if s is None else s
                if not (isinstance(g, int) and g < 2):
                    sp.wait_ge(s_fs, g - 1)
                for k in range(K):
                    sp.dma_start(tab[:, s, k], ns_v[k][:, bass.ds(g * GT, GT), :]).then_inc(s_nt[s], 16)

            with sp.If_eq(sp.to_reg(sp.value_load(in_order[0:1, 0:1], min_val=0, max_val=1)), 0):
                in_turns(sp, steps, load_dst, B, 2, 2, 2)
                for k in range(K):
                    sp.wait_ge(s_mt[k], 16 * EB // K * B)
                in_turns(sp, steps, load_tables, G, 2, 3, 2)

            def store_x3(g, s=None):
                s = g % 2 if s is None else s
                n = bass.ds(g * GT, GT)
                sp.wait_ge(s_v3, g + 1)
                sp.dma_start(out_v[:, n, :], x[:, n, :]).then_inc(s_base, 16)
                sp.wait_ge(s_x3c, g + 1)
                sp.dma_start(x3_v[:, n, 0:PROB], stage[:, s, :, 0:PROB]).then_inc(s_rows[s], 16)

            in_turns(sp, steps, store_x3, G, 2, 3, 2)
            sp.wait_ge(s_pset, 1)
            with nc.allow_non_contiguous_dma(reason="a column of the experts' rows"):
                sp.dma_start(x3_v[:, :, PROB:XW], prob.unsqueeze(2)).then_inc(s_prob, 16)

            def load_expert(e, s=None):
                s = e % 2 if s is None else s
                if isinstance(e, int) and e < 2:
                    if e == 0:
                        for i in range(2):
                            sp.wait_ge(s_rows[i], 16 * ((G + 1 - i) // 2))
                        sp.wait_ge(s_slots, 1)
                else:
                    sp.wait_ge(s_y5, (e - 1) * QE)
                sp.dma_start(w1E[:, s], a["L1_ffn_w1"][bass.ds(e, 1)].rearrange("a (c p) f -> p (a c) f", p=128)).then_inc(s_wE[s], 16)
                sp.dma_start(w2E[:, s], a["L1_ffn_w2"][bass.ds(e, 1)].rearrange("a (c p) d -> p (a c) d", p=128)).then_inc(s_wE[s], 16)
                with nc.allow_non_contiguous_dma(reason="a bias as a column"):
                    sp.dma_start(b1E[:, s], a["L1_ffn_b1"][bass.ds(e, 1)].rearrange("a (c p) -> p (a c)", p=128)).then_inc(s_wE[s], 16)
                sp.dma_start(b2E[:, s], a["L1_ffn_b2"][bass.ds(e, 1)].rearrange("a d -> (a d)").partition_broadcast(P)).then_inc(s_wE[s], 16)

            in_turns(sp, steps, load_expert, E, 2, 2, 2)
            for s in range(2):
                sp.wait_ge(s_sc[s], 16 * GT * QN // 2)
            sp.wait_ge(s_base, 16 * G)

        @block.scalar
        def _(act):
            steps = Steps()
            act.wait_ge(s_zero, 1)
            z = hT[0:P, 0, :, :].rearrange("p m n -> p (m n)")
            for k in range(K):
                for c in range(3):
                    act.dma_start(edge_sum[k].rearrange("(p t) d -> p (t d)", p=P)[:, c * 1105:(c + 1) * 1105], z[:, 0:1105]).then_inc(s_ztab, 16)
            def row(name):
                return a[name].partition_broadcast(P)
            with nc.allow_non_contiguous_dma(reason="biases and u[0] as columns"):
                act.dma_start(b1A[:, :], a["L0_gnn_b1"].rearrange("(c p) -> p c", p=128)).then_inc(s_cst, 16)
                act.dma_start(u0[:, :], a["L0_gnn_u"][0:1, :].rearrange("a p -> p a")).then_inc(s_cst, 16)
            act.dma_start(b2A[:, :], row("L0_gnn_b2")).then_inc(s_cst, 16)
            act.dma_start(wr[:, :, :], a["L0_ffn_Wr"].rearrange("(c p) e -> p c e", p=128)).then_inc(s_cst, 16)
            act.dma_start(rt[:, 0, :], a["L0_ffn_br"].rearrange("(a e) -> a e", a=1)).then_inc(s_cst, 16)
            act.dma_start(gamma[:, :], row("L0_ffn_gamma")).then_inc(s_cst, 16)
            act.dma_start(beta[:, :], row("L0_ffn_beta")).then_inc(s_cst, 16)
            act.dma_start(wG[:, :, :], a["L1_gnn_W"].rearrange("(c p) e -> p c e", p=128)).then_inc(s_cst, 16)
            act.dma_start(gw[:, :, :], a["L1_ffn_gate_w"].rearrange("(c p) e -> p c e", p=128)).then_inc(s_cst, 16)
            act.dma_start(gb[:, :], row("L1_ffn_gate_b")).then_inc(s_cst, 16)

            def edge_copy(b, s=None, tiles=0):
                s = b % 2 if s is None else s
                act.wait_ge(s_emm, b + 1)
                if not (isinstance(b, int) and b < 2):
                    for k in range(K):
                        act.wait_ge(s_tab[k], 16 * EB // K * (b - 1))
                act.activation(ma[:, s].rearrange("p (h t) d -> p h (t d)", h=2),
                               ps[0:P, 2 + 2 * s:4 + 2 * s, 0:EB // 2 * DC], ACT.Copy)
                act.activation(idx_a[:, s, :], firsts[:, s], ACT.Copy).then_inc(s_ecp, 1)
                if tiles:
                    n = bass.ds(b * 2 if tiles == 2 else b + XB, tiles)
                    act.dma_start(x[:, n, :], x_in[:, n, :]).then_inc(s_x, 16)

            in_turns(act, steps, lambda b, s=None: edge_copy(b, s, tiles=2), XB, 2, 0, 2)
            in_turns(act, steps, lambda b, s=None: edge_copy(b, s, tiles=1), T - XB, 0, 0, 2, first=XB)
            in_turns(act, steps, edge_copy, AHEAD, 0, 0, 2, first=T - XB)

            act.wait_ge(s_bA, 1)
            act.wait_ge(s_cst, 160)
            for m in range(4):
                i_ = act.activation(biasA[:, m:m + 1], ps[:, 7, m:m + 1], ACT.Identity, bias=b1A[:, m:m + 1])
            i_.then_inc(s_bAset, 1)
            act.wait_ge(s_bAset, 1)
            act.wait_ge(s_ztab, 16 * 3 * K)

            def T0_copy(g, s):
                act.wait_ge(s_t0, g + 1)
                act.activation(xTg[:, s], ps[:, s, 0:2 * N].rearrange("p (c n) -> p c n", c=2), ACT.Copy).then_inc(s_t0e, 1)

            def hidden_x(g, s):
                if not (isinstance(g, int) and g == 0):
                    act.wait_ge(s_hxw, g * 16)
                for m in range(4):
                    act.wait_ge(s_h0, g * 4 + (m + 1))
                    act.activation(hT[:, s, m, :], ps[:, 6 + m % 2, 0:N], ACT.Identity, bias=biasA[:, m:m + 1]).then_inc(s_hx, 1)
                act.wait_ge(s_hx, g * 4 + 4)
                act.dma_start(hid_x[bass.ds(g, 1)].rearrange("a p (m n) -> p (a m) n", m=4), hT[:, s, 0:4, :]).then_inc(s_hxw, 16)

            def ahead(g, s=None):
                s = g % 2 if s is None else s
                edge_copy(g + AHEAD, s)
                T0_copy(g, s)
                if not (isinstance(g, int) and g == 0):
                    hidden_x(g - 1, 1 - s)

            in_turns(act, steps, ahead, G, 2, 1, 2)
            edge_copy(B - 1)
            hidden_x(G - 1, (G - 1) % 2)
            act.wait_ge(s_hxw, 16 * G)

            def aT_copy(g, s):
                act.wait_ge(s_aT, g + 1)
                act.activation(aT[:, s], ps[0:DE, 6, s * N:(s + 1) * N], ACT.Copy).then_inc(s_aTe, 1)

            def hidden(g, s):
                if not (isinstance(g, int) and g < 2):
                    act.wait_ge(s_o0, g - 1)
                for j in range(2):
                    act.wait_ge(s_hadd, g * 2 + (j + 1))
                    act.activation(hT[:, s, 2 * j:2 * j + 2, :], hx[:, s, 2 * j:2 * j + 2, :], ACT.Relu).then_inc(s_h1e, 1)

            def T1_copy(g, s):
                act.wait_ge(s_t1, g + 1)
                for c in range(2):
                    i_ = act.activation(xnT[:, c, bass.ds(g * N, N)], ps[:, 7, c * N:(c + 1) * N], ACT.Copy,
                                        accum_out=msum[:, c, bass.ds(g, 1)])
                i_.then_inc(s_t1e, 1)

            def mlp(g, s=None):
                fixed = isinstance(g, int)
                s = g % 2 if s is None else s
                if not (fixed and g == G - 1):
                    hidden(g + 1, 1 - s)
                if not (fixed and g >= G - 2):
                    aT_copy(g + 2, s)
                if not (fixed and g == 0):
                    T1_copy(g - 1, 1 - s)

            aT_copy(0, 0)
            aT_copy(1, 1)
            hidden(0, 0)
            in_turns(act, steps, mlp, G, 2, 3, 2)
            T1_copy(G - 1, (G - 1) % 2)

            act.wait_ge(s_e1, 1)
            act.activation(rt[:, 2, :], rt[:, 1, :], ACT.Exp, accum_out=rt[:, 9, 0:1]).then_inc(s_e1x, 1)
            act.wait_ge(s_e1, 2)
            act.activation(rt[:, 5, :], rt[:, 4, :], ACT.Exp, accum_out=rt[:, 9, 2:3]).then_inc(s_e1x, 1)
            act.wait_ge(s_e1, 3)
            act.activation(rt[:, 11, 0:2], rt[:, 10, 0:2], ACT.Exp, accum_out=rt[:, 9, 4:5]).then_inc(s_e1x, 1)

            act.wait_ge(s_wbc, 1)
            act.wait_ge(s_wB, 96)
            def x_hi(g, s):
                if not (isinstance(g, int) and g < 2):
                    act.wait_ge(s_hB, g * 4 - 4)
                act.activation(xB_hi[:, s], xnT[:, :, bass.ds(g * N, N)], ACT.Copy).then_inc(s_xhi, 1)

            def T2_copy(g, s):
                act.wait_ge(s_t2, g + 1)
                act.activation(xTg[:, s], ps[:, 0, 0:2 * N].rearrange("p (c n) -> p c n", c=2), ACT.Copy).then_inc(s_t2e, 1)

            def h_copy(g, s):
                act.wait_ge(s_hm, g + 1)
                if not (isinstance(g, int) and g < 2):
                    act.wait_ge(s_hw[s], uses(g, s, 16) - 16)
                for t in range(GT):
                    i_ = act.activation(hb[:, s, t, :], ps[0:P, 7, t * D:(t + 1) * D], ACT.Copy, scale=dis[:, bass.ds(g * GT + t, 1)])
                i_.then_inc(s_hrow, 1)

            def hidden0(g, s):
                def hi(i):
                    act.wait_ge(s_hBe, g * 4 + (i + 1))
                    act.activation(h_hi[:, s, 2 * i:2 * i + 2, :], h0_whole[:, s, 2 * i:2 * i + 2, :], ACT.Copy).then_inc(s_hBhi, 1)

                if not (isinstance(g, int) and g < 2):
                    act.wait_ge(s_oB, g - 1)
                for i in range(4):
                    act.wait_ge(s_hB, g * 4 + (i + 1))
                    for m in (2 * i, 2 * i + 1):
                        i_ = act.activation(h0_whole[:, s, m, :], ps[:, HALF0[i], m % 2 * N:(m % 2 + 1) * N], ACT.Gelu, bias=bB1[:, m:m + 1])
                    i_.then_inc(s_hBe, 1)
                    if i:
                        hi(i - 1)
                hi(3)

            def ffn0(g, s=None):
                fixed = isinstance(g, int)
                s = g % 2 if s is None else s
                if not (fixed and g < 2):
                    T2_copy(g - 2, s)
                if not (fixed and g == G - 1):
                    hidden0(g + 1, 1 - s)
                if not (fixed and g >= G - 3):
                    x_hi(g + 3, 1 - s)
                if not (fixed and g < 2):
                    h_copy(g - 2, s)

            for k in range(2):
                h = slice(k * HID1, (k + 1) * HID1)
                act.activation(wB1_hi[:, :, h], wB1[:, :, h], ACT.Copy).then_inc(s_wBhi, 1)
            x_hi(0, 0)
            for k in range(2):
                h = slice(4 * k, 4 * k + 4)
                act.activation(wB2_hi[:, h, :], wB2[:, h, :], ACT.Copy, scale=wcol[:, k:k + 1]).then_inc(s_wBhi, 1)
            x_hi(1, 1)
            hidden0(0, 0)
            x_hi(2, 0)
            in_turns(act, steps, ffn0, G, 4, 3, 2)
            for g in (G - 2, G - 1):
                T2_copy(g, g % 2)
                h_copy(g, g % 2)

            def select_nodes(b, s=None):
                s = b % 2 if s is None else s
                if not (isinstance(b, int) and b < 2):
                    act.wait_ge(s_pair, b * 2 - 2)
                act.activation(idx_a[:, s, :], src_f[:, bass.ds(b * EB, EB)], ACT.Copy).then_inc(s_idx, 1)
                for i in range(EB):
                    i_ = act.activation(onto[:, s, i, :], lo_iota[:, :], ACT.Abs, bias=not_dst[:, bass.ds(b * EB + i, 1)])
                i_.then_inc(s_offs, 1)
                act.wait_ge(s_offs, b + 1)
                act.activation(onto[:, s], onto[:, s], ACT.Relu, bias=1.0, scale=-1.0).then_inc(s_onto, 1)

            def msg_copy(b, s=None):
                s = b % 2 if s is None else s
                act.wait_ge(s_mmm, b + 1)
                if not (isinstance(b, int) and b < 2):
                    for k in range(K):
                        act.wait_ge(s_mt[k], 16 * EB // K * (b - 1))
                act.activation(ms[:, s].rearrange("p (h t) d -> p h (t d)", h=5), ps[0:P, 0:5, :], ACT.Copy).then_inc(s_mcp, 1)

            act.wait_ge(s_sched, 1)
            act.wait_ge(s_back, 16)
            with act.If_eq(act.to_reg(act.value_load(in_order[0:1, 0:1], min_val=0, max_val=1)), 1):
                in_turns(act, steps, select_nodes, B, 2, 2, 2)
            with act.Else():
                act.wait_ge(s_fz, 1)
                for k in range(K):
                    for c in range(8):
                        act.dma_start(node_sum[k].rearrange("(p t) d -> p (t d)", p=P)[:, c * 1632:(c + 1) * 1632], z[:, 0:1632]).then_inc(s_fzd, 16)
                in_turns(act, steps, msg_copy, B, 2, 2, 2)
                act.wait_ge(s_fzd, 16 * 8 * K)

            def gate_copy(g, s=None):
                s = g % 2 if s is None else s
                act.wait_ge(s_r3, g + 1)
                n = bass.ds(g * GT, GT)
                if not (isinstance(g, int) and g < 2):
                    act.wait_ge(s_rows[s], uses(g, s, 16) - 16)
                act.activation(stage[:, s, :, 0:D], x[:, n, :], ACT.Copy)
                act.activation(stage[:, s, :, MEAN:MEAN + 1], mv[:, s, :, 0:1], ACT.Copy)
                act.activation(stage[:, s, :, RSTD:RSTD + 1], rstd[:, s, :].unsqueeze(2), ACT.Copy).then_inc(s_x3c, 1)
                act.wait_ge(s_t3, g + 1)
                act.activation(xTg[:, s], ps[:, s, 0:2 * N].rearrange("p (c n) -> p c n", c=2), ACT.Copy).then_inc(s_t3e, 1)

            in_turns(act, steps, gate_copy, G, 4, 3, 2)
            act.wait_ge(s_ga1, 1)
            act.activation(gate[:, 1, :], gate[:, 1, :], ACT.Exp).then_inc(s_gexp, 1)

            def split_weights(e, es, k):
                act.activation(weight_piece(k, w1_hi[es], w2_hi[es]), weight_piece(k, w1E[:, es], w2E[:, es]), ACT.Copy).then_inc(s_whi, 1)

            def T5_hi(q, s):
                act.wait_ge(s_t5, q + 1)
                act.activation(xT_hi[:, s], ps[:, s, 0:2 * N].rearrange("p (c n) -> p c n", c=2), ACT.Copy).then_inc(s_t5hi, 1)

            def hidden5(q, s, es):
                fixed = isinstance(q, int)

                def hi(i):
                    act.wait_ge(s_h5e, q * 4 + (i + 1))
                    act.activation(h_hi[:, s, 2 * i:2 * i + 2, :], h_whole[:, 2 * i:2 * i + 2, :], ACT.Copy).then_inc(s_hhi, 1)

                if not (fixed and q < 2):
                    act.wait_ge(s_o5, q - 1)
                for i in range(4):
                    if not (fixed and q == 0):
                        act.wait_ge(s_hlo, q * 4 + (i - 3))
                    act.wait_ge(s_h5, q * 4 + (i + 1))
                    for m in (2 * i, 2 * i + 1):
                        i_ = act.activation(h_whole[:, m, :], ps[:, HALF[i], m % 2 * N:(m % 2 + 1) * N], ACT.Relu, bias=b1E[:, es, m:m + 1])
                    i_.then_inc(s_h5e, 1)
                    if i:
                        hi(i - 1)
                hi(3)

            def expert(e, es=None):
                last = isinstance(e, int) and e == E - 1
                es = e % 2 if es is None else es
                for j in range(QE):
                    q, s = e * QE + j, j % 2
                    if not (last and j >= QE - 2):
                        T5_hi(q + 2, s)
                    if not (last and j == QE - 1):
                        hidden5(q + 1, 1 - s, of_expert(e, es, j + 1)[1])
                    if j >= 2 and not last:
                        act.wait_ge(s_wE[1 - es], uses(e + 1, 1 - es, 64))
                        for k in range(2 * j - 4, 2 * j - 2):
                            split_weights(e + 1, 1 - es, k)

            act.wait_ge(s_base, 16 * G)
            act.wait_ge(s_wE[0], 64)
            for k in range(4):
                split_weights(0, 0, k)
            T5_hi(0, 0)
            T5_hi(1, 1)
            hidden5(0, 0, 0)
            in_turns(act, steps, expert, E, 2, 2, 2)

        @block.gpsimd
        def _(pool):
            steps = Steps()
            nc.gpsimd.memset(ident[:, :], 0.0).then_inc(s_pool, steps.up())
            nc.gpsimd.memset(not_first[:, :], 0.0).then_inc(s_pool, steps.up())
            nc.gpsimd.memset(before[:, :], 0.0).then_inc(s_pool, steps.up())
            nc.gpsimd.memset(ones[:, :], 1.0).then_inc(s_pool, steps.up())
            nc.gpsimd.memset(neg_half[:, :], -0.5).then_inc(s_pool, steps.up())
            nc.gpsimd.iota(iota_i[:, :], [[1, 2 * P]], base=0, channel_multiplier=0).then_inc(s_pool, steps.up())
            pool.wait_ge(s_pool, steps.value())
            nc.gpsimd.affine_select(out=ident[:, :], in_=ident[:, :], compare_op=ALU.not_equal, fill=1.0, base=0,
                                    pattern=[[-1, 128]], channel_multiplier=1).then_inc(s_pool, steps.up())
            nc.gpsimd.affine_select(out=before[:, :], in_=before[:, :], compare_op=ALU.is_ge, fill=1.0, base=0,
                                    pattern=[[-1, P]], channel_multiplier=1).then_inc(s_pool, steps.up())
            nc.gpsimd.affine_select(out=not_first[:, :], in_=not_first[:, :], compare_op=ALU.is_ge, fill=1.0, base=0,
                                    pattern=[[1, P]], channel_multiplier=-1).then_inc(s_pool, steps.up())
            nc.gpsimd.tensor_copy(lo_iota[:, :], iota_i[:, :]).then_inc(s_pool, steps.up())
            nc.gpsimd.tensor_copy(hi_iota[:, :], iota_i[:, 0:T]).then_inc(s_pool, steps.up())
            nc.gpsimd.tensor_copy(e_iota[:, :], iota_i[:, 0:E]).then_inc(s_pool, steps.up())
            pool.wait_ge(s_pool, steps.value())
            nc.gpsimd.iota(iota_i[:, 0:T], [[P, T]], base=0, channel_multiplier=1).then_inc(s_pool, steps.up())
            pool.wait_ge(s_pool, steps.value())
            nc.gpsimd.tensor_copy(n_iota[:, :], iota_i[:, 0:T]).then_inc(s_pool, steps.up())
            nc.gpsimd.tensor_scalar(spare[:, :], iota_i[:, 0:1], float(NODES), None, ALU.add).then_inc(s_pool, steps.up())
            for k in range(2):
                i_ = nc.gpsimd.memset(va[:, k, :, DE:DC], 1.0)
            i_.then_inc(s_const, 1)

            pool.wait_ge(s_ztab, 16 * 3 * K)

            def edge_scatter(b, s=None):
                s = b % 2 if s is None else s
                pool.wait_ge(s_ecp, b + 1)
                for i in range(EB):
                    k = i % K
                    if not (isinstance(b, int) and b == 0 and i < K):
                        pool.wait_ge(s_tab[k], b * (16 * EB // K) + 16 * (i // K))
                    pool.nop(nofuse=True)
                    nc.gpsimd.indirect_dma_start(edge_sum[k], bass.IndirectOffsetOnAxis(idx_a[:, s, i:i + 1], 0),
                                                 ma[:, s, i, :], None, compute_op=ALU.add).then_inc(s_tab[k], 16)

            def root(ready, done, n, out_, in_):
                pool.wait_ge(ready, n)
                nc.gpsimd.tensor_tensor(out_, in_, neg_half[:, 0:in_.shape[1]], ALU.pow).then_inc(done, 1)

            in_turns(pool, steps, edge_scatter, AHEAD, 2, 0, 2)
            root(s_v0, s_r0, 1, rstd1[:, :], rstd1[:, :])
            pool.wait_ge(s_deg, 1)
            nc.gpsimd.tensor_tensor(dis[:, :], deg[:, :], neg_half[:, :], ALU.pow).then_inc(s_pool, steps.up())
            pool.wait_ge(s_pool, steps.value())
            nc.gpsimd.tensor_tensor(dis[:, :], dis[:, :], has[:, :], ALU.mult).then_inc(s_dis, 1)
            in_turns(pool, steps, edge_scatter, B, 0, 0, 2, first=AHEAD)

            def sum_chunk(c):
                first, n = CHUNKS[c] * GT, (CHUNKS[c + 1] - CHUNKS[c]) * GT
                rows = agg[:, first:first + n, :]
                pool.wait_ge(s_part[c % 3], 16 * K * (c // 3 + 1))
                for k in range(K - 1):
                    nc.gpsimd.tensor_tensor(rows, rows, part[c % 3][:, k, 0:n], ALU.add).then_inc(s_added, 1)
                    pool.wait_ge(s_added, c * (K - 1) + k + 1)
                pool.nop().then_inc(s_means, n // GT)

            def mlp_roots(g, s=None):
                s = g % 2 if s is None else s
                root(s_v1, s_r1, g + 1, rstd1[:, bass.ds(g * GT, GT)], var2[:, s, :])

            sum_chunk(0)
            sum_chunk(1)
            mlp_roots(0)
            sum_chunk(2)
            for c in range(3, len(CHUNKS) - 1):
                for g in range(max(CHUNKS[c - 1] - 6, 1), CHUNKS[c] - 6):
                    mlp_roots(g)
                sum_chunk(c)
            in_turns(pool, steps, mlp_roots, G, 0, 3, 2, first=CHUNKS[-2] - 6)

            def hidden0_lo(g, s, quarters):
                for i in quarters:
                    m = slice(2 * i, 2 * i + 2)
                    pool.wait_ge(s_hBhi, g * 4 + (i + 1))
                    nc.gpsimd.tensor_tensor(h0_lo[:, s, m, :], h0_whole[:, s, m, :], h_hi[:, s, m, :].bitcast(f32), ALU.subtract).then_inc(s_hBlo, 1)

            def ffn0(g, s=None):
                fixed = isinstance(g, int)
                s = g % 2 if s is None else s
                if not (fixed and g == G - 1):
                    hidden0_lo(g + 1, 1 - s, (0, 1))
                if not (fixed and g == 0):
                    root(s_vB, s_rB, g, rstd[:, 1 - s, :], var[:, 1 - s, :])
                if not (fixed and g == G - 1):
                    hidden0_lo(g + 1, 1 - s, (2, 3))
                if not (fixed and g == 0):
                    root(s_v2, s_r2, g, rstd2[:, 1 - s, :], var2[:, 1 - s, :])

            hidden0_lo(0, 0, range(4))
            in_turns(pool, steps, ffn0, G, 2, 3, 2)
            root(s_vB, s_rB, G, rstd[:, (G - 1) % 2, :], var[:, (G - 1) % 2, :])
            root(s_v2, s_r2, G, rstd2[:, (G - 1) % 2, :], var2[:, (G - 1) % 2, :])

            pool.wait_ge(s_hw[0], 16 * ((G + 1) // 2))
            pool.wait_ge(s_hw[1], 16 * (G // 2))

            def gather_in_order(b, s=None):
                s = b % 2 if s is None else s
                pool.wait_ge(s_idx, b + 1)
                if not (isinstance(b, int) and b < 2):
                    pool.wait_ge(s_pair, b * 2 - 2)
                pool.nop(nofuse=True)
                for i in range(EB):
                    nc.gpsimd.indirect_dma_start(mg[:, s, i, :], None, h_rows, bass.IndirectOffsetOnAxis(idx_a[:, s, i:i + 1], 0)).then_inc(s_gk[2 * s + i // HW], 16)

            def gather(b, s):
                pool.wait_ge(s_dsel, b + 1)
                if not (isinstance(b, int) and b < 2):
                    pool.wait_ge(s_mmm, b - 1)
                pool.nop(nofuse=True)
                for i in range(EB):
                    nc.gpsimd.indirect_dma_start(mg[:, s, i, :], None, h_rows, bass.IndirectOffsetOnAxis(idx_a[:, s, i:i + 1], 0)).then_inc(s_gk[2 * s + i // HW], 16)

            def messages(b, s=None):
                s = b % 2 if s is None else s
                if not (isinstance(b, int) and b == B - 1):
                    gather(b + 1, 1 - s)
                pool.wait_ge(s_mcp, b + 1)
                for i in range(EB):
                    k = i % K
                    if not (isinstance(b, int) and b == 0 and i < K):
                        pool.wait_ge(s_mt[k], b * (16 * EB // K) + 16 * (i // K))
                    pool.nop(nofuse=True)
                    nc.gpsimd.indirect_dma_start(node_sum[k], bass.IndirectOffsetOnAxis(idx_b[:, s, i:i + 1], 0),
                                                 ms[:, s, i, :], None, compute_op=ALU.add).then_inc(s_mt[k], 16)

            with pool.If_eq(pool.to_reg(pool.value_load(in_order[0:1, 0:1], min_val=0, max_val=1)), 1):
                in_turns(pool, steps, gather_in_order, B, 2, 2, 2)
            with pool.Else():
                pool.wait_ge(s_fzd, 16 * 8 * K)
                gather(0, 0)
                in_turns(pool, steps, messages, B, 2, 2, 2)

            def gate_roots(g, s=None):
                s = g % 2 if s is None else s
                root(s_v3, s_r3, g + 1, rstd[:, s, :], var[:, s, :])

            in_turns(pool, steps, gate_roots, G, 2, 3, 2)
            def hidden_lo(q, s):
                if not (isinstance(q, int) and q < 2):
                    pool.wait_ge(s_o5, q - 1)
                for i in range(4):
                    m = slice(2 * i, 2 * i + 2)
                    pool.wait_ge(s_hhi, q * 4 + (i + 1))
                    nc.gpsimd.tensor_tensor(h_lo[:, s, m, :], h_whole[:, m, :], h_hi[:, s, m, :].bitcast(f32), ALU.subtract).then_inc(s_hlo, 1)

            def scatter_results(q, es, j):
                pool.wait_ge(s_y5, q + 1)
                pool.nop(nofuse=True)
                for t in range(GT):
                    nc.gpsimd.indirect_dma_start(out, bass.IndirectOffsetOnAxis(out_idx[:, es, GT * j + t:GT * j + t + 1], 0), yb[:, j % 2, t, :],
                                                 None, bounds_check=NODES - 1, oob_is_err=False).then_inc(s_sc[j % 2], 16)

            def gather_rows(es, j):
                for t in range(GT * j, GT * (j + 1)):
                    nc.gpsimd.indirect_dma_start(xe[:, es, t, :], None, x3_rows, bass.IndirectOffsetOnAxis(from_idx[:, es, t:t + 1], 0)).then_inc(s_xe[j % 2], 16)

            def expert(e, es=None):
                fixed = isinstance(e, int)
                es = e % 2 if es is None else es
                for j in range(QE):
                    q, s = e * QE + j, j % 2
                    if not (fixed and e == E - 1 and j == QE - 1):
                        hidden_lo(q + 1, 1 - s)
                    if not (fixed and q == 0):
                        scatter_results(q - 1, es if j else 1 - es, j - 1 if j else QE - 1)
                    if not (fixed and e == E - 1):
                        if j == 0:
                            pool.wait_ge(s_from, e + 2)
                            pool.nop(nofuse=True)
                        gather_rows(1 - es, j)

            for i in range(2):
                pool.wait_ge(s_rows[i], 16 * ((G + 1 - i) // 2))
            pool.wait_ge(s_prob, 16)
            pool.wait_ge(s_from, 1)
            pool.nop(nofuse=True)
            for j in range(QE):
                if j >= 2:
                    pool.wait_ge(s_xe[j % 2], 16 * GT)
                    pool.nop(nofuse=True)
                gather_rows(0, j)
            pool.wait_ge(s_base, 16 * G)
            hidden_lo(0, 0)
            in_turns(pool, steps, expert, E, 2, 2, 2)
            scatter_results(QN - 1, (E - 1) % 2, QE - 1)

        @block.vector
        def _(dve):
            v = nc.vector
            st = Steps(s_dve)
            unsorted = Steps(s_dvf)

            def settle(c=st):
                dve.wait_ge(c.sem, c.value())

            def settle_fixed():
                settle()
                dve.nop(nofuse=True)

            v.memset(hT[:, 0, :, :], 0.0).then_inc(s_zero, 1)
            dve.wait_ge(s_raw, 32)
            v.tensor_copy(raw_f, raw_i).then_inc(s_rawf, 1)
            dve.wait_ge(s_rawT, 1)
            for k, f in enumerate((src_f, dst_f)):
                v.tensor_copy(f[:, :].rearrange("p (h c t) -> p h (c t)", h=2, c=4), ps[0:P, 2 * k:2 * k + 2, 0:400]).then_inc(s_dve, st.up())
            settle()
            dve.wait_ge(s_const, 1)
            v.tensor_scalar(hl_i, dst_f[:, :], 1.0 / P, None, ALU.mult).then_inc(s_dve, st.up())
            settle()
            v.tensor_copy(hi, hl_i).then_inc(s_dve, st.up())
            settle()
            v.scalar_tensor_tensor(lo, hi, -float(P), dst_f[:, :], ALU.mult, ALU.add).then_inc(s_dve, st.up())
            settle()
            for sign, op, bound in ((-1.0, ALU.is_lt, 0.0), (1.0, ALU.is_ge, float(P))):
                v.tensor_scalar(hl_w, lo, bound, sign, op, ALU.mult).then_inc(s_dve, st.up())
                settle()
                v.tensor_tensor(hi, hi, hl_w, ALU.add).then_inc(s_dve, st.up())
                v.scalar_tensor_tensor(lo, hl_w, -float(P), lo, ALU.mult, ALU.add).then_inc(s_dve, st.up())
                settle()

            def rows_to_add(s, col, rows, done, c=st):
                v.tensor_tensor(SL, S[:, s], not_first[:, :].unsqueeze(1).to_broadcast([P, EB, P]), ALU.mult).then_inc(c.sem, c.up())
                v.tensor_scalar(away[:, s], col, -1.0, spare[:, 0:1], ALU.mult, ALU.add).then_inc(c.sem, c.up())
                settle(c)
                v.tensor_reduce(dup[:, s], SL, AX, ALU.max).then_inc(c.sem, c.up())
                settle(c)
                v.tensor_tensor(dup[:, s], dup[:, s], away[:, s], ALU.mult).then_inc(c.sem, c.up())
                settle(c)
                v.tensor_tensor(rows, dup[:, s], col, ALU.add).then_inc(done, 1)

            def by_turns(body, total, c, first_turn=0):
                body(total[0], 0, total[0] // 2 + 1)
                had = c.value()
                body(total[0] + 1, 1, total[0] // 2 + 1)
                per, start = c.value() - had, c.value()
                with dve.Fori(total[0] // 2 + 1, total[1] // 2) as i:
                    for s in range(2):
                        c.base, c.k = start + (i * 2 + s - 2 - total[0]) * per, 0
                        body(i * 2 + s, s, i + 1)
                        assert c.k == per
                c.base, c.k = start + (total[1] - total[0] - 2) * per, 0

            def edge_select(b, s=None, counts=False):
                s = b % 2 if s is None else s
                dve.wait_ge(s_row[s], uses(b, s, 16))
                if not (isinstance(b, int) and b < 2):
                    dve.wait_ge(s_emm, b - 1)
                    dve.wait_ge(s_ecp, b - 1)
                col = src_f[:, bass.ds(b * EB, EB)]
                v.tensor_tensor(S[:, s], rowb[:, s], col.unsqueeze(2).to_broadcast([P, EB, P]), ALU.is_equal).then_inc(s_dve, st.up())
                if counts:
                    two = bass.ds(b * (2 * EB), 2 * EB)
                    v.tensor_tensor(ohh[:, s], hi_iota[:, :].unsqueeze(1).to_broadcast([P, 2 * EB, T]),
                                    hi[:, two].unsqueeze(2).to_broadcast([P, 2 * EB, T]), ALU.is_equal).then_inc(s_dve, st.up())
                    v.tensor_tensor(ohl[:, s], lo_iota[:, 0:P].unsqueeze(1).to_broadcast([P, 2 * EB, P]),
                                    lo[:, two].unsqueeze(2).to_broadcast([P, 2 * EB, P]), ALU.is_equal).then_inc(s_dve, st.up())
                settle()
                rows_to_add(s, col, firsts[:, s], s_esel)

            in_turns(dve, st, lambda b, s=None: edge_select(b, s, counts=True), HB, 2, 0, 2)
            edge_select(HB)

            dve.wait_ge(s_emm, HB)
            v.tensor_copy(cnt[:, :], ps[0:P, 7, 0:T]).then_inc(s_dve, st.up())
            v.tensor_scalar(windows[:, :], hi[0:1, :].rearrange("a (b k) -> a b k", k=HW)[:, :, 0:1].rearrange("a b k -> a (b k)"),
                            float(T - 2), None, ALU.min).then_inc(s_sch, 1)
            settle()
            v.tensor_scalar(has[:, :], cnt[:, :], 0.0, None, ALU.is_gt).then_inc(s_dve, st.up())
            v.tensor_scalar(deg[:, :], cnt[:, :], 1.0, None, ALU.max).then_inc(s_deg, 1)
            edge_select(HB + 1)
            dve.wait_ge(s_sch, 1)
            w2 = windows[:, :].rearrange("a (b k) -> a b k", k=2)
            v.scalar_tensor_tensor(words[:, :], w2[:, :, 1:2].rearrange("a b k -> a (b k)"), 64.0, w2[:, :, 0:1].rearrange("a b k -> a (b k)"),
                                   ALU.mult, ALU.add).then_inc(s_dve, st.up())
            dve.wait_ge(s_schp, 1)
            v.scalar_tensor_tensor(not_dst.rearrange("p (b k) -> p b k", k=HW), ps[0:P, 6, 0:2 * B].unsqueeze(2).to_broadcast([P, 2 * B, HW]), float(P),
                                   dst_f.rearrange("p (b k) -> p b k", k=HW), ALU.mult, ALU.subtract).then_inc(s_dve, st.up())
            edge_select(HB + 2)
            v.tensor_scalar(hits[0], not_dst, 0.0, None, ALU.is_le).then_inc(s_dve, st.up())
            settle()
            v.scalar_tensor_tensor(hits[1], not_dst, -2.0 * P, hits[0], ALU.is_gt, ALU.mult).then_inc(s_dve, st.up())
            settle()
            v.tensor_reduce(met[:, :], hits[1], AX, ALU.add).then_inc(s_sch, 1)
            edge_select(HB + 3)
            dve.wait_ge(s_schp, 2)
            v.tensor_scalar(in_order[:, :], ps[0:1, 0, 0:1], float(EDGES), None, ALU.is_equal).then_inc(s_sched, 1)

            def edges_and_stats(b, s=None):
                edge_select(b, s)
                tiles = (b - (HB + PLAN)) * 5
                dve.nop(nofuse=True)
                for t in range(5):
                    v.bn_stats(stat5[:, t, :], x[:, bass.ds(tiles + t, 1), :].rearrange("p a d -> p (a d)")).then_inc(s_dve, st.up())
                settle_fixed()
                for t in range(5):
                    v.bn_aggr(mv5[:, t, :], stat5[:, t, :]).then_inc(s_dve, st.up())
                settle()
                v.tensor_copy(mv1[:, bass.ds(tiles, 5), :], mv5[:, :, :]).then_inc(s_dve, st.up())
                settle()

            dve.wait_ge(s_x, 16 * (T - XB))
            in_turns(dve, st, edges_and_stats, AHEAD, 2, 0, 2, first=HB + PLAN)
            v.tensor_scalar(rstd1[:, :], mv1[:, :, 1:2].rearrange("p t a -> p (t a)"), EPS, None, ALU.add).then_inc(s_v0, 1)

            def ahead(g, s=None):
                s = g % 2 if s is None else s
                edge_select(g + AHEAD, s)
                if not (isinstance(g, int) and g < 2):
                    dve.wait_ge(s_t0, g - 1)
                for t in range(GT):
                    n = bass.ds(g * GT + t, 1)
                    i_ = v.tensor_scalar(xg[:, s, t, :], x[:, n, :].rearrange("p a d -> p (a d)"),
                                         mv1[:, n, 0:1].rearrange("p a d -> p (a d)"), rstd1[:, n], ALU.subtract, ALU.mult)
                i_.then_inc(s_x0, 1)

            dve.wait_ge(s_r0, 1)
            in_turns(dve, st, ahead, G, 2, 1, 2)
            edge_select(B - 1)

            def ln_stats(rows, s, stat_, mv_, var_, ready, meanwhile=None):
                dve.nop(nofuse=True)
                for t in range(GT):
                    v.bn_stats(stat_[:, s, t, :], rows(t)).then_inc(s_dve, st.up())
                if meanwhile:
                    meanwhile()
                settle_fixed()
                for t in range(GT):
                    v.bn_aggr(mv_[:, s, t, :], stat_[:, s, t, :]).then_inc(s_dve, st.up())
                settle()
                v.tensor_scalar(var_[:, s, :], mv_[:, s, :, 1:2].rearrange("p t a -> p (t a)"), EPS, None, ALU.add).then_inc(ready, 1)

            def edge_means(g, s):
                dve.wait_ge(s_means, g + 1)
                if not (isinstance(g, int) and g < 2):
                    dve.wait_ge(s_aT, g - 1)
                rows = agg[:, bass.ds(g * GT, GT), :]
                v.tensor_scalar(inv[:, s, :], rows[:, :, DE:DC].rearrange("p t a -> p (t a)"), 1.0, None, ALU.max).then_inc(s_dve, st.up())
                settle()
                v.reciprocal(inv[:, s, :], inv[:, s, :]).then_inc(s_dve, st.up())
                settle()
                v.tensor_tensor(ag[:, s], rows[:, :, 0:DE], inv[:, s, :].unsqueeze(2).to_broadcast([P, GT, DE]), ALU.mult).then_inc(s_a0, 1)

            def add_hidden(g, s):
                dve.wait_ge(s_hxin[s], uses(g, s, 16))
                for j in range(2):
                    half = hx[:, s, 2 * j:2 * j + 2, :]
                    dve.wait_ge(s_h1, g * 2 + (j + 1))
                    v.tensor_tensor(half, half, ps[:, 2 + j, 0:2 * N].rearrange("p (m n) -> p m n", m=2), ALU.add).then_inc(s_hadd, 1)

            def ln1_rows(g, s):
                dve.wait_ge(s_r1, g + 1)
                if not (isinstance(g, int) and g < 2):
                    dve.wait_ge(s_t1, g - 1)
                for t in range(GT):
                    n = bass.ds(g * GT + t, 1)
                    i_ = v.tensor_scalar(xh[:, s, t, :], x[:, n, :].rearrange("p a d -> p (a d)"),
                                         mv2[:, s, t, 0:1], rstd1[:, n], ALU.subtract, ALU.mult)
                i_.then_inc(s_x1, 1)

            def mlp(g, s=None):
                fixed = isinstance(g, int)
                s = g % 2 if s is None else s
                if not (fixed and g == G - 1):
                    add_hidden(g + 1, 1 - s)
                if not (fixed and g == 0):
                    ln1_rows(g - 1, 1 - s)
                if not (fixed and g >= G - 2):
                    edge_means(g + 2, s)
                xs = x[:, bass.ds(g * GT, GT), :]
                dve.wait_ge(s_o0, g + 1)
                v.tensor_tensor(yb[:, s], ps[0:P, 4 + s, :].rearrange("p (t d) -> p t d", t=GT),
                                b2A[:, :].unsqueeze(1).to_broadcast([P, GT, D]), ALU.add).then_inc(s_o0e, 1)
                dve.wait_ge(s_o0e, g + 1)
                v.tensor_tensor(xs, xs, yb[:, s], ALU.add).then_inc(s_dve, st.up())
                settle()
                ln_stats(lambda t: x[:, bass.ds(g * GT + t, 1), :].rearrange("p a d -> p (a d)"), s, stat2,
                         mv2, var2, s_v1)
                v.tensor_copy(mv1[:, bass.ds(g * GT, GT), :], mv2[:, s]).then_inc(s_dve, st.up())

            dve.wait_ge(s_cst, 160)
            edge_means(0, 0)
            edge_means(1, 1)
            add_hidden(0, 0)
            in_turns(dve, st, mlp, G, 2, 3, 2)
            ln1_rows(G - 1, (G - 1) % 2)

            dve.wait_ge(s_t1e, G)
            v.tensor_reduce(mean[:, :], msum[:, :, :], AX, ALU.add).then_inc(s_dve, st.up())
            settle()
            v.tensor_scalar(mean[:, :], mean[:, :], 1.0 / NODES, None, ALU.mult).then_inc(s_mean, 1)
            dve.wait_ge(s_lg, 1)
            v.tensor_tensor(rt[:, 1, :], ps[0:1, 6, 0:E], rt[:, 0, :], ALU.add).then_inc(s_dve, st.up())
            settle()

            def less_max(dst, src_, n):
                v.tensor_reduce(rt[:, 9, 6:7], src_, AX, ALU.max).then_inc(s_dve, st.up())
                settle()
                v.tensor_scalar(dst, src_, rt[:, 9, 6:7], None, ALU.subtract).then_inc(s_e1, 1)
                dve.wait_ge(s_e1x, n)

            def over_sum(dst, src_, at):
                v.reciprocal(rt[:, 9, at + 1:at + 2], rt[:, 9, at:at + 1]).then_inc(s_dve, st.up())
                settle()
                v.tensor_scalar(dst, src_, rt[:, 9, at + 1:at + 2], None, ALU.mult).then_inc(s_dve, st.up())
                settle()

            less_max(rt[:, 1, :], rt[:, 1, :], 1)
            over_sum(rt[:, 3, :], rt[:, 2, :], 0)
            v.tensor_scalar(rt[:, 6, :], rt[:, 3, :], float(NODES), None, ALU.mult).then_inc(s_dve, st.up())
            settle()
            v.reciprocal(rt[:, 7, :], rt[:, 6, :]).then_inc(s_dve, st.up())
            settle()
            v.tensor_scalar(rt[:, 8, :], rt[:, 7, :], float(CAP), 1.0, ALU.mult, ALU.min).then_inc(s_dve, st.up())
            settle()
            v.tensor_tensor(rt[:, 4, :], rt[:, 3, :], rt[:, 8, :], ALU.mult).then_inc(s_dve, st.up())
            settle()
            less_max(rt[:, 4, :], rt[:, 4, :], 2)
            over_sum(rt[:, 12, :], rt[:, 5, :], 2)
            v.max(rt[:, 13, :], rt[:, 12, :]).then_inc(s_dve, st.up())
            settle()
            v.max_index(rt_id[:, :], rt[:, 13, :], rt[:, 12, :]).then_inc(s_rid, 1)
            v.tensor_scalar(rt[:, 10, 0:2], rt[:, 13, 0:2], rt[:, 13, 0:1], None, ALU.subtract).then_inc(s_e1, 1)
            dve.wait_ge(s_e1x, 3)
            over_sum(rt[:, 14, 0:2], rt[:, 11, 0:2], 4)
            for k in range(2):
                i_ = v.tensor_copy(wrow[:, k, :], rt[:, 14, k:k + 1].to_broadcast([1, P]))
            i_.then_inc(s_e2x, 1)
            dve.wait_ge(s_wb, 1)
            v.tensor_copy(b2B[:, :], ps[0:P, 5, 0:D]).then_inc(s_dve, st.up())
            v.tensor_copy(wcol[:, :], ps[:, 4, 0:2]).then_inc(s_wbc, 1)
            dve.wait_ge(s_wbc, 1)

            def x_lo(g, s):
                dve.wait_ge(s_xhi, g + 1)
                v.tensor_tensor(xB_lo[:, s], xnT[:, :, bass.ds(g * N, N)], xB_hi[:, s].bitcast(f32), ALU.subtract).then_inc(s_xlo, 1)

            for k in range(2):
                h = slice(k * HID1, (k + 1) * HID1)
                dve.wait_ge(s_wBhi, k + 1)
                v.tensor_tensor(wB1_lo[:, :, h], wB1[:, :, h], wB1_hi[:, :, h].bitcast(f32), ALU.subtract).then_inc(s_wBlo, 1)
            x_lo(0, 0)
            for k in range(2):
                h = slice(4 * k, 4 * k + 4)
                dve.wait_ge(s_wBhi, k + 3)
                v.scalar_tensor_tensor(wB2_lo[:, h, :], wB2[:, h, :], wcol[:, k:k + 1], wB2_hi[:, h, :].bitcast(f32), ALU.mult, ALU.subtract).then_inc(s_wBlo, 1)
            x_lo(1, 1)
            x_lo(2, 0)

            def ffn0(g, s=None):
                fixed = isinstance(g, int)
                s = g % 2 if s is None else s
                xs = x[:, bass.ds(g * GT, GT), :]
                y, z = yb[:, s], wk[:, s]

                def wide(r):
                    return r[:, :].unsqueeze(1).to_broadcast([P, GT, D])
                for t in range(GT):
                    v.tensor_scalar(z[:, t, :], x[:, bass.ds(g * GT + t, 1), :].rearrange("p a d -> p (a d)"),
                                    mv1[:, bass.ds(g * GT + t, 1), 0:1].rearrange("p a d -> p (a d)"),
                                    rstd1[:, bass.ds(g * GT + t, 1)], ALU.subtract, ALU.mult).then_inc(s_dve, st.up())
                settle()
                v.tensor_tensor(z, z, wide(b2B), ALU.add).then_inc(s_dve, st.up())
                settle()
                dve.wait_ge(s_oB, g + 1)
                v.tensor_tensor(y, ps[0:P, 4 + s, :].rearrange("p (t d) -> p t d", t=GT), z, ALU.add).then_inc(s_oBe, 1)
                dve.wait_ge(s_oBe, g + 1)
                ln_stats(lambda t: y[:, t, :], s, stat, mv, var, s_vB)
                if not (fixed and g >= G - 3):
                    x_lo(g + 3, 1 - s)
                dve.wait_ge(s_rB, g + 1)
                for t in range(GT):
                    v.tensor_scalar(z[:, t, :], y[:, t, :], mv[:, s, t, 0:1], rstd[:, s, t:t + 1], ALU.subtract, ALU.mult).then_inc(s_dve, st.up())
                settle()
                v.tensor_tensor(z, z, wide(gamma), ALU.mult).then_inc(s_dve, st.up())
                settle()
                v.tensor_tensor(z, z, wide(beta), ALU.add).then_inc(s_dve, st.up())
                settle()
                v.tensor_tensor(xs, xs, z, ALU.add).then_inc(s_dve, st.up())
                settle()
                ln_stats(lambda t: x[:, bass.ds(g * GT + t, 1), :].rearrange("p a d -> p (a d)"), s, stat2,
                         mv2, var2, s_v2)
                dve.wait_ge(s_r2, g + 1)
                if not (fixed and g < 2):
                    dve.wait_ge(s_t2, g - 1)
                for t in range(GT):
                    i_ = v.tensor_scalar(xh[:, s, t, :], x[:, bass.ds(g * GT + t, 1), :].rearrange("p a d -> p (a d)"),
                                         mv2[:, s, t, 0:1], rstd2[:, s, t:t + 1], ALU.subtract, ALU.mult)
                i_.then_inc(s_x2, 1)

            in_turns(dve, st, ffn0, G, 2, 3, 2)

            def add_to_windows(b, s=None):
                s = b % 2 if s is None else s
                word = dve.value_load(words[0:1, bass.ds(b, 1)], min_val=0, max_val=(T - 2) * 65)
                for j, w in enumerate((dve.snap(word & 63), dve.snap(word >> 6))):
                    w = nc.s_assert_within(w, 0, T - 2, skip_runtime_bounds_check_because="windows are set to at most T - 2")
                    rows = acc[:, bass.ds(w, 2), :].rearrange("p w d -> p (w d)")
                    dve.wait_ge(s_pair, b * 2 + (j + 1))
                    if not (isinstance(b, int) and b == 0 and j == 0):
                        dve.wait_ge(s_acc, b * 2 + j)
                    v.tensor_tensor(rows, rows, ps[0:P, 2 * s + j, :], ALU.add).then_inc(s_acc, 1)

            def msg_select(b, s, turn):
                c = unsorted
                dve.wait_ge(s_drow[s], turn * 16)
                if not (isinstance(b, int) and b < 2):
                    dve.wait_ge(s_mmm, b - 1)
                    for k in range(K):
                        dve.wait_ge(s_mt[k], (b - 1) * (16 * EB // K))
                col = dst_f[:, bass.ds(b * EB, EB)]
                v.tensor_copy(idx_a[:, s, :], src_f[:, bass.ds(b * EB, EB)]).then_inc(c.sem, c.up())
                v.tensor_tensor(S[:, s], rowb[:, s], col.unsqueeze(2).to_broadcast([P, EB, P]), ALU.is_equal).then_inc(c.sem, c.up())
                settle(c)
                rows_to_add(s, col, idx_b[:, s, :], s_dsel, c)

            def sum_tables(g, s, turn):
                c = unsorted
                dve.wait_ge(s_nt[s], turn * (16 * K))
                for k in range(1, K):
                    o_ = acc[:, bass.ds(g * GT, GT), :] if k == K - 1 else yb[:, s]
                    v.tensor_tensor(o_, tab[:, s, 0] if k == 1 else yb[:, s], tab[:, s, k], ALU.add).then_inc(
                        s_fs if k == K - 1 else c.sem, 1 if k == K - 1 else c.up())
                    if k < K - 1:
                        settle(c)

            dve.wait_ge(s_dis, 1)
            dve.wait_ge(s_xlo, G)
            dve.wait_ge(s_back, 16)
            with dve.If_eq(dve.to_reg(dve.value_load(in_order[0:1, 0:1], min_val=0, max_val=1)), 1):
                v.memset(acc, 0.0).then_inc(s_accz, 1)
                dve.wait_ge(s_accz, 1)
                in_turns(dve, Steps(), add_to_windows, B, 2, 2, 2)
                dve.wait_ge(s_acc, 2 * B)
            with dve.Else():
                dve.wait_ge(s_hrow, G)
                v.memset(hT[:, 0, :, :], 0.0).then_inc(s_fz, 1)
                by_turns(msg_select, (0, B), unsorted)
                by_turns(sum_tables, (0, G - 1), unsorted)
                sum_tables(G - 1, 0, G // 2 + 1)
                dve.wait_ge(s_fs, G)

            def ln3_rows(g, s):
                dve.wait_ge(s_r3, g + 1)
                if not (isinstance(g, int) and g < 2):
                    dve.wait_ge(s_t3, g - 1)
                for t in range(GT):
                    i_ = v.tensor_scalar(xh[:, s, t, :], x[:, bass.ds(g * GT + t, 1), :].rearrange("p a d -> p (a d)"),
                                         mv[:, s, t, 0:1], rstd[:, s, t:t + 1], ALU.subtract, ALU.mult)
                i_.then_inc(s_x3, 1)

            def logits(g, s):
                dve.wait_ge(s_l3, g + 1)
                v.tensor_tensor(gate3[:, 0, bass.ds(g * GT, GT), :], ps[0:P, 6 + s, 0:GT * E].rearrange("p (t e) -> p t e", t=GT),
                                gb[:, :].unsqueeze(1).to_broadcast([P, GT, E]), ALU.add).then_inc(s_l3e, 1)

            def gate_group(g, s=None):
                fixed = isinstance(g, int)
                s = g % 2 if s is None else s
                for t in range(GT):
                    xs = x[:, bass.ds(g * GT + t, 1), :].rearrange("p a d -> p (a d)")
                    v.scalar_tensor_tensor(xs, acc[:, bass.ds(g * GT + t, 1), :].rearrange("p a d -> p (a d)"), dis[:, bass.ds(g * GT + t, 1)],
                                           xs, ALU.mult, ALU.add).then_inc(s_dve, st.up())
                if not (fixed and g == 0):
                    ln3_rows(g - 1, 1 - s)
                if not (fixed and g < 2):
                    dve.wait_ge(s_x3c, g - 1)
                settle()
                ln_stats(lambda t: x[:, bass.ds(g * GT + t, 1), :].rearrange("p a d -> p (a d)"), s, stat, mv, var, s_v3,
                         None if fixed and g < 3 else lambda: logits(g - 3, 1 - s))

            in_turns(dve, st, gate_group, G, 4, 3, 2)
            ln3_rows(G - 1, (G - 1) % 2)
            for g in (G - 3, G - 2, G - 1):
                logits(g, g % 2)
            dve.wait_ge(s_l3e, G)

            def tt(o_, i0, i1, op):
                v.tensor_tensor(o_, i0, i1, op).then_inc(s_dve, st.up())
                settle()

            def ts(o_, i0, c1, c2, op0, op1=ALU.bypass):
                v.tensor_scalar(o_, i0, c1, c2, op0, op1).then_inc(s_dve, st.up())
                settle()

            def red(o_, i_, op):
                v.tensor_reduce(o_, i_, AX, op).then_inc(s_dve, st.up())
                settle()

            def per_token(k):
                return g50[:, k, :].unsqueeze(2).to_broadcast([P, T, E])

            def per_expert(r):
                return r.unsqueeze(1).to_broadcast([P, T, E])
            red(g50[:, 0, :], gate3[:, 0], ALU.max)
            v.tensor_tensor(gate3[:, 1], gate3[:, 0], per_token(0), ALU.subtract).then_inc(s_ga1, 1)
            dve.wait_ge(s_gexp, 1)
            red(g50[:, 1, :], gate3[:, 1], ALU.add)
            red(g50[:, 2, :], gate3[:, 1], ALU.max)
            v.reciprocal(g50[:, 3, :], g50[:, 1, :]).then_inc(s_dve, st.up())
            settle()
            v.tensor_tensor(prob, g50[:, 2, :], g50[:, 3, :], ALU.mult).then_inc(s_pset, 1)
            tt(gate3[:, 2], gate3[:, 1], per_token(2), ALU.is_ge)
            ts(gate3[:, 3], gate3[:, 2], -float(E), float(E), ALU.mult, ALU.add)
            tt(gate3[:, 4], gate3[:, 3], per_expert(e_iota[:, :]), ALU.add)
            red(g50[:, 4, :], gate3[:, 4], ALU.min)
            v.tensor_tensor(gate3[:, 5], per_expert(e_iota[:, :]), per_token(4), ALU.is_equal).then_inc(s_goh, 1)
            dve.wait_ge(s_grk, 1)
            v.tensor_copy(gate[:, 6, :], ps[0:P, 2, 0:T * E]).then_inc(s_dve, st.up())
            v.tensor_copy(gate[:, 7, :], ps[0:P, 3, 0:T * E]).then_inc(s_dve, st.up())
            v.memset(gate[:, 8, :], 1.0).then_inc(s_dve, st.up())
            settle()
            for e in range(E):
                v.tensor_tensor_scan(gate3[:, 9, :, e], gate3[:, 8, :, e], gate3[:, 7, :, e], 0.0, ALU.mult, ALU.add).then_inc(s_dve, st.up())
            settle()
            tt(gate3[:, 9], gate3[:, 9], gate3[:, 7], ALU.subtract)
            tt(gate3[:, 9], gate3[:, 9], gate3[:, 6], ALU.add)
            tt(gate3[:, 9], gate3[:, 9], gate3[:, 5], ALU.mult)
            red(g50[:, 5, :], gate3[:, 9], ALU.add)
            ts(g50[:, 6, :], g50[:, 5, :], float(CAP), None, ALU.is_lt)
            ts(tile_end, e_iota[:, :], float(P), None, ALU.mult)
            tt(gate3[:, 9], g50[:, 5, :].unsqueeze(2).to_broadcast([P, T, ST]), tile_end.unsqueeze(1).to_broadcast([P, T, ST]), ALU.is_ge)
            red(g50[:, 7, :], gate3[:, 9], ALU.add)
            v.scalar_tensor_tensor(g50[:, 8, :], g50[:, 7, :], -float(P), g50[:, 5, :], ALU.mult, ALU.add).then_inc(s_dve, st.up())
            v.scalar_tensor_tensor(g50[:, 9, :], g50[:, 4, :], float(ST), g50[:, 7, :], ALU.mult, ALU.add).then_inc(s_dve, st.up())
            settle()
            ts(g50[:, 10, :], g50[:, 8, :], float(P), None, ALU.add)
            tt(g50[:, 11, :], g50[:, 9, :], g50[:, 6, :], ALU.mult)
            v.tensor_scalar(g50[:, 12, :], n_iota[:, :], 1.0, None, ALU.add).then_inc(s_slots, 1)
            dve.wait_ge(s_slots, 1)
            for c in range(T // EB):
                s, n = c % 2, slice(c * EB, (c + 1) * EB)
                hi_, lo_ = hi_hot[:, s], lo_hot[:, s]
                if c >= 2:
                    dve.wait_ge(s_inv, c - 1)
                v.tensor_tensor(hi_, lo_iota[:, 1:1 + E * ST].unsqueeze(1).to_broadcast([P, EB, E * ST]),
                                g50[:, 11, n].unsqueeze(2).to_broadcast([P, EB, E * ST]), ALU.is_equal).then_inc(s_dve, st.up())
                v.tensor_tensor(lo_, lo_iota[:, 0:P].unsqueeze(1).to_broadcast([P, EB, P]),
                                g50[:, 10, n].unsqueeze(2).to_broadcast([P, EB, P]), ALU.is_equal).then_inc(s_dve, st.up())
                settle()
                v.tensor_tensor(hi_, hi_, g50[:, 12, n].unsqueeze(2).to_broadcast([P, EB, E * ST]), ALU.mult).then_inc(s_hot, 1)
            dve.wait_ge(s_inv, T // EB)
            v.tensor_copy(slot_token, ps[0:P, 4, 0:E * ST]).then_inc(s_dve, st.up())
            settle()
            ts(slot_none, slot_token, 0.0, float(NODES + 1), ALU.is_equal, ALU.mult)
            v.scalar_tensor_tensor(slot_to, slot_token, -1.0, slot_none, ALU.add, ALU.add).then_inc(s_dve, st.up())
            ts(slot_from, slot_token, -1.0, 0.0, ALU.add, ALU.max)
            v.tensor_copy(from_idx[:, 0, :], slot_from[:, 0:ST]).then_inc(s_from, 1)

            def split_weights(e, es, k):
                piece = weight_piece(k, w1E[:, es], w2E[:, es])
                dve.wait_ge(s_whi, e * 4 + (k + 1))
                v.tensor_tensor(weight_piece(k, w1_lo[:, es], w2_lo[:, es]), piece, weight_piece(k, w1_hi[es], w2_hi[es]).bitcast(f32),
                                ALU.subtract).then_inc(s_wlo, 1)

            def T5_lo(q, s):
                dve.wait_ge(s_t5hi, q + 1)
                v.tensor_tensor(xT_lo[:, s], ps[:, s, 0:2 * N].rearrange("p (c n) -> p c n", c=2), xT_hi[:, s].bitcast(f32), ALU.subtract).then_inc(s_t5lo, 1)

            def slot_rows(q, s, es, j):
                if not (isinstance(q, int) and q < 2):
                    dve.wait_ge(s_t5, q - 1)
                for t in range(GT):
                    row = xe[:, es, GT * j + t, :]
                    i_ = v.tensor_scalar(xh[:, s, t, :], row[:, 0:D], row[:, MEAN:MEAN + 1], row[:, RSTD:RSTD + 1], ALU.subtract, ALU.mult)
                i_.then_inc(s_xn, 1)

            def expert_out(e, es=None):
                fixed = isinstance(e, int)
                es = e % 2 if es is None else es
                for j in range(QE):
                    s = j % 2
                    q = e * QE + j
                    y, r = yb[:, s], nanw
                    last = fixed and e == E - 1
                    if j == 0:
                        v.tensor_copy(out_idx[:, es, :], slot_to[:, bass.ds(e * ST, ST)]).then_inc(s_dve, st.up())
                        settle()
                        if not last:
                            v.tensor_copy(from_idx[:, 1 - es, :], slot_from[:, bass.ds((e + 1) * ST, ST)]).then_inc(s_from, 1)
                    if not (last and j >= QE - 2):
                        T5_lo(q + 2, s)
                    if not (last and j >= QE - 3):
                        _, es3, j3 = of_expert(e, es, j + 3)
                        dve.wait_ge(s_xe[1 - s], uses(q + 3, 1 - s, 16 * GT))
                        slot_rows(q + 3, 1 - s, es3, j3)
                    if j >= 2 and not last:
                        for k in range(2 * j - 4, 2 * j - 2):
                            split_weights(e + 1, 1 - es, k)
                    dve.wait_ge(s_o5, q + 1)
                    v.tensor_tensor(r[:, 0], ps[0:P, 4 + s, :].rearrange("p (t d) -> p t d", t=GT),
                                    b2E[:, es, :].unsqueeze(1).to_broadcast([P, GT, D]), ALU.add).then_inc(s_dve, st.up())
                    settle()
                    for t in range(GT):
                        i_ = v.tensor_scalar(r[:, 1, t, :], r[:, 0, t, :], xe[:, es, GT * j + t, PROB:PROB + 1], None, ALU.mult)
                    i_.then_inc(s_o5e, 1)
                    dve.wait_ge(s_o5e, q + 1)
                    if not (fixed and q < 2):
                        dve.wait_ge(s_sc[s], uses(q, s, 16 * GT) - 16 * GT)
                    v.tensor_scalar(r[:, 2], r[:, 1], FMAX, 1e4, ALU.is_gt, ALU.mult).then_inc(s_dve, st.up())
                    v.tensor_scalar(r[:, 0], r[:, 1], -FMAX, -1e4, ALU.is_lt, ALU.mult).then_inc(s_dve, st.up())
                    v.tensor_scalar(r[:, 3], r[:, 1], FMAX, None, ALU.is_le).then_inc(s_dve, st.up())
                    settle()
                    v.tensor_tensor(y, r[:, 2], r[:, 0], ALU.add).then_inc(s_dve, st.up())
                    v.scalar_tensor_tensor(r[:, 3], r[:, 1], -FMAX, r[:, 3], ALU.is_ge, ALU.mult).then_inc(s_dve, st.up())
                    settle_fixed()
                    v.copy_predicated(y, r[:, 3].bitcast(u32), r[:, 1]).then_inc(s_dve, st.up())
                    settle()
                    v.tensor_tensor(y, y, xe[:, es, GT * j:GT * (j + 1), 0:D], ALU.add).then_inc(s_y5, 1)
                    dve.wait_ge(s_y5, q + 1)

            for k in range(4):
                split_weights(0, 0, k)
            dve.wait_ge(s_xe[0], 16 * GT)
            slot_rows(0, 0, 0, 0)
            dve.wait_ge(s_xe[1], 16 * GT)
            slot_rows(1, 1, 0, 1)
            T5_lo(0, 0)
            T5_lo(1, 1)
            dve.wait_ge(s_xe[0], 2 * 16 * GT)
            slot_rows(2, 0, 0, 2)
            in_turns(dve, st, expert_out, E, 2, 2, 2)

        @block.tensor
        def _(pe):
            steps = Steps()
            mm, tr = nc.tensor.matmul, nc.tensor.transpose
            pe.wait_ge(s_const, 1)
            pe.wait_ge(s_rawf, 1)
            for k in range(2):
                for c in range(8):
                    i_ = tr(ps[0:P, 2 * k + c // 4, (c % 4) * 100:(c % 4 + 1) * 100], raw_f[:, k, c, :], ident[0:100, 0:100])
            i_.then_inc(s_rawT, 1)

            def edge_sums(b, s=None, first=False, counts=False, last=False):
                s = b % 2 if s is None else s
                pe.wait_ge(s_esel, b + 1)
                pe.wait_ge(s_va[s], uses(b, s, 16))
                if not first:
                    pe.wait_ge(s_ecp, b - 1)
                for i in range(2 * EB if counts else 0):
                    mm(ps[0:P, 7, 0:T], ohl[:, s, i, :], ohh[:, s, i, :], start=(first and s == 0 and i == 0), stop=(last and s == 1 and i == 2 * EB - 1))
                for i in range(EB):
                    i_ = mm(ps[0:P, 2 + 2 * s + i // 5, (i % 5) * DC:(i % 5 + 1) * DC], S[:, s, i, :], va[:, s, i, :], start=True, stop=True)
                i_.then_inc(s_emm, 1)

            edge_sums(0, first=True, counts=True)
            edge_sums(1, first=True, counts=True)
            in_turns(pe, steps, lambda b, s=None: edge_sums(b, s, counts=True), HB - 2, 0, 0, 2, first=2)
            edge_sums(HB - 2, counts=True, last=True)
            edge_sums(HB - 1, counts=True, last=True)
            edge_sums(HB)

            pe.wait_ge(s_sch, 1)
            mm(ps[0:P, 6, 0:2 * B], ones[0:1, :], windows[:, :], start=True, stop=True).then_inc(s_schp, 1)
            edge_sums(HB + 1)
            edge_sums(HB + 2)
            pe.wait_ge(s_sch, 2)
            mm(ps[0:1, 0, 0:1], met[:, :], ones[:, 0:1], start=True, stop=True).then_inc(s_schp, 1)
            edge_sums(HB + 3)

            in_turns(pe, steps, edge_sums, AHEAD, 0, 0, 2, first=HB + PLAN)

            pe.wait_ge(s_wA, 64)
            pe.wait_ge(s_cst, 160)
            pe.wait_ge(s_sched, 1)
            for m in range(4):
                i_ = mm(ps[:, 7, m:m + 1], wU[:, m * 128:(m + 1) * 128], u0[:, :], start=True, stop=True)
            i_.then_inc(s_bA, 1)

            def T0(g, s):
                pe.wait_ge(s_x0, g + 1)
                if not (isinstance(g, int) and g < 2):
                    pe.wait_ge(s_t0e, g - 1)
                for t in range(GT):
                    for c in range(2):
                        i_ = tr(ps[:, s, c * N + t * P:c * N + (t + 1) * P], xg[:, s, t, c * 128:(c + 1) * 128], ident[0:P, 0:P])
                i_.then_inc(s_t0, 1)

            def hidden_x(g, s):
                pe.wait_ge(s_t0e, g + 1)
                for m in range(4):
                    if isinstance(g, int) and g == 0 and m < 2:
                        pe.wait_ge(s_bAset, 1)
                    else:
                        pe.wait_ge(s_hx, g * 4 + (m - 1))
                    for c in range(2):
                        i_ = mm(ps[:, 6 + m % 2, 0:N], wA1x[:, c, m * 128:(m + 1) * 128], xTg[:, s, c, :], start=(c == 0), stop=(c == 1))
                    i_.then_inc(s_h0, 1)

            def ahead(g, s=None):
                s = g % 2 if s is None else s
                edge_sums(g + AHEAD, s)
                T0(g, s)
                if not (isinstance(g, int) and g == 0):
                    hidden_x(g - 1, 1 - s)

            in_turns(pe, steps, ahead, G, 2, 1, 2)
            edge_sums(B - 1)
            hidden_x(G - 1, (G - 1) % 2)

            def means_T(g, s):
                pe.wait_ge(s_a0, g + 1)
                if isinstance(g, int) and g == 0:
                    pe.wait_ge(s_hx, 4 * G)
                else:
                    pe.wait_ge(s_aTe, g)
                pe.nop(nofuse=True)
                for t in range(GT):
                    i_ = tr(ps[0:DE, 6, s * N + t * P:s * N + (t + 1) * P], ag[:, s, t, :], ident[0:P, 0:P])
                i_.then_inc(s_aT, 1)

            def hidden(g, s):
                pe.wait_ge(s_aTe, g + 1)
                for j in range(2):
                    if not (isinstance(g, int) and g == 0):
                        pe.wait_ge(s_hadd, g * 2 + (j - 1))
                    for m in (2 * j, 2 * j + 1):
                        i_ = mm(ps[:, 2 + j, m % 2 * N:(m % 2 + 1) * N], wA1e[:, m * 128:(m + 1) * 128], aT[:, s, :], start=True, stop=True)
                    i_.then_inc(s_h1, 1)

            def T1(g, s):
                pe.wait_ge(s_x1, g + 1)
                if not (isinstance(g, int) and g == 0):
                    pe.wait_ge(s_t1e, g)
                for t in range(GT):
                    for c in range(2):
                        i_ = tr(ps[:, 7, c * N + t * P:c * N + (t + 1) * P], xh[:, s, t, c * 128:(c + 1) * 128], ident[0:P, 0:P])
                i_.then_inc(s_t1, 1)

            def mlp(g, s=None):
                fixed = isinstance(g, int)
                s = g % 2 if s is None else s
                if not (fixed and g == G - 1):
                    hidden(g + 1, 1 - s)
                pe.wait_ge(s_h1e, g * 2 + 2)
                if not (fixed and g < 2):
                    pe.wait_ge(s_o0e, g - 1)
                for t in range(GT):
                    for m in range(4):
                        i_ = mm(ps[0:P, 4 + s, t * D:(t + 1) * D], hT[:, s, m, t * P:(t + 1) * P], wA2[:, m, :], start=(m == 0), stop=(m == 3))
                i_.then_inc(s_o0, 1)
                if not (fixed and g >= G - 2):
                    means_T(g + 2, s)
                if not (fixed and g == 0):
                    T1(g - 1, 1 - s)

            pe.wait_ge(s_ecp, B)
            means_T(0, 0)
            means_T(1, 1)
            hidden(0, 0)
            in_turns(pe, steps, mlp, G, 2, 3, 2)
            T1(G - 1, (G - 1) % 2)

            pe.wait_ge(s_mean, 1)
            for c in range(2):
                i_ = mm(ps[0:1, 6, 0:E], mean[:, c:c + 1], wr[:, c, :], start=(c == 0), stop=(c == 1))
            i_.then_inc(s_lg, 1)
            pe.wait_ge(s_o0e, G)
            pe.wait_ge(s_e2x, 1)
            pe.wait_ge(s_b2r, 32)
            mm(ps[:, 4, 0:2], ones[0:1, 0:1].to_broadcast([1, 128]), rt[:, 14, 0:2], start=True, stop=True)
            for k in range(2):
                i_ = mm(ps[0:P, 5, 0:D], wrow[:, k, :], b2rows[:, k, :], start=(k == 0), stop=(k == 1))
            i_.then_inc(s_wb, 1)

            def T2(g, s):
                pe.wait_ge(s_x2, g + 1)
                if not (isinstance(g, int) and g == 0):
                    pe.wait_ge(s_t2e, g)
                for t in range(GT):
                    for c in range(2):
                        i_ = tr(ps[:, 0, c * N + t * P:c * N + (t + 1) * P], xh[:, s, t, c * 128:(c + 1) * 128], ident[0:P, 0:P])
                i_.then_inc(s_t2, 1)

            def H(g, s):
                pe.wait_ge(s_t2e, g + 1)
                if not (isinstance(g, int) and g == 0):
                    pe.wait_ge(s_hrow, g)
                for t in range(GT):
                    for c in range(2):
                        i_ = mm(ps[0:P, 7, t * D:(t + 1) * D], xTg[:, s, c, t * P:(t + 1) * P], wG[:, c, :], start=(c == 0), stop=(c == 1))
                i_.then_inc(s_hm, 1)

            def hidden0(g, s):
                pe.wait_ge(s_xlo, g + 1)
                for i in range(4):
                    if not (isinstance(g, int) and g == 0):
                        pe.wait_ge(s_hBe, g * 4 + (i - 3))
                    for m in (2 * i, 2 * i + 1):
                        f = slice(m * 128, (m + 1) * 128)
                        o_ = ps[:, HALF0[i], m % 2 * N:(m % 2 + 1) * N]
                        for c in range(2):
                            mm(o_, wB1_hi[:, c, f], xB_hi[:, s, c, :], start=(c == 0), stop=False)
                            mm(o_, wB1_hi[:, c, f], xB_lo[:, s, c, :], start=False, stop=False)
                            i_ = mm(o_, wB1_lo[:, c, f], xB_hi[:, s, c, :], start=False, stop=(c == 1))
                    i_.then_inc(s_hB, 1)

            def ffn0(g, s=None):
                fixed = isinstance(g, int)
                s = g % 2 if s is None else s
                if not (fixed and g < 2):
                    T2(g - 2, s)
                if not (fixed and g == G - 1):
                    hidden0(g + 1, 1 - s)
                if not (fixed and g < 2):
                    H(g - 2, s)
                if fixed and g == 0:
                    pe.wait_ge(s_wBlo, 4)
                pe.wait_ge(s_hBhi, g * 4 + 4)
                pe.wait_ge(s_hBlo, g * 4 + 4)
                if not (fixed and g < 2):
                    pe.wait_ge(s_oBe, g - 1)
                for t in range(GT):
                    rows, o_ = slice(t * P, (t + 1) * P), ps[0:P, 4 + s, t * D:(t + 1) * D]
                    for m in range(8):
                        mm(o_, h_hi[:, s, m, rows], wB2_hi[:, m, :], start=(m == 0), stop=False)
                        mm(o_, h_hi[:, s, m, rows], wB2_lo[:, m, :], start=False, stop=False)
                        i_ = mm(o_, h0_lo[:, s, m, rows], wB2_hi[:, m, :], start=False, stop=(m == 7))
                i_.then_inc(s_oB, 1)

            pe.wait_ge(s_wbc, 1)
            pe.wait_ge(s_wBlo, 2)
            hidden0(0, 0)
            in_turns(pe, steps, ffn0, G, 4, 3, 2)
            for g in (G - 2, G - 1):
                T2(g, g % 2)
                H(g, g % 2)

            def window_sums(b, s=None):
                s = b % 2 if s is None else s
                pe.wait_ge(s_onto, b + 1)
                for j in range(2):
                    pe.wait_ge(s_gk[2 * s + j], uses(b, s, 16 * HW))
                    if not (isinstance(b, int) and b < 2):
                        pe.wait_ge(s_acc, b * 2 + (j - 3))
                    for w in range(2):
                        for i in range(HW):
                            t = j * HW + i
                            i_ = mm(ps[0:P, 2 * s + j, w * D:(w + 1) * D], onto[:, s, t, w * P:(w + 1) * P], mg[:, s, t, :], start=(i == 0), stop=(i == HW - 1))
                    i_.then_inc(s_pair, 1)

            def msg_sums(b, s, turns, first=False):
                pe.wait_ge(s_dsel, b + 1)
                for j in range(2):
                    pe.wait_ge(s_gk[2 * s + j], turns * (16 * HW))
                if not first:
                    pe.wait_ge(s_mcp, b)
                for i in range(EB):
                    i_ = mm(ps[0:P, i // 2, (i % 2) * D:(i % 2 + 1) * D], S[:, s, i, :], mg[:, s, i, :], start=True, stop=True)
                i_.then_inc(s_mmm, 1)

            pe.wait_ge(s_hrow, G)
            with pe.If_eq(pe.to_reg(pe.value_load(in_order[0:1, 0:1], min_val=0, max_val=1)), 1):
                in_turns(pe, steps, window_sums, B, 2, 2, 2)
                pe.wait_ge(s_acc, 2 * B)
            with pe.Else():
                msg_sums(0, 0, 1, first=True)
                msg_sums(1, 1, 1)
                with pe.Fori(1, B // 2) as i:
                    msg_sums(i * 2, 0, i + 1)
                    msg_sums(i * 2 + 1, 1, i + 1)
                pe.wait_ge(s_mcp, B)

            def T3(g, s):
                pe.wait_ge(s_x3, g + 1)
                if not (isinstance(g, int) and g < 2):
                    pe.wait_ge(s_t3e, g - 1)
                for t in range(GT):
                    for c in range(2):
                        i_ = tr(ps[:, s, c * N + t * P:c * N + (t + 1) * P], xh[:, s, t, c * 128:(c + 1) * 128], ident[0:P, 0:P])
                i_.then_inc(s_t3, 1)

            def gate_mm(g, s=None):
                s = g % 2 if s is None else s
                if not (isinstance(g, int) and g == G - 1):
                    T3(g + 1, 1 - s)
                pe.wait_ge(s_t3e, g + 1)
                if not (isinstance(g, int) and g < 2):
                    pe.wait_ge(s_l3e, g - 1)
                for t in range(GT):
                    for c in range(2):
                        i_ = mm(ps[0:P, 6 + s, t * E:(t + 1) * E], xTg[:, s, c, t * P:(t + 1) * P], gw[:, c, :], start=(c == 0), stop=(c == 1))
                i_.then_inc(s_l3, 1)

            T3(0, 0)
            in_turns(pe, steps, gate_mm, G, 2, 3, 2)
            pe.wait_ge(s_goh, 1)
            mm(ps[0:P, 2, 0:T * E], before[:, :], gate[:, 5, :], start=True, stop=True)
            mm(ps[0:P, 3, 0:T * E], ones[:, :], gate[:, 5, :], start=True, stop=True).then_inc(s_grk, 1)
            for c in range(T // EB):
                pe.wait_ge(s_hot, c + 1)
                for i in range(EB):
                    i_ = mm(ps[0:P, 4, 0:E * ST], lo_hot[:, c % 2, i, :], hi_hot[:, c % 2, i, :],
                            start=(c == 0 and i == 0), stop=(c == T // EB - 1 and i == EB - 1))
                i_.then_inc(s_inv, 1)

            def T5(q, s):
                pe.wait_ge(s_xn, q + 1)
                if not (isinstance(q, int) and q < 2):
                    pe.wait_ge(s_t5lo, q - 1)
                for t in range(GT):
                    for c in range(2):
                        i_ = tr(ps[:, s, c * N + t * P:c * N + (t + 1) * P], xh[:, s, t, c * 128:(c + 1) * 128], ident[0:P, 0:P])
                i_.then_inc(s_t5, 1)

            def hidden5(q, s, es):
                pe.wait_ge(s_t5lo, q + 1)
                for i in range(4):
                    if not (isinstance(q, int) and q == 0):
                        pe.wait_ge(s_h5e, q * 4 + (i - 3))
                    for m in (2 * i, 2 * i + 1):
                        f = slice(m * 128, (m + 1) * 128)
                        for c in range(2):
                            o_ = ps[:, HALF[i], m % 2 * N:(m % 2 + 1) * N]
                            mm(o_, w1_hi[es][:, c, f], xT_hi[:, s, c, :], start=(c == 0), stop=False)
                            mm(o_, w1_hi[es][:, c, f], xT_lo[:, s, c, :], start=False, stop=False)
                            i_ = mm(o_, w1_lo[:, es, c, f], xT_hi[:, s, c, :], start=False, stop=(c == 1))
                    i_.then_inc(s_h5, 1)

            def out5(q, s, es):
                pe.wait_ge(s_hhi, q * 4 + 4)
                pe.wait_ge(s_hlo, q * 4 + 4)
                if not (isinstance(q, int) and q < 2):
                    pe.wait_ge(s_o5e, q - 1)
                for t in range(GT):
                    rows, o_ = slice(t * P, (t + 1) * P), ps[0:P, 4 + s, t * D:(t + 1) * D]
                    for m in range(8):
                        mm(o_, h_hi[:, s, m, rows], w2_hi[es][:, m, :], start=(m == 0), stop=False)
                        mm(o_, h_hi[:, s, m, rows], w2_lo[:, es, m, :], start=False, stop=False)
                        i_ = mm(o_, h_lo[:, s, m, rows], w2_hi[es][:, m, :], start=False, stop=(m == 7))
                i_.then_inc(s_o5, 1)

            def expert(e, es=None):
                last = isinstance(e, int) and e == E - 1
                es = e % 2 if es is None else es
                for j in range(QE):
                    q, s = e * QE + j, j % 2
                    if not (last and j >= QE - 2):
                        T5(q + 2, s)
                    if not (last and j == QE - 1):
                        if j == QE - 1:
                            pe.wait_ge(s_wlo, e * 4 + 6)
                        hidden5(q + 1, 1 - s, of_expert(e, es, j + 1)[1])
                    if j == 0:
                        pe.wait_ge(s_wlo, e * 4 + 4)
                    out5(q, s, es)

            T5(0, 0)
            T5(1, 1)
            pe.wait_ge(s_wlo, 2)
            hidden5(0, 0, 0)
            in_turns(pe, steps, expert, E, 2, 2, 2)


_INS = ["x", "src", "dst", "edge_attr_64", "L0_gnn_u", "L0_gnn_W1", "L0_gnn_b1", "L0_gnn_W2", "L0_gnn_b2", "L0_ffn_Wr",
        "L0_ffn_br", "L0_ffn_W1", "L0_ffn_b1", "L0_ffn_W2", "L0_ffn_b2", "L0_ffn_gamma", "L0_ffn_beta", "L1_gnn_W",
        "L1_ffn_gate_w", "L1_ffn_gate_b", "L1_ffn_w1", "L1_ffn_b1", "L1_ffn_w2", "L1_ffn_b2"]


def kernel(**inputs):
    import numpy as np
    import concourse.bacc as bacc
    from concourse import mybir as mb
    from concourse.bass_utils import run_bass_kernel_spmd as run

    nc = bacc.Bacc("TRN2", target_bir_lowering=False, num_devices=1)
    arrays, aps = {}, {}
    for name in _INS:
        v = np.ascontiguousarray(inputs[name])
        arrays[f"in_{name}"] = v
        aps[name] = nc.dram_tensor(f"in_{name}", v.shape, mb.dt.from_np(v.dtype), kind="ExternalInput").ap()
    out = nc.dram_tensor("out_0", (NODES, D), mb.dt.float32, kind="ExternalOutput").ap()
    build(nc, aps, out)
    return run(nc, [arrays], core_ids=[0]).results[0]["out_0"]
```
